# Optimizing a Trainium2 kernel written in Bass

```python
import numpy as np
import jax
import jax.numpy as jnp

def _softmax(x, axis=-1):
    return jax.nn.softmax(x, axis=axis)

def _gelu(x):
    return jax.nn.gelu(x, approximate=True)

def _silu(x):
    return jax.nn.silu(x)

def _sigmoid(x):
    return jax.nn.sigmoid(x)

def _layernorm(x, axis=-1, eps=1e-05):
    m = jnp.mean(x, axis=axis, keepdims=True)
    v = jnp.var(x, axis=axis, keepdims=True)
    return (x - m) / jnp.sqrt(v + eps)

def _scatter_add(tgt, idx, src, axis=0):
    return tgt.at[idx].add(src)

def _segment_sum(src, seg, n):
    return jax.ops.segment_sum(src, seg, n)
kernel_name = 'mk_gps_d2_gnn_r32_9100d7'

def setup_inputs(seed: int=0):
    np.random.seed(seed)
    _w = jnp.asarray

    def _rec_inputs():
        import jax
        import jax.numpy as jnp
        _gk = jax.random.key(seed)
        x = -0.0002117 + 1 * jax.random.normal(jax.random.fold_in(_gk, 1), (3125, 256), jnp.float32)
        src = jax.random.randint(jax.random.fold_in(_gk, 2), (50000,), 0, 3125, jnp.int32)
        dst = jax.random.randint(jax.random.fold_in(_gk, 3), (50000,), 0, 3125, jnp.int32)
        _o = jnp.argsort(dst, stable=True)
        src = src[_o]
        dst = dst[_o]
        return (x, src, dst)
    x, src, dst = _rec_inputs()

    def _L0_gnn_setup():
        import jax, jax.numpy as jnp
        import numpy as np
        N_NODES = 3125
        N_EDGES = 100000
        IN_F = 256
        OUT_F = 256
        NEG_SLOPE = 0.2
        key = jax.random.key(seed)
        ks = jax.random.split(key, 8)
        x = jax.random.normal(ks[0], (N_NODES, IN_F), dtype=jnp.float32)
        Wv = jax.random.normal(ks[1], (IN_F, OUT_F), dtype=jnp.float32) / np.sqrt(IN_F)
        bv = jnp.zeros((OUT_F,), dtype=jnp.float32)
        wq = jax.random.normal(ks[2], (OUT_F,), dtype=jnp.float32) / np.sqrt(OUT_F)
        bq = jnp.zeros((), dtype=jnp.float32)
        wk = jax.random.normal(ks[3], (OUT_F,), dtype=jnp.float32) / np.sqrt(OUT_F)
        bk = jnp.zeros((), dtype=jnp.float32)
        src = jax.random.randint(ks[4], (N_EDGES,), 0, N_NODES, dtype=jnp.int32)
        dst = jax.random.randint(ks[5], (N_EDGES,), 0, N_NODES, dtype=jnp.int32)
        return {'x': x, 'Wv': Wv, 'bv': bv, 'wq': wq, 'bq': bq, 'wk': wk, 'bk': bk, 'src': src, 'dst': dst}
    _L0_gnn_all = _L0_gnn_setup()
    _L0_gnn_in = {k: v for k, v in _L0_gnn_all.items() if k in ('Wv', 'bv', 'wq', 'bq', 'wk', 'bk')}
    del _L0_gnn_all

    def _L0_mix_setup():
        import jax, jax.numpy as jnp
        import numpy as np
        N, F, C, H = (32, 128, 256, 8)
        D = C // H
        EPS_ATTN = 1e-06
        EPS_LN = 1e-05

        def layer_norm(x, g, b):
            mu = jnp.mean(x, axis=-1, keepdims=True)
            var = jnp.var(x, axis=-1, keepdims=True)
            return (x - mu) * jax.lax.rsqrt(var + EPS_LN) * g + b
        key = jax.random.key(seed)
        ks = jax.random.split(key, 8)
        s = 1.0 / np.sqrt(C)
        return {'x': jax.random.normal(ks[0], (N, F, C), jnp.float32), 'Wqkv': jax.random.uniform(ks[1], (3 * C, C), jnp.float32, -s, s), 'ln1_g': jnp.ones((C,), jnp.float32), 'ln1_b': jnp.zeros((C,), jnp.float32), 'W1': jax.random.uniform(ks[2], (C, C), jnp.float32, -s, s), 'b1': jax.random.uniform(ks[3], (C,), jnp.float32, -s, s), 'W2': jax.random.uniform(ks[4], (C, C), jnp.float32, -s, s), 'b2': jax.random.uniform(ks[5], (C,), jnp.float32, -s, s), 'ln2_g': jnp.ones((C,), jnp.float32), 'ln2_b': jnp.zeros((C,), jnp.float32)}
    _L0_mix_all = _L0_mix_setup()
    _L0_mix_in = {k: v for k, v in _L0_mix_all.items() if k in ('Wqkv', 'ln1_g', 'ln1_b', 'W1', 'b1', 'W2', 'b2', 'ln2_g', 'ln2_b')}
    del _L0_mix_all

    def _L0_ffn_setup():
        import jax, jax.numpy as jnp
        import numpy as np
        TOP_K = 2
        LN_EPS = 1e-05
        key = jax.random.key(seed)
        ks = jax.random.split(key, 8)
        B, S, D, E, H = (16, 1024, 256, 8, 1024)
        x = jax.random.normal(ks[0], (B, S, D), dtype=jnp.float32)
        Wr = jax.random.normal(ks[1], (D, E), dtype=jnp.float32) * 0.1
        br = jnp.zeros((E,), dtype=jnp.float32)
        ln_g = jnp.ones((E, D), dtype=jnp.float32)
        ln_b = jnp.zeros((E, D), dtype=jnp.float32)
        W1 = jax.random.normal(ks[2], (E, D, H), dtype=jnp.float32) * (1.0 / np.sqrt(D))
        b1 = jnp.zeros((E, H), dtype=jnp.float32)
        W2 = jax.random.normal(ks[3], (E, H, D), dtype=jnp.float32) * (1.0 / np.sqrt(H))
        b2 = jnp.zeros((E, D), dtype=jnp.float32)
        return {'x': x, 'Wr': Wr, 'br': br, 'ln_g': ln_g, 'ln_b': ln_b, 'W1': W1, 'b1': b1, 'W2': W2, 'b2': b2}
    _L0_ffn_all = _L0_ffn_setup()
    _L0_ffn_in = {k: v for k, v in _L0_ffn_all.items() if k in ('Wr', 'br', 'ln_g', 'ln_b', 'W1', 'b1', 'W2', 'b2')}
    del _L0_ffn_all

    def _L1_gnn_setup():
        import jax, jax.numpy as jnp
        import numpy as np
        N_NODES = 3125
        N_EDGES = 9375
        D_IN = 256
        D_OUT = 256
        NEG_SLOPE = 0.2
        key = jax.random.key(seed)
        ks = jax.random.split(key, 6)
        feat = jax.random.normal(ks[0], (N_NODES, D_IN), dtype=jnp.float32)
        scale = (2.0 / (D_IN + D_OUT)) ** 0.5
        W_src = jax.random.normal(ks[1], (D_IN, D_OUT), dtype=jnp.float32) * scale
        b_src = jnp.zeros((D_OUT,), dtype=jnp.float32)
        W_dst = jax.random.normal(ks[2], (D_IN, D_OUT), dtype=jnp.float32) * scale
        b_dst = jnp.zeros((D_OUT,), dtype=jnp.float32)
        attn = jax.random.normal(ks[3], (D_OUT,), dtype=jnp.float32) * scale
        src = jax.random.randint(ks[4], (N_EDGES,), 0, N_NODES, dtype=jnp.int32)
        dst = jax.random.randint(ks[5], (N_EDGES,), 0, N_NODES, dtype=jnp.int32)
        return {'feat': feat, 'W_src': W_src, 'b_src': b_src, 'W_dst': W_dst, 'b_dst': b_dst, 'attn': attn, 'src': src, 'dst': dst}
    _L1_gnn_all = _L1_gnn_setup()
    _L1_gnn_in = {k: v for k, v in _L1_gnn_all.items() if k in ('W_src', 'b_src', 'W_dst', 'b_dst', 'attn')}
    del _L1_gnn_all

    def _L1_mix_setup():
        import jax, jax.numpy as jnp
        import numpy as np
        HEADS = 8
        EPS = 1e-05

        def _ln(t, w, b, headc):
            m = jnp.mean(t, axis=-1, keepdims=True)
            d = t - m
            std = jnp.sqrt(jnp.sum(d * d, axis=-1, keepdims=True) / (headc - 1))
            return w * (d / (std + EPS)) + b
        key = jax.random.key(seed)
        B, N, C = (32, 128, 256)
        headc = C // HEADS
        x = jax.random.normal(key, (B, N, C), dtype=jnp.float32)
        return {'x': x, 'kln_weight': jnp.ones((HEADS, 1, headc), dtype=jnp.float32), 'kln_bias': jnp.zeros((HEADS, 1, headc), dtype=jnp.float32), 'vln_weight': jnp.ones((HEADS, 1, headc), dtype=jnp.float32), 'vln_bias': jnp.zeros((HEADS, 1, headc), dtype=jnp.float32)}
    _L1_mix_all = _L1_mix_setup()
    _L1_mix_in = {k: v for k, v in _L1_mix_all.items() if k in ('kln_weight', 'kln_bias', 'vln_weight', 'vln_bias')}
    del _L1_mix_all

    def _L1_ffn_setup():
        import jax, jax.numpy as jnp
        import numpy as np
        B, A = (128, 8)
        IN, OUT = (256, 256)
        SH1, SH2 = (256, 128)
        EH1, EH2 = (128, 64)
        E, TOPK = (4, 2)

        def _shared_mlp(x, W1, b1, W2, b2, W3, b3):
            h = jax.nn.relu(x @ W1 + b1)
            h = jax.nn.relu(h @ W2 + b2)
            return h @ W3 + b3

        def _experts_mlp(x, eW1, eb1, eW2, eb2, eW3, eb3):
            h = jax.nn.relu(jnp.einsum('baf,efh->ebah', x, eW1) + eb1[:, None, None, :])
            h = jax.nn.relu(jnp.einsum('ebah,ehg->ebag', h, eW2) + eb2[:, None, None, :])
            o = jnp.einsum('ebag,ego->ebao', h, eW3) + eb3[:, None, None, :]
            return jnp.moveaxis(o, 0, -1)
        key = jax.random.key(seed)
        ks = jax.random.split(key, 16)
        s = 0.05
        return {'x': jax.random.normal(ks[0], (B, A, IN), jnp.float32), 'sW1': jax.random.normal(ks[1], (IN, SH1), jnp.float32) * s, 'sb1': jnp.zeros((SH1,), jnp.float32), 'sW2': jax.random.normal(ks[2], (SH1, SH2), jnp.float32) * s, 'sb2': jnp.zeros((SH2,), jnp.float32), 'sW3': jax.random.normal(ks[3], (SH2, OUT), jnp.float32) * s, 'sb3': jnp.zeros((OUT,), jnp.float32), 'eW1': jax.random.normal(ks[4], (E, IN, EH1), jnp.float32) * s, 'eb1': jnp.zeros((E, EH1), jnp.float32), 'eW2': jax.random.normal(ks[5], (E, EH1, EH2), jnp.float32) * s, 'eb2': jnp.zeros((E, EH2), jnp.float32), 'eW3': jax.random.normal(ks[6], (E, EH2, OUT), jnp.float32) * s, 'eb3': jnp.zeros((E, OUT), jnp.float32), 'gW': jax.random.normal(ks[7], (IN, E), jnp.float32) * s, 'gb': jnp.zeros((E,), jnp.float32)}
    _L1_ffn_all = _L1_ffn_setup()
    _L1_ffn_in = {k: v for k, v in _L1_ffn_all.items() if k in ('sW1', 'sb1', 'sW2', 'sb2', 'sW3', 'sb3', 'eW1', 'eb1', 'eW2', 'eb2', 'eW3', 'eb3', 'gW', 'gb')}
    del _L1_ffn_all
    return {'x': x, 'src': src, 'dst': dst, 'L0_gnn_Wv': _L0_gnn_in['Wv'], 'L0_gnn_bv': _L0_gnn_in['bv'], 'L0_gnn_wq': _L0_gnn_in['wq'], 'L0_gnn_bq': _L0_gnn_in['bq'], 'L0_gnn_wk': _L0_gnn_in['wk'], 'L0_gnn_bk': _L0_gnn_in['bk'], 'L0_mix_Wqkv': _L0_mix_in['Wqkv'], 'L0_mix_ln1_g': _L0_mix_in['ln1_g'], 'L0_mix_ln1_b': _L0_mix_in['ln1_b'], 'L0_mix_W1': _L0_mix_in['W1'], 'L0_mix_b1': _L0_mix_in['b1'], 'L0_mix_W2': _L0_mix_in['W2'], 'L0_mix_b2': _L0_mix_in['b2'], 'L0_mix_ln2_g': _L0_mix_in['ln2_g'], 'L0_mix_ln2_b': _L0_mix_in['ln2_b'], 'L0_ffn_Wr': _L0_ffn_in['Wr'], 'L0_ffn_br': _L0_ffn_in['br'], 'L0_ffn_ln_g': _L0_ffn_in['ln_g'], 'L0_ffn_ln_b': _L0_ffn_in['ln_b'], 'L0_ffn_W1': _L0_ffn_in['W1'], 'L0_ffn_b1': _L0_ffn_in['b1'], 'L0_ffn_W2': _L0_ffn_in['W2'], 'L0_ffn_b2': _L0_ffn_in['b2'], 'L1_gnn_W_src': _L1_gnn_in['W_src'], 'L1_gnn_b_src': _L1_gnn_in['b_src'], 'L1_gnn_W_dst': _L1_gnn_in['W_dst'], 'L1_gnn_b_dst': _L1_gnn_in['b_dst'], 'L1_gnn_attn': _L1_gnn_in['attn'], 'L1_mix_kln_weight': _L1_mix_in['kln_weight'], 'L1_mix_kln_bias': _L1_mix_in['kln_bias'], 'L1_mix_vln_weight': _L1_mix_in['vln_weight'], 'L1_mix_vln_bias': _L1_mix_in['vln_bias'], 'L1_ffn_sW1': _L1_ffn_in['sW1'], 'L1_ffn_sb1': _L1_ffn_in['sb1'], 'L1_ffn_sW2': _L1_ffn_in['sW2'], 'L1_ffn_sb2': _L1_ffn_in['sb2'], 'L1_ffn_sW3': _L1_ffn_in['sW3'], 'L1_ffn_sb3': _L1_ffn_in['sb3'], 'L1_ffn_eW1': _L1_ffn_in['eW1'], 'L1_ffn_eb1': _L1_ffn_in['eb1'], 'L1_ffn_eW2': _L1_ffn_in['eW2'], 'L1_ffn_eb2': _L1_ffn_in['eb2'], 'L1_ffn_eW3': _L1_ffn_in['eW3'], 'L1_ffn_eb3': _L1_ffn_in['eb3'], 'L1_ffn_gW': _L1_ffn_in['gW'], 'L1_ffn_gb': _L1_ffn_in['gb']}

def reference(x, src, dst, L0_gnn_Wv, L0_gnn_bv, L0_gnn_wq, L0_gnn_bq, L0_gnn_wk, L0_gnn_bk, L0_mix_Wqkv, L0_mix_ln1_g, L0_mix_ln1_b, L0_mix_W1, L0_mix_b1, L0_mix_W2, L0_mix_b2, L0_mix_ln2_g, L0_mix_ln2_b, L0_ffn_Wr, L0_ffn_br, L0_ffn_ln_g, L0_ffn_ln_b, L0_ffn_W1, L0_ffn_b1, L0_ffn_W2, L0_ffn_b2, L1_gnn_W_src, L1_gnn_b_src, L1_gnn_W_dst, L1_gnn_b_dst, L1_gnn_attn, L1_mix_kln_weight, L1_mix_kln_bias, L1_mix_vln_weight, L1_mix_vln_bias, L1_ffn_sW1, L1_ffn_sb1, L1_ffn_sW2, L1_ffn_sb2, L1_ffn_sW3, L1_ffn_sb3, L1_ffn_eW1, L1_ffn_eb1, L1_ffn_eW2, L1_ffn_eb2, L1_ffn_eW3, L1_ffn_eb3, L1_ffn_gW, L1_ffn_gb):
    import jax
    import jax.numpy as jnp

    def _L0_gnn_ref(x, Wv, bv, wq, bq, wk, bk, src, dst):
        import jax, jax.numpy as jnp
        import numpy as np
        N_NODES = 3125
        N_EDGES = 100000
        IN_F = 256
        OUT_F = 256
        NEG_SLOPE = 0.2
        n = x.shape[0]
        h = x @ Wv + bv
        q = h @ wq + bq
        k = h @ wk + bk
        e = q[src] + k[dst]
        c = jnp.where(e > 0, e, NEG_SLOPE * e)
        m = jax.ops.segment_max(c, dst, num_segments=n)
        ex = jnp.exp(c - m[dst])
        s = jax.ops.segment_sum(ex, dst, num_segments=n)
        attn = ex / s[dst]
        msg = h[src] * attn[:, None]
        out = jax.ops.segment_sum(msg, dst, num_segments=n)
        return out

    def _L0_mix_ref(x, Wqkv, ln1_g, ln1_b, W1, b1, W2, b2, ln2_g, ln2_b):
        import jax, jax.numpy as jnp
        import numpy as np
        N, F, C, H = (32, 128, 256, 8)
        D = C // H
        EPS_ATTN = 1e-06
        EPS_LN = 1e-05

        def layer_norm(x, g, b):
            mu = jnp.mean(x, axis=-1, keepdims=True)
            var = jnp.var(x, axis=-1, keepdims=True)
            return (x - mu) * jax.lax.rsqrt(var + EPS_LN) * g + b
        n, f, c = x.shape
        qkv = jnp.einsum('nfc,oc->nfo', x, Wqkv)
        q, k, v = jnp.split(qkv, 3, axis=-1)
        q = q.reshape(n, f, H, D)
        k = k.reshape(n, f, H, D)
        v = v.reshape(n, f, H, D)
        q = jax.nn.elu(q) + 1.0
        k = jax.nn.elu(k) + 1.0
        kv = jnp.einsum('nshd,nshm->nhmd', k, v)
        ksum = jnp.sum(k, axis=1)
        z = 1.0 / (jnp.einsum('nlhd,nhd->nlh', q, ksum) + EPS_ATTN)
        t = jnp.einsum('nlhd,nhmd,nlh->nlhm', q, kv, z)
        t = t.reshape(n, f, c)
        x1 = layer_norm(t + x, ln1_g, ln1_b)
        h = jax.nn.gelu(jnp.einsum('nfc,oc->nfo', x1, W1) + b1, approximate=False)
        y = jnp.einsum('nfc,oc->nfo', h, W2) + b2
        return layer_norm(y + x1, ln2_g, ln2_b)

    def _L0_ffn_ref(x, Wr, br, ln_g, ln_b, W1, b1, W2, b2):
        import jax, jax.numpy as jnp
        import numpy as np
        TOP_K = 2
        LN_EPS = 1e-05
        B, S, D = x.shape
        N = B * S
        xt = x.reshape(N, D)
        logits = xt @ Wr + br
        probs = jax.nn.softmax(logits, axis=-1)
        top_p, top_idx = jax.lax.top_k(probs, TOP_K)
        weights = top_p / top_p.sum(axis=-1, keepdims=True)
        mu = xt.mean(axis=-1, keepdims=True)
        var = ((xt - mu) ** 2).mean(axis=-1, keepdims=True)
        xn = (xt - mu) * jax.lax.rsqrt(var + LN_EPS)
        xe = xn[None, :, :] * ln_g[:, None, :] + ln_b[:, None, :]
        h = jax.nn.gelu(jnp.einsum('end,edh->enh', xe, W1) + b1[:, None, :], approximate=False)
        y = jnp.einsum('enh,ehd->end', h, W2) + b2[:, None, :]
        y_tok = jnp.transpose(y, (1, 0, 2))
        sel = jnp.take_along_axis(y_tok, top_idx[:, :, None], axis=1)
        out = (weights[:, :, None] * sel).sum(axis=1)
        return out.reshape(B, S, D)

    def _L1_gnn_ref(feat, W_src, b_src, W_dst, b_dst, attn, src, dst):
        import jax, jax.numpy as jnp
        import numpy as np
        N_NODES = 3125
        N_EDGES = 9375
        D_IN = 256
        D_OUT = 256
        NEG_SLOPE = 0.2
        N = feat.shape[0]
        el = feat @ W_src + b_src
        er = feat @ W_dst + b_dst
        e = jax.nn.leaky_relu(el[src] + er[dst], NEG_SLOPE)
        score = e @ attn
        smax = jax.ops.segment_max(score, dst, num_segments=N)
        ex = jnp.exp(score - smax[dst])
        ssum = jax.ops.segment_sum(ex, dst, num_segments=N)
        a = ex / ssum[dst]
        out = jax.ops.segment_sum(el[src] * a[:, None], dst, num_segments=N)
        return out

    def _L1_mix_ref(x, kln_weight, kln_bias, vln_weight, vln_bias):
        import jax, jax.numpy as jnp
        import numpy as np
        HEADS = 8
        EPS = 1e-05

        def _ln(t, w, b, headc):
            m = jnp.mean(t, axis=-1, keepdims=True)
            d = t - m
            std = jnp.sqrt(jnp.sum(d * d, axis=-1, keepdims=True) / (headc - 1))
            return w * (d / (std + EPS)) + b
        B, N, C = x.shape
        headc = C // HEADS
        qkv = x.reshape(B, N, HEADS, headc).transpose(0, 2, 1, 3)
        k = _ln(qkv, kln_weight, kln_bias, headc)
        v = _ln(qkv, vln_weight, vln_bias, headc)
        kv = jnp.einsum('bhnd,bhne->bhde', k, v) / N
        out = jnp.einsum('bhnd,bhde->bhne', qkv, kv)
        out = out.transpose(0, 2, 1, 3).reshape(B, N, C)
        return out + x

    def _L1_ffn_ref(x, sW1, sb1, sW2, sb2, sW3, sb3, eW1, eb1, eW2, eb2, eW3, eb3, gW, gb):
        import jax, jax.numpy as jnp
        import numpy as np
        B, A = (128, 8)
        IN, OUT = (256, 256)
        SH1, SH2 = (256, 128)
        EH1, EH2 = (128, 64)
        E, TOPK = (4, 2)

        def _shared_mlp(x, W1, b1, W2, b2, W3, b3):
            h = jax.nn.relu(x @ W1 + b1)
            h = jax.nn.relu(h @ W2 + b2)
            return h @ W3 + b3

        def _experts_mlp(x, eW1, eb1, eW2, eb2, eW3, eb3):
            h = jax.nn.relu(jnp.einsum('baf,efh->ebah', x, eW1) + eb1[:, None, None, :])
            h = jax.nn.relu(jnp.einsum('ebah,ehg->ebag', h, eW2) + eb2[:, None, None, :])
            o = jnp.einsum('ebag,ego->ebao', h, eW3) + eb3[:, None, None, :]
            return jnp.moveaxis(o, 0, -1)
        all_out = _experts_mlp(x, eW1, eb1, eW2, eb2, eW3, eb3)
        shared = _shared_mlp(x, sW1, sb1, sW2, sb2, sW3, sb3)
        gates = jax.nn.softmax(x @ gW + gb, axis=-1)
        topv, topi = jax.lax.top_k(gates, TOPK)
        topw = jax.nn.softmax(topv, axis=-1)
        sel = jnp.take_along_axis(all_out, topi[:, :, None, :], axis=-1)
        gated = jnp.sum(sel * topw[:, :, None, :], axis=-1)
        return shared + gated
    xn = _layernorm(x, axis=-1)
    x = x + _L0_gnn_ref(xn, L0_gnn_Wv, L0_gnn_bv, L0_gnn_wq, L0_gnn_bq, L0_gnn_wk, L0_gnn_bk, src, dst) + _L0_mix_ref(xn[None], L0_mix_Wqkv, L0_mix_ln1_g, L0_mix_ln1_b, L0_mix_W1, L0_mix_b1, L0_mix_W2, L0_mix_b2, L0_mix_ln2_g, L0_mix_ln2_b)[0]
    x = x + _L0_ffn_ref(_layernorm(x, axis=-1)[None], L0_ffn_Wr, L0_ffn_br, L0_ffn_ln_g, L0_ffn_ln_b, L0_ffn_W1, L0_ffn_b1, L0_ffn_W2, L0_ffn_b2)[0]
    xn = _layernorm(x, axis=-1)
    x = x + _L1_gnn_ref(xn, L1_gnn_W_src, L1_gnn_b_src, L1_gnn_W_dst, L1_gnn_b_dst, L1_gnn_attn, src, dst) + _L1_mix_ref(xn[None], L1_mix_kln_weight, L1_mix_kln_bias, L1_mix_vln_weight, L1_mix_vln_bias)[0]
    x = x + _L1_ffn_ref(_layernorm(x, axis=-1)[None], L1_ffn_sW1, L1_ffn_sb1, L1_ffn_sW2, L1_ffn_sb2, L1_ffn_sW3, L1_ffn_sb3, L1_ffn_eW1, L1_ffn_eb1, L1_ffn_eW2, L1_ffn_eb2, L1_ffn_eW3, L1_ffn_eb3, L1_ffn_gW, L1_ffn_gb)[0]
    return x

_drawn_inputs = setup_inputs


def setup_inputs(seed=0):
    import zlib

    import numpy as np

    out = dict(_drawn_inputs(seed))
    spreads = {'L0_gnn_bv': (0.0, 0.1),
     'L0_mix_ln1_g': (1.0, 0.2),
     'L0_mix_ln1_b': (0.0, 0.1),
     'L0_mix_ln2_g': (1.0, 0.2),
     'L0_mix_ln2_b': (0.0, 0.1),
     'L0_ffn_br': (0.0, 0.1),
     'L0_ffn_ln_g': (1.0, 0.2),
     'L0_ffn_ln_b': (0.0, 0.308),
     'L0_ffn_b1': (0.0, 0.304),
     'L0_ffn_b2': (0.0, 0.1),
     'L1_gnn_b_src': (0.0, 0.344),
     'L1_gnn_b_dst': (0.0, 0.8),
     'L1_mix_kln_weight': (1.0, 0.2),
     'L1_mix_kln_bias': (0.0, 0.375),
     'L1_mix_vln_weight': (1.0, 0.2),
     'L1_mix_vln_bias': (0.0, 0.374),
     'L1_ffn_sb1': (0.0, 2.0),
     'L1_ffn_sb2': (0.0, 0.8),
     'L1_ffn_sb3': (0.0, 0.348),
     'L1_ffn_eb1': (0.0, 0.8),
     'L1_ffn_eb2': (0.0, 0.8),
     'L1_ffn_eb3': (0.0, 0.494),
     'L1_ffn_gb': (0.0, 0.8)}
    factors = {'L0_mix_Wqkv': 4.114,
     'L0_mix_b1': 4.414,
     'L1_gnn_W_dst': 3.654,
     'L1_ffn_eW1': 5.459,
     'L1_ffn_eW2': 4.775,
     'L1_ffn_eW3': 3.75,
     'L1_ffn_gW': 3.661,
     'L1_ffn_sW1': 3.164}
    for name, (base, spread) in spreads.items():
        noise = np.random.default_rng([zlib.crc32(name.encode()), seed]).standard_normal(out[name].shape)
        drawn = base * np.exp(spread * noise) if base else spread * noise
        out[name] = jnp.asarray(drawn.astype(out[name].dtype))
    for name, factor in factors.items():
        out[name] = (out[name] * factor).astype(out[name].dtype)
    return out
```

```python
import concourse.bass as bass
from concourse import mybir
from contextlib import ExitStack

F32 = mybir.dt.float32
I32 = mybir.dt.int32
U32 = mybir.dt.uint32
ALU = mybir.AluOpType
ACT = mybir.ActivationFunctionType
AX = mybir.AxisListType

P = 128
NODES, D = 3125, 256
NODE_TILES = -(-NODES // P)
NODES_PAD = NODE_TILES * P
LAST_ROWS = NODES - (NODE_TILES - 1) * P
PAD_NODE = NODES_PAD - 1
EDGES = 50000
EDGE_CHUNKS = 4
EDGE_ROWS = 98
EDGE_TILES = EDGE_CHUNKS * EDGE_ROWS
GROUP = 5
GROUPS = 84
STEPS = GROUP * GROUPS
HEADS, HD = 8, 32
E0, HID = 8, 1024
SLOT_TILES = 56
SLOTS = SLOT_TILES * P
SLOT_ROWS = SLOTS + P
BIG = 1e30
T5 = NODE_TILES // 5


class Own:

    def __init__(self, eng, sem):
        self.eng, self.sem = eng, sem
        self.total = 0
        self.i = None

    def __call__(self, ins):
        ins.then_inc(self.sem, 1)
        self.total += 1
        return ins

    def wait(self):
        if self.i is None:
            self.eng.wait_ge(self.sem, self.total)
        else:
            self.eng.wait_ge(self.sem, self.i * self.per + (self.total - self.first * self.per))

    def loop(self, i, per, first=0):
        self.i, self.per, self.first, self.at = i, per, first, self.total

    def end(self, last):
        assert self.total - self.at == self.per, (self.total - self.at, self.per)
        self.total += (last - self.first - 1) * self.per
        self.i = None


class State:
    pass


class Phase:

    numbers = set()
    lasting = None

    def __init__(self, nc, tag):
        self.nc, self.tag, self.ctx, self.sems = nc, tag, ExitStack(), {}

    def __enter__(self):
        self.ctx.__enter__()
        return self

    def __exit__(self, *a):
        return self.ctx.__exit__(*a)

    def sb(self, name, shape, dt=F32):
        return self.ctx.enter_context(self.nc.sbuf_tensor(f"{self.tag}_{name}", shape, dt))

    def sem(self, name):
        sem = self.ctx.enter_context(self.nc.semaphore(f"{self.tag}_{name}"))
        self.numbers.add(sem.num)
        return sem

    def __getitem__(self, name):
        if name not in self.sems:
            self.sems[name] = self.sem(name)
        return self.sems[name]

    def for_gathers(self, *names):
        for name in names:
            self.sems[name] = self.lasting.enter_context(self.nc.semaphore(f"{self.tag}_{name}"))

    def block(self):
        return self.ctx.enter_context(self.nc.Block())


def bcast(vec):
    return vec.partition_broadcast(P)


def layernorm_stats(nc, dve, own, src, stats, mv, rstd, eps_done, sqrt_done, eps=1e-5):
    for t in range(NODE_TILES):
        own(nc.vector.bn_stats(stats[:, t, :], src[:, t, :]))
    own.wait()
    for t in range(NODE_TILES):
        own(nc.vector.bn_aggr(mv[:, t, :], stats[:, t, :]))
    own.wait()
    nc.vector.tensor_scalar_add(rstd[:, :], mv[:, :, 1], eps).then_inc(eps_done, 1)
    dve.wait_ge(sqrt_done, 1)
    own(nc.vector.reciprocal(rstd[:, :], rstd[:, :]))
    own.wait()


def prepare_edges(nc, S, A):
    with Phase(nc, "prepare_edges") as ph:
        srcI = ph.sb("src_rows_i", [EDGE_ROWS, EDGE_CHUNKS, P], I32)
        dstI = ph.sb("dst_rows_i", [EDGE_ROWS, EDGE_CHUNKS, P], I32)
        startI = ph.sb("dst_before_tile_i", [EDGE_ROWS, EDGE_CHUNKS], I32)
        blkI = ph.sb("block_i", [EDGE_ROWS, 2, EDGE_CHUNKS], I32)
        srcF = ph.sb("src_rows", [EDGE_ROWS, EDGE_CHUNKS, P])
        dstF = ph.sb("dst_rows", [EDGE_ROWS, EDGE_CHUNKS, P])
        first = ph.sb("first_step", [EDGE_ROWS, 2, EDGE_CHUNKS])
        tile_no = ph.sb("tile_no", [EDGE_ROWS, 2, EDGE_CHUNKS])
        step_row = ph.sb("step_row", [P, STEPS])
        step_col = ph.sb("step_col", [GROUPS, GROUP])
        reached = ph.sb("reached", [EDGE_ROWS, EDGE_CHUNKS, STEPS])
        pick = ph.sb("pick", [EDGE_ROWS, EDGE_CHUNKS, STEPS])
        blk = ph.sb("block_of_step", [P, STEPS])
        blkT = ph.sb("block_of_step_col", [GROUPS, GROUP])
        relR = ph.sb("rel_rows_sb", [GROUPS, GROUP, P])
        keyR = ph.sb("key_rows_sb", [GROUPS, GROUP, P])
        tmpR = ph.sb("tmp_rows", [GROUPS, GROUP, P])
        edge = ph.sb("key_ends", [1, 2])
        keyS = ph.sb("key_scan", [GROUPS, 3, GROUP * P])
        zero = ph.sb("zeros", [P, D])
        loaded, made, own_s, got, rows_out, ends_out, keys_in, zs = (ph.sem(n) for n in (
            "edge_loads", "pool_made", "dve_own", "pe_done", "rows_out", "ends_out", "keys_in", "zero_out"))
        block = ph.block()

        @block.vector
        def _(dve):
            v, own = nc.vector, Own(dve, own_s)
            dve.wait_ge(loaded, 64)
            dve.wait_ge(made, 6)
            own(v.tensor_copy(srcF[:, :, :], srcI[:, :, :]))
            own(v.tensor_copy(dstF[:, :, :], dstI[:, :, :]))
            own(v.tensor_scalar(blkI[:, 0, :], startI[:, :], 7, None, ALU.arith_shift_right))
            own(v.tensor_scalar(blkI[:, 1, :], dstI[:, :, P - 1], 7, None, ALU.arith_shift_right))
            own.wait()
            own(v.tensor_copy(first[:, :, :], blkI[:, :, :]))
            own.wait()
            own(v.tensor_tensor(first[:, :, :], first[:, :, :], tile_no[:, :, :], ALU.add))
            own.wait()
            for c in range(EDGE_CHUNKS):
                own(v.tensor_scalar(reached[:, c, :], step_row[0:EDGE_ROWS, :], first[:, 0, c:c + 1], None, ALU.is_ge))
            own.wait()
            for c in range(EDGE_CHUNKS):
                own(v.scalar_tensor_tensor(pick[:, c, :], step_row[0:EDGE_ROWS, :], first[:, 1, c:c + 1],
                                           reached[:, c, :], ALU.is_lt, ALU.mult))
            own.wait()
            S.picked = own.total
            dve.wait_ge(got, 1)
            own(v.tensor_copy(S.srcX[:, :], S.ps[:, 0, 0:STEPS]))
            own(v.scalar_tensor_tensor(blk[:, :], step_row[:, :], 1.0, S.ps[:, 2, 0:STEPS], ALU.add, ALU.subtract))
            own(v.scalar_tensor_tensor(blkT[:, :], step_col[:, :], 1.0, S.ps[0:GROUPS, 5, 0:GROUP], ALU.add,
                                       ALU.subtract))
            own.wait()
            own(v.tensor_scalar_min(blk[:, :], blk[:, :], float(NODE_TILES - 1)))
            own(v.tensor_scalar_min(blkT[:, :], blkT[:, :], float(NODE_TILES - 1)))
            own.wait()
            own(v.tensor_copy(S.blockI[:, :], blk[0:1, :]))
            own(v.scalar_tensor_tensor(S.relX[:, :], blk[:, :], -float(P), S.ps[:, 1, 0:STEPS], ALU.mult, ALU.add))
            for k in range(GROUP):
                src = S.ps[0:GROUPS, 3 + k // 4, (k % 4) * P:(k % 4 + 1) * P]
                own(v.tensor_scalar(blkT[:, k:k + 1], blkT[:, k:k + 1], -float(P), None, ALU.mult))
                own.wait()
                own(v.tensor_scalar(relR[:, k, :], src, blkT[:, k:k + 1], None, ALU.add))
            own.wait()
            own(v.tensor_scalar(S.validX[:, :], S.relX[:, :], 0.0, None, ALU.is_ge))
            own(v.tensor_scalar(keyR[:, :, :], relR[:, :, :], 0.0, None, ALU.is_ge))
            own.wait()
            own(v.scalar_tensor_tensor(S.validX[:, :], S.relX[:, :], float(P - 1), S.validX[:, :], ALU.is_le, ALU.mult))
            own(v.scalar_tensor_tensor(keyR[:, :, :], relR[:, :, :], float(P - 1), keyR[:, :, :], ALU.is_le, ALU.mult))
            own.wait()
            own(v.tensor_scalar(S.penX[:, :], S.validX[:, :], BIG, -BIG, ALU.mult, ALU.add))
            own(v.scalar_tensor_tensor(tmpR[:, :, :], relR[:, :, :], 1.0, keyR[:, :, :], ALU.add, ALU.mult))
            own.wait()
            own(v.tensor_scalar(keyR[:, :, :], tmpR[:, :, :], -1.0, None, ALU.add))
            S.rows_ready = own.total
            dve.wait_ge(keys_in, 48)
            for n, o in ((0, 0), (1, 2)):
                own(v.tensor_tensor(S.cut[:, n, :], keyS[:, 1, :], keyS[:, o, :], ALU.not_equal))
            own.wait()
            own(v.tensor_scalar(S.cut[:, :, :], S.cut[:, :, :], -BIG, None, ALU.mult))
            own.wait()
            for n in range(2):
                own(v.tensor_reduce(S.row_cut[:, n:n + 1], S.cut[:, n, :], AX.X, ALU.min))
            own.wait()

        @block.sync
        def _(sp):
            sp.dma_start(srcI[:, :, :], A["src"].rearrange("(c p) e -> p c e", p=EDGE_ROWS)).then_inc(loaded, 16)
            sp.dma_start(dstI[:, :, :], A["dst"].rearrange("(c p) e -> p c e", p=EDGE_ROWS)).then_inc(loaded, 16)
            sp.dma_start(startI[:, :], A["dst_before"]).then_inc(loaded, 16)
            sp.dma_start(S.X[:, :, :], A["x"].rearrange("(t p) d -> p t d", p=P)).then_inc(loaded, 16)
            sp.wait_ge(own_s, S.rows_ready)
            sp.dma_start(S.rel_dram.rearrange("(k p) e -> p k e", p=GROUPS), relR[:, :, :]).then_inc(rows_out, 16)
            key_rows = S.key_dram[1:1 + STEPS * P].rearrange("(k p e) -> p k e", p=GROUPS, e=P)
            sp.dma_start(key_rows, keyR[:, :, :]).then_inc(rows_out, 16)
            sp.wait_ge(made, 6)
            sp.dma_start(S.key_dram[0:1].rearrange("(a b) -> a b", a=1), edge[0:1, 0:1]).then_inc(ends_out, 16)
            sp.dma_start(S.key_dram[1 + STEPS * P:2 + STEPS * P].rearrange("(a b) -> a b", a=1),
                         edge[0:1, 1:2]).then_inc(ends_out, 16)
            sp.wait_ge(rows_out, 32)
            sp.wait_ge(ends_out, 32)
            for o in range(3):
                sp.dma_start(keyS[:, o, :], S.key_dram[o:o + STEPS * P].rearrange("(p e) -> p e", p=GROUPS)
                             ).then_inc(keys_in, 16)
            sp.wait_ge(zs, 16)

        @block.scalar
        def _(act):
            act.wait_ge(made, 6)
            act.dma_start(S.y_dram[SLOTS:SLOT_ROWS, :], zero[:, :]).then_inc(zs, 16)

        @block.gpsimd
        def _(pool):
            g = nc.gpsimd
            g.memset(S.ident[:, :], 0.0).then_inc(made, 1)
            pool.wait_ge(made, 1)
            g.affine_select(out=S.ident[:, :], in_=S.ident[:, :], compare_op=ALU.not_equal, fill=1.0, base=0,
                            pattern=[[-1, P]], channel_multiplier=1).then_inc(made, 1)
            g.iota(S.iota_row[:, :], [[1, P]], base=0, channel_multiplier=0, allow_small_or_imprecise_dtypes=True)
            g.iota(S.iota_col[:, :], [[0, 1]], base=0, channel_multiplier=1, allow_small_or_imprecise_dtypes=True)
            g.iota(step_row[:, :], [[1, STEPS]], base=0, channel_multiplier=0, allow_small_or_imprecise_dtypes=True)
            g.iota(step_col[:, :], [[GROUPS, GROUP]], base=0, channel_multiplier=1,
                   allow_small_or_imprecise_dtypes=True)
            g.iota(tile_no[:, :, :], [[1, 2], [EDGE_ROWS, EDGE_CHUNKS]], base=0, channel_multiplier=1,
                   allow_small_or_imprecise_dtypes=True).then_inc(made, 1)
            g.memset(edge[:, :], -2.0).then_inc(made, 1)
            g.memset(zero[:, :], 0.0).then_inc(made, 1)
            g.memset(S.ones[:, :], 1.0).then_inc(made, 1)

        @block.tensor
        def _(pe):
            t = nc.tensor
            pe.wait_ge(own_s, S.picked)
            for c in range(EDGE_CHUNKS):
                st, sp = c == 0, c == EDGE_CHUNKS - 1
                t.matmul(S.ps[:, 0, 0:STEPS], srcF[:, c, :], pick[:, c, :], start=st, stop=sp)
                t.matmul(S.ps[:, 1, 0:STEPS], dstF[:, c, :], pick[:, c, :], start=st, stop=sp)
                t.matmul(S.ps[:, 2, 0:STEPS], S.ones[0:EDGE_ROWS, :], reached[:, c, :], start=st, stop=sp)
            for k in range(GROUP):
                for c in range(EDGE_CHUNKS):
                    st, sp = c == 0, c == EDGE_CHUNKS - 1
                    t.matmul(S.ps[0:GROUPS, 3 + k // 4, (k % 4) * P:(k % 4 + 1) * P],
                             pick[:, c, k * GROUPS:(k + 1) * GROUPS], dstF[:, c, :], start=st, stop=sp)
                for c in range(EDGE_CHUNKS):
                    st, sp = c == 0, c == EDGE_CHUNKS - 1
                    last = t.matmul(S.ps[0:GROUPS, 5, k:k + 1], reached[:, c, k * GROUPS:(k + 1) * GROUPS],
                                    S.ones[0:EDGE_ROWS, 0:1], start=st, stop=sp)
            last.then_inc(got, 1)


RING = 5


def tiles(eng):
    with eng.Fori(0, T5) as i:
        for j in range(RING):
            yield i, i * RING + j, j, i * RING + (j + 1)


def after(eng, sem, n):
    eng.wait_ge(sem, n + RING)


def again(eng, sem, n):
    eng.wait_ge(sem, n)


def bank_again(eng, sem, j, n):
    eng.wait_ge(sem, n + RING - (1 if j == 0 else 2))


def norm_five(nc, ph, dve, src, mv, rstd, ring, i):
    for j in range(RING):
        t, n = i * RING + j, i * RING + (j + 1)
        again(dve, ph["xT_psum"], n)
        again(dve, ph["xn_kept"], n)
        nc.vector.tensor_scalar(ring[:, j, :], src[:, bass.ds(t, 1), :].squeeze(1), mv[:, bass.ds(t, 1), 0],
                                rstd[:, bass.ds(t, 1)], ALU.subtract, ALU.mult).then_inc(ph["xn_ready"], 1)


def keep_tiles(nc, ph, pool, ring, dst):
    pool.sem_inc(ph["xn_kept"], RING)
    for i, t, j, n in tiles(pool):
        after(pool, ph["xn_ready"], n)
        nc.gpsimd.tensor_copy(dst[:, bass.ds(t, 1), :], ring[:, j:j + 1, :]).then_inc(ph["xn_kept"], 1)


def copy_transposed(nc, ph, act, j, n, bank, xT, name="xT"):
    after(act, ph[name + "_psum"], n)
    nc.scalar.activation(xT[:, j, :, :], ph.ps[:, bank, 0:D].rearrange("p (c n) -> p c n", c=2),
                         ACT.Copy).then_inc(ph[name + "_ready"], 1)


def transpose_tile(nc, ph, pe, src, j, bank, ident, name="xT"):
    for c in range(2):
        last = nc.tensor.transpose(ph.ps[:, bank, c * P:(c + 1) * P], src[:, j, c * P:(c + 1) * P], ident[:, :])
    last.then_inc(ph[name + "_psum"], 1)


def project_layer0(nc, S, A):
    with Phase(nc, "project_layer0") as ph:
        ph.ps = S.ps
        W = ph.sb("w_proj", [P, 2, 4 * D])
        bv = ph.sb("bv_rows", [P, D])
        wqk = ph.sb("wqk_rows", [P, 2, D])
        bqk = ph.sb("bqk_rows", [P, 2])
        stats = ph.sb("ln_stats", [P, NODE_TILES, 6])
        mv = ph.sb("ln_mean_var", [P, NODE_TILES, 2])
        rstd = ph.sb("ln_rstd", [P, NODE_TILES])
        xn = ph.sb("xn_ring", [P, RING, D])
        xT = ph.sb("xn_T", [P, RING, 2, P])
        hrow = ph.sb("h_rows", [P, RING, D + 1])
        prod = ph.sb("h_times_w", [P, RING, 2, D])
        qk5 = ph.sb("q_k_of_five", [P, 2, RING])
        neg = ph.sb("neg_part", [P, RING, 2, D])
        kf = ph.sb("k_feature", [P, RING, D])
        vf = ph.sb("v_feature", [P, RING, 2, P + 1])
        mask4 = ph.sb("head_mask", [P, 4])
        kvs = ph.sb("kv_raw", [P, 2, P + 1])
        hq_bank = lambda j: j % 2
        kv_bank = lambda j: 2 + j % 2
        block = ph.block()

        @block.sync
        def _(sp):
            sp.dma_start(W[:, :, 0:D], A["Wv"].rearrange("(c p) n -> p c n", p=P)).then_inc(ph["weights_in"], 16)
            sp.dma_start(W[:, :, D:4 * D], A["WqkvT"].rearrange("(c p) n -> p c n", p=P)
                         ).then_inc(ph["weights_in"], 16)
            for dst, src in ((bv[:, :], "bv"), (wqk[:, 0, :], "wq"), (wqk[:, 1, :], "wk"), (bqk[:, 0:1], "bq"),
                             (bqk[:, 1:2], "bk")):
                sp.dma_start(dst, bcast(A[src])).then_inc(ph["rows_in"], 16)
            with sp.Fori(0, T5) as i:
                sp.wait_ge(ph["h_done"], i + 1)
                sp.dma_start(S.htab_dram[bass.ds(i * (RING * P), RING * P), :].rearrange("(t p) d -> p t d", p=P),
                             hrow[:, :, :]).then_inc(ph["h_table_out"], 16)
            sp.wait_ge(ph["h_table_out"], 16 * T5 + 16)

        @block.gpsimd
        def _(pool):
            g, made = nc.gpsimd, ph["pool_made"]
            g.memset(vf[:, :, :, P:P + 1], 1.0).then_inc(made, 1)
            g.memset(mask4[:, :], 1.0).then_inc(made, 1)
            pool.wait_ge(made, 2)
            g.affine_select(out=mask4[:, :], in_=mask4[:, :], compare_op=ALU.is_ge, fill=0.0, base=0,
                            pattern=[[-HD, 4]], channel_multiplier=1).then_inc(made, 1)
            pool.wait_ge(made, 3)
            g.affine_select(out=mask4[:, :], in_=mask4[:, :], compare_op=ALU.is_ge, fill=0.0, base=HD - 1,
                            pattern=[[HD, 4]], channel_multiplier=-1).then_inc(made, 1)
            pool.wait_ge(made, 4)
            g.tensor_copy(S.head_blocks[:, :].rearrange("p (h m) -> p h m", m=HD),
                          mask4[:, :].unsqueeze(2).broadcast_to([P, 4, HD])).then_inc(made, 1)
            keep_tiles(nc, ph, pool, xn, S.XN)

        @block.vector
        def _(dve):
            v, own = nc.vector, Own(dve, ph["dve_own"])
            layernorm_stats(nc, dve, own, S.X, stats, mv, rstd, ph["eps_done"], ph["sqrt_done"])
            dve.wait_ge(ph["rows_in"], 80)

            dve.sem_inc(ph["h_table_out"], 16)
            for name in ("xn_ready", "h_biased", "q_feature", "k_feature", "qk_dots"):
                dve.sem_inc(ph[name], RING)
            for i, t, j, n in tiles(dve):
                if j == 0:
                    norm_five(nc, ph, dve, S.X, mv, rstd, xn, i)
                    dve.wait_ge(ph["h_table_out"], i * 16 + 16)
                after(dve, ph["q_exp"], n)
                v.tensor_tensor(hrow[:, j, 0:D], S.ps[:, hq_bank(j), 0:D], bv[:, :], ALU.add
                                ).then_inc(ph["h_biased"], 1)
                v.scalar_tensor_tensor(S.QF[:, bass.ds(t, 1), :], S.ps[:, hq_bank(j):hq_bank(j) + 1, D:2 * D], 0.0,
                                       neg[:, j:j + 1, 0, :], ALU.max, ALU.add).then_inc(ph["q_feature"], 1)
                after(dve, ph["k_exp"], n)
                again(dve, ph["kv_used"], n)
                v.scalar_tensor_tensor(kf[:, j, :], S.ps[:, kv_bank(j), 0:D], 0.0, neg[:, j, 1, :], ALU.max,
                                       ALU.add).then_inc(ph["k_feature"], 1)
                after(dve, ph["h_biased"], n)
                for m in range(2):
                    ins = v.tensor_tensor_reduce(out=prod[:, j, m, :], in0=hrow[:, j, 0:D], in1=wqk[:, m, :],
                                                 scale=1.0, scalar=0.0, op0=ALU.mult, op1=ALU.add,
                                                 accum_out=qk5[:, m, j:j + 1])
                ins.then_inc(ph["qk_dots"], 1)
                if j == RING - 1:
                    after(dve, ph["qk_dots"], n)
                    v.tensor_copy(S.qk[:, :, bass.ds(i * RING, RING)], qk5[:, :, :])
                    v.tensor_scalar(hrow[:, :, D], qk5[:, 0, :], bqk[:, 0:1], None, ALU.add
                                    ).then_inc(ph["h_done"], 1)
            dve.wait_ge(ph["h_done"], T5)
            own(v.tensor_scalar(S.qk[:, 1, :], S.qk[:, 1, :], bqk[:, 1:2], None, ALU.add))
            after(dve, ph["kv_used"], NODE_TILES)
            dve.wait_ge(ph["pool_made"], 5)
            own(v.tensor_copy(kvs[:, :, :], S.ps[:, 6:8, 0:P + 1]))
            own.wait()
            for c in range(2):
                own(v.tensor_tensor(S.kvbd[:, c, 0:P], kvs[:, c, 0:P], S.head_blocks[:, :], ALU.mult))
                own(v.tensor_scalar(S.kvbd[:, c, P:P + 4], mask4[:, :], kvs[:, c, P:P + 1], None, ALU.mult))
            own.wait()

        @block.scalar
        def _(act):
            a = nc.scalar
            act.wait_ge(ph["eps_done"], 1)
            a.activation(rstd[:, :], rstd[:, :], ACT.Sqrt).then_inc(ph["sqrt_done"], 1)
            for name in ("xT_ready", "q_neg", "q_exp", "k_neg", "k_exp", "v_feature"):
                act.sem_inc(ph[name], RING)
            act.wait_ge(ph["pool_made"], 1)
            for i, t, j, n in tiles(act):
                again(act, ph["kv_psum"], n)
                copy_transposed(nc, ph, act, j, n, 4 + j % 2, xT)
                for m, (psum, neg_s, exp_s, used, bank, off) in enumerate((
                        ("hq_psum", "q_neg", "q_exp", "q_feature", hq_bank(j), D),
                        ("kv_psum", "k_neg", "k_exp", "k_feature", kv_bank(j), 0))):
                    after(act, ph[psum], n)
                    again(act, ph[used], n)
                    a.activation(neg[:, j, m, :], S.ps[:, bank, off:off + D], ACT.Relu, scale=-1.0
                                 ).then_inc(ph[neg_s], 1)
                    if m == 1:
                        again(act, ph["kv_used"], n)
                        a.activation(vf[:, j, :, 0:P], S.ps[:, bank, D:2 * D].rearrange("p (c n) -> p c n", c=2),
                                     ACT.Copy).then_inc(ph["v_feature"], 1)
                        after(act, ph["v_feature"], n)
                    after(act, ph[neg_s], n)
                    a.activation(neg[:, j, m, :], neg[:, j, m, :], ACT.Exp, scale=-1.0).then_inc(ph[exp_s], 1)

        @block.tensor
        def _(pe):
            t_ = nc.tensor
            pe.wait_ge(ph["weights_in"], 32)
            for name in ("xT_psum", "hq_psum", "kv_psum", "kv_used"):
                pe.sem_inc(ph[name], RING)

            def products(j, n):
                after(pe, ph["xn_ready"], n)
                bank_again(pe, ph["xT_ready"], j, n)
                transpose_tile(nc, ph, pe, xn, j, 4 + j % 2, S.ident)
                after(pe, ph["xT_ready"], n)
                for half, (psum, bank) in enumerate((("hq_psum", hq_bank(j)), ("kv_psum", kv_bank(j)))):
                    for used in (("h_biased", "q_feature") if half == 0 else ("k_feature", "v_feature")):
                        bank_again(pe, ph[used], j, n)
                    for c in range(2):
                        ins = t_.matmul(S.ps[:, bank, :], xT[:, j, c, :], W[:, c, half * 512:(half + 1) * 512],
                                        start=c == 0, stop=c == 1)
                    ins.then_inc(ph[psum], 1)

            def group(i, first, last):
                for j in range(RING):
                    products(j, i * RING + (j + 1))
                for j in range(RING):
                    after(pe, ph["k_feature"], i * RING + (j + 1))
                    after(pe, ph["v_feature"], i * RING + (j + 1))
                    rows = LAST_ROWS if last and j == RING - 1 else P
                    for c in range(2):
                        ins = t_.matmul(S.ps[:, 6 + c, 0:P + 1], kf[0:rows, j, c * P:(c + 1) * P],
                                        vf[0:rows, j, c, :], start=first and j == 0, stop=last and j == RING - 1)
                    ins.then_inc(ph["kv_used"], 1)

            group(0, True, False)
            with pe.Fori(1, T5 - 1) as i:
                group(i, False, False)
            group(T5 - 1, False, True)


HALVES = 2


def groups(eng):
    with eng.Fori(0, GROUPS // HALVES) as i:
        for h in range(HALVES):
            yield i, h, i * HALVES + h, i * HALVES + (h + 1)


def dst_block(eng, S, k, j):
    return eng.value_load(S.blockI[0:1, bass.ds(k * GROUP + j, 1)], min_val=0, max_val=NODE_TILES - 1)


def gather_edges(nc, S, ph, block, table, idx, got, relB, before=None, slope=None):
    ph.for_gathers("gathered0", "gathered1")

    @block.gpsimd
    def _(pool):
        g = nc.gpsimd
        for i, h, k, n in groups(pool):
            pool.wait_ge(ph["rows_used"], n)
            pool.wait_ge(ph[f"kept{h}"], i * 16 + 16)
            g.tensor_copy(idx[:, h, :], S.srcX[:, bass.ds(k * GROUP, GROUP)]).then_inc(ph["idx_ready"], 1)
            pool.wait_ge(ph["idx_ready"], n)
            pool.sem_inc(ph["gather_gate"], 1)
            for j in range(GROUP):
                g.indirect_dma_start(got[:, h, j, :], None, table,
                                     bass.IndirectOffsetOnAxis(ap=idx[:, h, j:j + 1], axis=0)
                                     ).then_inc(ph[f"gathered{h}"], 16)

    @block.sync
    def _(sp):
        if before:
            before(sp)
        for h in range(HALVES):
            sp.sem_inc(ph[f"kept{h}"], 16)
        for i, h, k, n in groups(sp):
            sp.wait_ge(ph[f"gathered{h}"], i * (16 * GROUP) + 16 * GROUP)
            sp.dma_start(S.step_dram[bass.ds(k, 1), :, :].rearrange("a p (g d) -> (a p) g d", d=D),
                         got[:, h, :, 0:D]).then_inc(ph[f"kept{h}"], 16)
        for h in range(HALVES):
            sp.wait_ge(ph[f"kept{h}"], 16 * (GROUPS // HALVES) + 16)

    @block.scalar
    def _(act):
        stream_rel(nc, S, ph, act, relB, slope)


def stream_rel(nc, S, ph, act, relB, slope):
    for i, h, k, n in groups(act):
        act.wait_ge(ph["hot_ready"], n)
        act.dma_start(relB[:, h, :], S.rel_dram[bass.ds(k * GROUP, GROUP), :].rearrange("g e -> (g e)")
                      .partition_broadcast(P)).then_inc(ph[f"rel_in{h}"], 16)
        if slope:
            slope(act, i, h, k, n)


def onehot_T(nc, S, ph, dve, hot, relB, i, h, n):
    dve.wait_ge(ph[f"rel_in{h}"], i * 16 + 16)
    dve.wait_ge(ph["dst_psum"], n)
    nc.vector.tensor_scalar(hot[:, h, :], relB[:, h, :], S.iota_col[:, 0:1], None, ALU.is_equal
                            ).then_inc(ph["hot_ready"], 1)


def score_layer0(nc, S, A):
    with Phase(nc, "score_layer0") as ph:
        idx = ph.sb("gather_idx", [P, HALVES, GROUP], I32)
        got = ph.sb("h_of_sources", [P, HALVES, GROUP, D + 1])
        relB = ph.sb("rel_bcast", [P, HALVES, GROUP * P])
        hot = ph.sb("dst_onehot_T", [P, HALVES, GROUP * P])
        block = ph.block()
        gather_edges(nc, S, ph, block, S.htab_dram, idx, got, relB)

        @block.vector
        def _(dve):
            v = nc.vector
            for name in ("hot_ready", "rows_used"):
                dve.sem_inc(ph[name], HALVES)
            for i, h, k, n in groups(dve):
                onehot_T(nc, S, ph, dve, hot, relB, i, h, n)
                dve.wait_ge(ph[f"gathered{h}"], i * (16 * GROUP) + 16 * GROUP)
                dve.wait_ge(ph["dst_psum"], n + HALVES)
                v.tensor_tensor(S.scoreX[:, bass.ds(k * GROUP, GROUP)], S.ps[:, h, 0:GROUP], got[:, h, :, D],
                                ALU.add).then_inc(ph["rows_used"], 1)

        @block.tensor
        def _(pe):
            pe.sem_inc(ph["dst_psum"], HALVES)
            for i, h, k, n in groups(pe):
                pe.wait_ge(ph["hot_ready"], n + HALVES)
                pe.wait_ge(ph["rows_used"], n)
                for j in range(GROUP):
                    b = dst_block(pe, S, k, j)
                    last = nc.tensor.matmul(S.ps[:, h, j:j + 1], hot[:, h, j * P:(j + 1) * P],
                                            S.qk[:, 1, bass.ds(b, 1)], start=True, stop=True)
                last.then_inc(ph["dst_psum"], 1)


def softmax_weights(nc, S, A, leaky):
    N = GROUP * P
    with Phase(nc, f"softmax_weights_{S.layer}") as ph:
        score = ph.sb("score_scan", [GROUPS, N])
        fwd = ph.sb("max_forward", [GROUPS, N])
        bwd = ph.sb("max_backward", [GROUPS, N])
        ends = ph.sb("row_ends", [GROUPS, 2])
        rows = ph.sb("row_ends_T", [1, 4, GROUPS])
        carry = ph.sb("carry_rows", [1, 2, GROUPS + 1])
        carryT = ph.sb("carry_cols", [GROUPS, 2])
        ps2 = S.ps[:, :, :].rearrange("p b n -> p (b n)")
        block = ph.block()

        @block.vector
        def _(dve):
            v, own = nc.vector, Own(dve, ph["dve_own"])
            if leaky:
                own(v.tensor_scalar(S.weightX[:, :], S.scoreX[:, :], 0.2, None, ALU.mult))
                own.wait()
                own(v.tensor_tensor(S.scoreX[:, :], S.scoreX[:, :], S.weightX[:, :], ALU.max))
                own.wait()
            own(v.tensor_tensor(S.scoreX[:, :], S.scoreX[:, :], S.validX[:, :], ALU.mult))
            own.wait()
            v.tensor_tensor(S.scoreX[:, :], S.scoreX[:, :], S.penX[:, :], ALU.add).then_inc(ph["score_ready"], 1)
            own(v.memset(carry[:, :, :], -BIG))
            dve.wait_ge(ph["score_psum"], 1)
            own(v.tensor_copy(score[:, :], ps2[0:GROUPS, 0:N]))
            own.wait()
            own(v.tensor_tensor_scan(fwd[:, :], S.cut[:, 0, :], score[:, :], -BIG, ALU.add, ALU.max))
            own(v.tensor_tensor_scan(bwd[:, ::-1], S.cut[:, 1, ::-1], score[:, ::-1], -BIG, ALU.add, ALU.max))
            own.wait()
            own(v.tensor_copy(ends[:, 0:1], fwd[:, N - 1:N]))
            v.tensor_copy(ends[:, 1:2], bwd[:, 0:1]).then_inc(ph["ends_ready"], 1)
            dve.wait_ge(ph["ends_psum"], 1)
            own(v.tensor_copy(rows[:, :, :], ps2[0:1, 1024:1024 + 4 * GROUPS].rearrange("p (a n) -> p a n", a=4)))
            own.wait()
            own(v.tensor_tensor_scan(carry[:, 0, 1:GROUPS + 1], rows[:, 2, :], rows[:, 0, :], -BIG, ALU.add, ALU.max))
            own(v.tensor_tensor_scan(carry[:, 1, 0:GROUPS][:, ::-1], rows[:, 3, ::-1], rows[:, 1, ::-1], -BIG, ALU.add,
                                     ALU.max))
            own.wait()
            S.carry_ready = own.total
            dve.wait_ge(ph["carry_psum"], 1)
            own(v.tensor_copy(carryT[:, :], ps2[0:GROUPS, 1536:1538]))
            own.wait()
            own(v.tensor_tensor_scan(fwd[:, :], S.cut[:, 0, :], score[:, :], carryT[:, 0:1], ALU.add, ALU.max))
            own(v.tensor_tensor_scan(bwd[:, ::-1], S.cut[:, 1, ::-1], score[:, ::-1], carryT[:, 1:2], ALU.add,
                                     ALU.max))
            own.wait()
            own(v.tensor_tensor(fwd[:, :], fwd[:, :], bwd[:, :], ALU.max))
            own.wait()
            v.tensor_tensor(score[:, :], score[:, :], fwd[:, :], ALU.subtract).then_inc(ph["shifted"], 1)
            dve.wait_ge(ph["weight_psum"], 1)
            own(v.tensor_tensor(S.weightX[:, :].rearrange("p (q g) -> p q g", g=GROUP),
                                ps2[:, 2048:2048 + STEPS].rearrange("p (g q) -> p q g", g=GROUP),
                                S.validX[:, :].rearrange("p (q g) -> p q g", g=GROUP), ALU.mult))
            own.wait()

        @block.scalar
        def _(act):
            act.wait_ge(ph["shifted"], 1)
            nc.scalar.activation(score[:, :], score[:, :], ACT.Exp).then_inc(ph["exps"], 1)

        @block.tensor
        def _(pe):
            t = nc.tensor
            pe.wait_ge(ph["score_ready"], 1)
            for g in range(GROUP):
                ins = t.transpose(ps2[0:GROUPS, g * P:(g + 1) * P], S.scoreX[:, g::GROUP], S.ident[:, :])
            ins.then_inc(ph["score_psum"], 1)
            pe.wait_ge(ph["ends_ready"], 1)
            idg = S.ident[0:GROUPS, 0:GROUPS]
            for m, col in enumerate((ends[:, 0:1], ends[:, 1:2], S.row_cut[:, 0:1], S.row_cut[:, 1:2])):
                ins = t.transpose(ps2[0:1, 1024 + m * GROUPS:1024 + (m + 1) * GROUPS], col, idg)
            ins.then_inc(ph["ends_psum"], 1)
            pe.wait_ge(ph["dve_own"], S.carry_ready)
            t.transpose(ps2[0:GROUPS, 1536:1537], carry[0:1, 0, 0:GROUPS], S.ident[0:1, 0:1])
            t.transpose(ps2[0:GROUPS, 1537:1538], carry[0:1, 1, 1:GROUPS + 1], S.ident[0:1, 0:1]
                        ).then_inc(ph["carry_psum"], 1)
            pe.wait_ge(ph["exps"], 1)
            for g in range(GROUP):
                ins = t.transpose(ps2[:, 2048 + g * GROUPS:2048 + (g + 1) * GROUPS], score[:, g * P:(g + 1) * P], idg)
            ins.then_inc(ph["weight_psum"], 1)


def aggregate(nc, S, A):
    with Phase(nc, f"aggregate_{S.layer}") as ph:
        rowsB = ph.sb("step_rows", [P, HALVES, GROUP, D + 1])
        hotw = ph.sb("weighted_onehot", [P, HALVES, GROUP, P])
        block = ph.block()

        @block.gpsimd
        def _(pool):
            nc.gpsimd.memset(S.acc[:, :, :], 0.0).then_inc(ph["pool_made"], 1)
            nc.gpsimd.memset(rowsB[:, :, :, D:D + 1], 1.0).then_inc(ph["pool_made"], 1)

        @block.sync
        def _(sp):
            for i, h, k, n in groups(sp):
                sp.wait_ge(ph["sums_psum"], n * GROUP)
                sp.dma_start(rowsB[:, h, :, 0:D], S.step_dram[bass.ds(k, 1), :, :].rearrange(
                    "a p (g d) -> (a p) g d", d=D)).then_inc(ph[f"rows_in{h}"], 16)

        @block.vector
        def _(dve):
            v = nc.vector
            dve.wait_ge(ph["pool_made"], 2)
            dve.sem_inc(ph["hotw_ready"], HALVES)
            dve.sem_inc(ph["added"], GROUP)

            def weigh(h, k, n):
                dve.wait_ge(ph["sums_psum"], n * GROUP)
                for j in range(GROUP):
                    ins = v.tensor_scalar(hotw[:, h, j, :], S.iota_row[:, :], S.relX[:, bass.ds(k * GROUP + j, 1)],
                                          S.weightX[:, bass.ds(k * GROUP + j, 1)], ALU.is_equal, ALU.mult)
                ins.then_inc(ph["hotw_ready"], 1)

            for i, h, k, n in groups(dve):
                weigh(h, k, n)
                for j in range(GROUP):
                    m = n * GROUP + (j + 1 - GROUP)
                    b = dst_block(dve, S, k, j)
                    dve.wait_ge(ph["sums_psum"], m + HALVES * GROUP)
                    dve.wait_ge(ph["added"], m + GROUP - 1)
                    v.tensor_tensor(S.acc[:, bass.ds(b, 1), :], S.ps[:, j:j + 1, 0:D + 1],
                                    S.acc[:, bass.ds(b, 1), :], ALU.add).then_inc(ph["added"], 1)

        @block.tensor
        def _(pe):
            pe.sem_inc(ph["sums_psum"], HALVES * GROUP)
            pe.wait_ge(ph["pool_made"], 2)
            for i, h, k, n in groups(pe):
                pe.wait_ge(ph["hotw_ready"], n + HALVES)
                pe.wait_ge(ph[f"rows_in{h}"], i * 16 + 16)
                for j in range(GROUP):
                    pe.wait_ge(ph["added"], n * GROUP + (j + 1 - GROUP))
                    nc.tensor.matmul(S.ps[:, j, 0:D + 1], hotw[:, h, j, :], rowsB[:, h, j, :],
                                     start=True, stop=True).then_inc(ph["sums_psum"], 1)


def ln_scratch(ph):
    return (ph.sb("ln_stats", [P, NODE_TILES, 6]), ph.sb("ln_mean_var", [P, NODE_TILES, 2]),
            ph.sb("ln_rstd", [P, NODE_TILES]))


def ln_root(nc, ph, act, rstd):
    act.wait_ge(ph["eps_done"], 1)
    nc.scalar.activation(rstd[:, :], rstd[:, :], ACT.Sqrt).then_inc(ph["sqrt_done"], 1)


def stage_tiles(nc, ph, pool, src, ring, name, used):
    pool.sem_inc(ph[name], RING)
    for i, t, j, n in tiles(pool):
        again(pool, ph[used], n)
        nc.gpsimd.tensor_copy(ring[:, j:j + 1, :], src[:, bass.ds(t, 1), :]).then_inc(ph[name], 1)


def linear_attention(nc, S, A):
    with Phase(nc, "linear_attention") as ph:
        ph.ps = S.ps
        qr = ph.sb("q_ring", [P, RING, D])
        qT = ph.sb("q_T", [P, RING, 2, P])
        z = ph.sb("inv_den", [P, RING, 2, 4])
        tt = ph.sb("attended", [P, RING, 2, P])
        block = ph.block()

        @block.gpsimd
        def _(pool):
            stage_tiles(nc, ph, pool, S.QF, qr, "q_staged", "xT_psum")

        @block.scalar
        def _(act):
            act.sem_inc(ph["xT_ready"], RING)
            for i, t, j, n in tiles(act):
                again(act, ph["num_psum"], n)
                copy_transposed(nc, ph, act, j, n, 4 + j % 2, qT)

        @block.tensor
        def _(pe):
            pe.sem_inc(ph["xT_psum"], RING)
            pe.sem_inc(ph["num_psum"], RING)
            for i, t, j, n in tiles(pe):
                after(pe, ph["q_staged"], n)
                bank_again(pe, ph["xT_ready"], j, n)
                transpose_tile(nc, ph, pe, qr, j, 4 + j % 2, S.ident)
                after(pe, ph["xT_ready"], n)
                bank_again(pe, ph["attended"], j, n)
                for c in range(2):
                    ins = nc.tensor.matmul(S.ps[:, j % 2, c * (P + 4):(c + 1) * (P + 4)], qT[:, j, c, :],
                                           S.kvbd[:, c, :], start=True, stop=True)
                ins.then_inc(ph["num_psum"], 1)

        @block.vector
        def _(dve):
            v = nc.vector
            for name in ("attended", "den_eps", "den_inv"):
                dve.sem_inc(ph[name], RING)
            for i, t, j, n in tiles(dve):
                both = S.ps[:, j % 2, 0:2 * (P + 4)].rearrange("p (c n) -> p c n", c=2)
                after(dve, ph["num_psum"], n)
                v.tensor_scalar_add(z[:, j, :, :], both[:, :, P:P + 4], 1e-6).then_inc(ph["den_eps"], 1)
                after(dve, ph["den_eps"], n)
                v.reciprocal(z[:, j, :, :], z[:, j, :, :]).then_inc(ph["den_inv"], 1)
                after(dve, ph["den_inv"], n)
                for c in range(2):
                    ins = v.tensor_tensor(tt[:, j, c, :].rearrange("p (h m) -> p h m", h=4),
                                          both[:, c, 0:P].rearrange("p (h m) -> p h m", h=4),
                                          z[:, j, c, :].unsqueeze(2).broadcast_to([P, 4, HD]), ALU.mult)
                ins.then_inc(ph["attended"], 1)
                after(dve, ph["attended"], n)
                v.tensor_tensor(S.QF[:, bass.ds(t, 1), :], tt[:, j:j + 1, :, :].rearrange("p a c n -> p a (c n)"),
                                S.XN[:, bass.ds(t, 1), :], ALU.add)


def mix_mlp(nc, S, A):
    with Phase(nc, "mix_mlp") as ph:
        ph.ps = S.ps
        W1 = ph.sb("w1", [P, 2, D])
        W2 = ph.sb("w2", [P, 2, D])
        b1 = ph.sb("b1", [P, 2])
        rows = ph.sb("ln1_g_b_b2", [P, 3, D])
        stats, mv, rstd = ln_scratch(ph)
        x1 = ph.sb("x1_ring", [P, RING, D])
        xs = ph.sb("x1_scaled", [P, RING, D])
        xT = ph.sb("x1_T", [P, RING, 2, P])
        hT = ph.sb("hidden_T", [P, RING, 2, P])
        block = ph.block()

        @block.sync
        def _(sp):
            for dst, src in ((W1, "mW1T"), (W2, "mW2T")):
                sp.dma_start(dst[:, :, :], A[src].rearrange("(c p) n -> p c n", p=P)).then_inc(ph["weights_in"], 16)
            sp.dma_start(b1[:, :], A["mb1"]).then_inc(ph["weights_in"], 16)
            for m, src in enumerate(("ln1_g", "ln1_b", "mb2")):
                sp.dma_start(rows[:, m, :], bcast(A[src])).then_inc(ph["weights_in"], 16)
            sp.wait_ge(ph["weights_in"], 96)

        @block.vector
        def _(dve):
            v, own = nc.vector, Own(dve, ph["dve_own"])
            layernorm_stats(nc, dve, own, S.QF, stats, mv, rstd, ph["eps_done"], ph["sqrt_done"])
            dve.wait_ge(ph["weights_in"], 96)
            for name in ("xn_ready", "x1_scaled", "y_biased", "y_done"):
                dve.sem_inc(ph[name], RING)
            for i, t, j, n in tiles(dve):
                if j == 0:
                    for jj in range(RING):
                        tt, nn = i * RING + jj, i * RING + (jj + 1)
                        again(dve, ph["xT_psum"], nn)
                        v.scalar_tensor_tensor(xs[:, jj, :], S.QF[:, bass.ds(tt, 1), :].squeeze(1),
                                               mv[:, bass.ds(tt, 1), 0], rows[:, 0, :], ALU.subtract, ALU.mult
                                               ).then_inc(ph["x1_scaled"], 1)
                    for jj in range(RING):
                        tt, nn = i * RING + jj, i * RING + (jj + 1)
                        after(dve, ph["x1_scaled"], nn)
                        v.scalar_tensor_tensor(x1[:, jj, :], xs[:, jj, :], rstd[:, bass.ds(tt, 1)], rows[:, 1, :],
                                               ALU.mult, ALU.add).then_inc(ph["xn_ready"], 1)
                after(dve, ph["y_psum"], n)
                v.tensor_tensor(S.QF[:, bass.ds(t, 1), :].squeeze(1), S.ps[:, 6 + j % 2, 0:D], x1[:, j, :], ALU.add
                                ).then_inc(ph["y_done"], 1)
                after(dve, ph["y_done"], n)
                v.tensor_tensor(S.QF[:, bass.ds(t, 1), :].squeeze(1), S.QF[:, bass.ds(t, 1), :].squeeze(1),
                                rows[:, 2, :], ALU.add).then_inc(ph["y_biased"], 1)

        @block.scalar
        def _(act):
            ln_root(nc, ph, act, rstd)
            act.sem_inc(ph["xT_ready"], RING)
            act.sem_inc(ph["hidden"], RING)
            act.wait_ge(ph["weights_in"], 96)
            for i, t, j, n in tiles(act):
                again(act, ph["h_psum"], n)
                copy_transposed(nc, ph, act, j, n, 4 + j % 2, xT)
                after(act, ph["h_psum"], n)
                again(act, ph["y_psum"], n)
                for m in range(2):
                    ins = nc.scalar.activation(hT[:, j, m, :], S.ps[:, j % 2, m * P:(m + 1) * P], ACT.Gelu,
                                               bias=b1[:, m:m + 1])
                ins.then_inc(ph["hidden"], 1)

        @block.tensor
        def _(pe):
            pe.wait_ge(ph["weights_in"], 96)
            for name in ("xT_psum", "h_psum", "y_psum"):
                pe.sem_inc(ph[name], RING)
            for i, t, j, n in tiles(pe):
                after(pe, ph["xn_ready"], n)
                bank_again(pe, ph["xT_ready"], j, n)
                transpose_tile(nc, ph, pe, x1, j, 4 + j % 2, S.ident)
                after(pe, ph["xT_ready"], n)
                bank_again(pe, ph["hidden"], j, n)
                for m in range(2):
                    for c in range(2):
                        ins = nc.tensor.matmul(S.ps[:, j % 2, m * P:(m + 1) * P], W1[:, c, m * P:(m + 1) * P],
                                               xT[:, j, c, :], start=c == 0, stop=c == 1)
                ins.then_inc(ph["h_psum"], 1)
                after(pe, ph["hidden"], n)
                bank_again(pe, ph["y_done"], j, n)
                for c in range(2):
                    ins = nc.tensor.matmul(S.ps[:, 6 + j % 2, 0:D], hT[:, j, c, :], W2[:, c, :],
                                           start=c == 0, stop=c == 1)
                ins.then_inc(ph["y_psum"], 1)


def add_edge_sums(nc, ph, S, dve):
    v, own = nc.vector, Own(dve, ph["dve_own_sums"])
    inv = S.inv_sum
    own(v.tensor_scalar_max(inv[:, :], S.acc[:, :, D], 1e-30))
    own.wait()
    own(v.reciprocal(inv[:, :], inv[:, :]))
    own.wait()
    for t in range(NODE_TILES):
        own(v.scalar_tensor_tensor(S.X[:, t, :], S.acc[:, t, 0:D], inv[:, t:t + 1], S.X[:, t, :],
                                   ALU.mult, ALU.add))
    own.wait()


def router(nc, S, A):
    with Phase(nc, "router") as ph:
        ph.ps = S.ps
        Wr = ph.sb("w_router", [P, 2, E0])
        br = ph.sb("b_router", [P, E0])
        rows = ph.sb("ln2_g_b", [P, 2, D])
        stats, mv, rstd = ln_scratch(ph)
        mv2 = ph.sb("ln_mean_var_x", [P, NODE_TILES, 2])
        rstd2 = ph.sb("ln_rstd_x", [P, NODE_TILES])
        xt = ph.sb("xt_ring", [P, RING, D])
        xT = ph.sb("xt_T", [P, RING, 2, P])
        block = ph.block()

        @block.sync
        def _(sp):
            sp.dma_start(Wr[:, :, :], A["Wr"].rearrange("(c p) n -> p c n", p=P)).then_inc(ph["weights_in"], 16)
            sp.dma_start(br[:, :], bcast(A["br"])).then_inc(ph["weights_in"], 16)
            for m, src in enumerate(("ln2_g", "ln2_b")):
                sp.dma_start(rows[:, m, :], bcast(A[src])).then_inc(ph["weights_in"], 16)
            sp.wait_ge(ph["weights_in"], 64)

        @block.vector
        def _(dve):
            v, own = nc.vector, Own(dve, ph["dve_own"])
            layernorm_stats(nc, dve, own, S.QF, stats, mv, rstd, ph["eps_done"], ph["sqrt_done"])
            dve.wait_ge(ph["weights_in"], 64)
            add_edge_sums(nc, ph, S, dve)
            for t in range(NODE_TILES):
                own(v.scalar_tensor_tensor(S.QF[:, t, :], S.QF[:, t, :], mv[:, t, 0:1], rows[:, 0, :],
                                           ALU.subtract, ALU.mult))
            own.wait()
            for t in range(NODE_TILES):
                own(v.scalar_tensor_tensor(S.QF[:, t, :], S.QF[:, t, :], rstd[:, t:t + 1], rows[:, 1, :],
                                           ALU.mult, ALU.add))
            own.wait()
            for t in range(NODE_TILES):
                own(v.tensor_tensor(S.X[:, t, :], S.X[:, t, :], S.QF[:, t, :], ALU.add))
            own.wait()
            layernorm_stats(nc, dve, own, S.X, stats, mv2, rstd2, ph["eps_done2"], ph["sqrt_done2"])
            for name in ("xn_ready", "logits"):
                dve.sem_inc(ph[name], RING)
            for i, t, j, n in tiles(dve):
                if j == 0:
                    norm_five(nc, ph, dve, S.X, mv2, rstd2, xt, i)
                after(dve, ph["l_psum"], n)
                v.tensor_tensor(S.logits[:, bass.ds(t, 1), :].squeeze(1), S.ps[:, j % 2, 0:E0], br[:, :], ALU.add
                                ).then_inc(ph["logits"], 1)
            after(dve, ph["logits"], NODE_TILES)

        @block.gpsimd
        def _(pool):
            pool.wait_ge(ph["qf_free"], 1)
            keep_tiles(nc, ph, pool, xt, S.QF)

        @block.scalar
        def _(act):
            ln_root(nc, ph, act, rstd)
            act.wait_ge(ph["eps_done2"], 1)
            act.sem_inc(ph["qf_free"], 1)
            nc.scalar.activation(rstd2[:, :], rstd2[:, :], ACT.Sqrt).then_inc(ph["sqrt_done2"], 1)
            act.sem_inc(ph["xT_ready"], RING)
            for i, t, j, n in tiles(act):
                again(act, ph["l_psum"], n)
                copy_transposed(nc, ph, act, j, n, 4 + j % 2, xT)

        @block.tensor
        def _(pe):
            pe.wait_ge(ph["weights_in"], 64)
            for name in ("xT_psum", "l_psum"):
                pe.sem_inc(ph[name], RING)
            for i, t, j, n in tiles(pe):
                after(pe, ph["xn_ready"], n)
                bank_again(pe, ph["xT_ready"], j, n)
                transpose_tile(nc, ph, pe, xt, j, 4 + j % 2, S.ident)
                after(pe, ph["xT_ready"], n)
                bank_again(pe, ph["logits"], j, n)
                for c in range(2):
                    ins = nc.tensor.matmul(S.ps[:, j % 2, 0:E0], xT[:, j, c, :], Wr[:, c, :],
                                           start=c == 0, stop=c == 1)
                ins.then_inc(ph["l_psum"], 1)


def top_two(nc, own, logits, top, idx, idxf, hot1, hot2, iota8, width):
    v = nc.vector
    for t in range(NODE_TILES):
        own(v.max(top[:, t, :], logits[:, t, :]))
    own.wait()
    for t in range(NODE_TILES):
        own(v.max_index(idx[:, t, :], top[:, t, :], logits[:, t, :]))
    own.wait()
    own(v.tensor_copy(idxf[:, :, :], idx[:, :, :]))
    own.wait()
    for m, hot in enumerate((hot1, hot2)):
        w = hot.shape[2]
        own(v.tensor_tensor(hot[:, :, :], iota8[:, 0:w].unsqueeze(1).broadcast_to([P, NODE_TILES, w]),
                            idxf[:, :, m:m + 1].broadcast_to([P, NODE_TILES, w]), ALU.is_equal))
    own.wait()


def dispatch_plan(nc, S, A):
    with Phase(nc, "dispatch_plan") as ph:
        top = ph.sb("top8", [P, NODE_TILES, 8])
        idx = ph.sb("top8_idx", [P, NODE_TILES, 8], U32)
        idxf = ph.sb("top8_idx_f", [P, NODE_TILES, 8])
        hot1 = ph.sb("hot1", [P, NODE_TILES, E0])
        hot2 = ph.sb("hot2", [P, NODE_TILES, E0])
        both = ph.sb("hot_both", [P, NODE_TILES, E0])
        tri = ph.sb("strictly_before", [P, P])
        tot = ph.sb("tile_totals", [P, NODE_TILES, E0])
        cum = ph.sb("totals_up_to", [P, NODE_TILES, E0])
        one = ph.sb("one_row", [P, NODE_TILES])
        tl = ph.sb("tiles_of_expert", [P, E0])
        tlI = ph.sb("tiles_of_expert_i", [P, E0], I32)
        end = ph.sb("end_tile", [P, E0])
        base = ph.sb("first_slot", [P, E0])
        posf = ph.sb("slot_f", [P, 2, NODE_TILES])
        trash = ph.sb("padding_slot", [P, 1])
        step = ph.sb("slot_tile_no", [P, SLOT_TILES])
        ex = ph.sb("expert_of_tile_f", [P, SLOT_TILES])
        partI = ph.sb("slot_parts_i", [P, 2, 2, NODE_TILES], I32)
        part = ph.sb("slot_parts", [P, 2, 2, NODE_TILES])
        node_no = ph.sb("node_no", [P, NODE_TILES])
        hot_row = ph.sb("slot_row_onehot", [P, RING, 2, P])
        hot_tile = ph.sb("slot_tile_onehot", [P, RING, 2, SLOT_TILES])
        block = ph.block()

        @block.gpsimd
        def _(pool):
            g, made = nc.gpsimd, ph["pool_made"]
            g.memset(tri[:, :], 1.0).then_inc(made, 1)
            g.memset(one[:, :], 1.0).then_inc(made, 1)
            g.memset(S.node_mask[:, :], 1.0).then_inc(made, 1)
            g.iota(trash[:, :], [[0, 1]], base=SLOTS, channel_multiplier=1,
                   allow_small_or_imprecise_dtypes=True).then_inc(made, 1)
            g.iota(step[:, :], [[1, SLOT_TILES]], base=0, channel_multiplier=0,
                   allow_small_or_imprecise_dtypes=True).then_inc(made, 1)
            g.iota(node_no[:, :], [[P, NODE_TILES]], base=0, channel_multiplier=1,
                   allow_small_or_imprecise_dtypes=True).then_inc(made, 1)
            pool.wait_ge(made, 6)
            g.affine_select(out=tri[:, :], in_=tri[:, :], compare_op=ALU.is_gt, fill=0.0, base=0,
                            pattern=[[1, P]], channel_multiplier=-1).then_inc(made, 1)
            g.affine_select(out=S.node_mask[:, NODE_TILES - 1:], in_=S.node_mask[:, NODE_TILES - 1:],
                            compare_op=ALU.is_ge, fill=0.0, base=LAST_ROWS - 1, pattern=[[0, 1]],
                            channel_multiplier=-1).then_inc(made, 1)

        @block.vector
        def _(dve):
            v, own = nc.vector, Own(dve, ph["dve_own"])
            top_two(nc, own, S.logits, top, idx, idxf, hot1, hot2, S.iota_row, E0)
            v.tensor_tensor(S.w2[:, :], top[:, :, 1], top[:, :, 0], ALU.subtract).then_inc(ph["gap"], 1)
            own(v.tensor_tensor(both[:, :, :], hot1[:, :, :], hot2[:, :, :], ALU.add))
            dve.wait_ge(ph["pool_made"], 8)
            own.wait()
            own(v.tensor_tensor(both[:, :, :], both[:, :, :],
                                S.node_mask[:, :].unsqueeze(2).broadcast_to([P, NODE_TILES, E0]), ALU.mult))
            dve.wait_ge(ph["gap_exp"], 1)
            own(v.tensor_scalar_add(S.w1[:, :], S.w2[:, :], 1.0))
            own.wait()
            S.both_ready = own.total
            own(v.reciprocal(S.w1[:, :], S.w1[:, :]))
            own.wait()
            own(v.tensor_tensor(S.w2[:, :], S.w2[:, :], S.w1[:, :], ALU.mult))
            own.wait()
            for w, hot, dst in ((S.w1, hot1, S.wexp), (S.w2, hot2, tot)):
                own(v.tensor_tensor(dst[:, :, :], hot[:, :, :], w[:, :].unsqueeze(2).broadcast_to(
                    [P, NODE_TILES, E0]), ALU.mult))
            own.wait()
            own(v.tensor_tensor(S.wexp[:, :, :], S.wexp[:, :, :], tot[:, :, :], ALU.add))
            own.wait()
            dve.wait_ge(ph["counts"], 1)
            flat = NODE_TILES * E0
            own(v.tensor_copy(tot[:, :, :], S.ps[:, 1, 0:flat].rearrange("p (t e) -> p t e", e=E0)))
            own.wait()
            for e in range(E0):
                own(v.tensor_tensor_scan(cum[:, :, e], one[:, :], tot[:, :, e], 0.0, ALU.mult, ALU.add))
            own.wait()
            own(v.tensor_scalar_add(tlI[:, :], cum[:, NODE_TILES - 1, :], float(P - 1)))
            own.wait()
            own(v.tensor_scalar(tlI[:, :], tlI[:, :], 7, None, ALU.arith_shift_right))
            own.wait()
            own(v.tensor_copy(tl[:, :], tlI[:, :]))
            own.wait()
            own(v.tensor_tensor_scan(end[:, :], one[:, 0:E0], tl[:, :], 0.0, ALU.mult, ALU.add))
            own.wait()
            own(v.tensor_tensor(base[:, :], end[:, :], tl[:, :], ALU.subtract))
            own(v.memset(ex[:, :], 0.0))
            own(v.tensor_tensor(cum[:, :, :], cum[:, :, :], tot[:, :, :], ALU.subtract))
            own.wait()
            own(v.tensor_scalar(base[:, :], base[:, :], float(P), None, ALU.mult))
            own(v.tensor_tensor(cum[:, :, :], cum[:, :, :],
                                S.ps[:, 0, 0:flat].rearrange("p (t e) -> p t e", e=E0), ALU.add))
            for e in range(E0 - 1):
                own.wait()
                own(v.scalar_tensor_tensor(ex[:, :], step[:, :], end[:, e:e + 1], ex[:, :], ALU.is_ge, ALU.add))
            own.wait()
            own(v.tensor_copy(S.expertI[:, :], ex[0:1, :]))
            own(v.tensor_tensor(cum[:, :, :], cum[:, :, :],
                                base[:, :].unsqueeze(1).broadcast_to([P, NODE_TILES, E0]), ALU.add))
            own.wait()
            for m, hot in enumerate((hot1, hot2)):
                own(v.tensor_tensor(tot[:, :, :], cum[:, :, :], hot[:, :, :], ALU.mult))
                own.wait()
                own(v.tensor_reduce(posf[:, m, :], tot[:, :, :], AX.X, ALU.add))
                own.wait()
            own(v.tensor_scalar(posf[:, :, :], posf[:, :, :], trash[:, 0:1], None, ALU.subtract))
            own.wait()
            own(v.tensor_tensor(posf[:, :, :], posf[:, :, :],
                                S.node_mask[:, :].unsqueeze(1).broadcast_to([P, 2, NODE_TILES]), ALU.mult))
            own.wait()
            own(v.tensor_scalar(S.posI[:, :, :], posf[:, :, :], trash[:, 0:1], None, ALU.add))
            own.wait()
            own(v.tensor_scalar(partI[:, 0, :, :], S.posI[:, :, :], P - 1, None, ALU.bitwise_and))
            own(v.tensor_scalar(partI[:, 1, :, :], S.posI[:, :, :], 7, None, ALU.arith_shift_right))
            own.wait()
            own(v.tensor_copy(part[:, :, :, :], partI[:, :, :, :]))
            own.wait()
            dve.sem_inc(ph["places"], RING)
            for i, t, j, n in tiles(dve):
                again(dve, ph["listed"], n)
                for m in range(2):
                    v.tensor_scalar(hot_row[:, j, m, :], S.iota_row[:, :], part[:, 0, m, bass.ds(t, 1)], None,
                                    ALU.is_equal)
                    ins = v.tensor_scalar(hot_tile[:, j, m, :], step[:, :], part[:, 1, m, bass.ds(t, 1)],
                                          node_no[:, bass.ds(t, 1)], ALU.is_equal, ALU.mult)
                ins.then_inc(ph["places"], 1)
            after(dve, ph["listed"], NODE_TILES)
            own(v.tensor_copy(S.slot_node[:, :], S.ps[:, 2, 0:SLOT_TILES]))
            own.wait()

        @block.scalar
        def _(act):
            act.wait_ge(ph["gap"], 1)
            nc.scalar.activation(S.w2[:, :], S.w2[:, :], ACT.Exp).then_inc(ph["gap_exp"], 1)

        @block.tensor
        def _(pe):
            flat = NODE_TILES * E0
            rhs = both[:, :, :].rearrange("p t e -> p (t e)")
            pe.wait_ge(ph["dve_own"], S.both_ready)
            nc.tensor.matmul(S.ps[:, 0, 0:flat], tri[:, :], rhs, start=True, stop=True)
            nc.tensor.matmul(S.ps[:, 1, 0:flat], S.ones[:, :], rhs, start=True, stop=True).then_inc(ph["counts"], 1)
            pe.sem_inc(ph["listed"], RING)

            def five(i, first, last):
                for j in range(RING):
                    after(pe, ph["places"], i * RING + (j + 1))
                    for m in range(2):
                        ins = nc.tensor.matmul(S.ps[:, 2, 0:SLOT_TILES], hot_row[:, j, m, :], hot_tile[:, j, m, :],
                                               start=first and j + m == 0, stop=last and j == RING - 1 and m == 1)
                    ins.then_inc(ph["listed"], 1)
            five(0, True, False)
            with pe.Fori(1, T5 - 1) as i:
                five(i, False, False)
            five(T5 - 1, False, True)


def expert_inputs(nc, S, A):
    with Phase(nc, "expert_inputs") as ph:
        stats, mv, rstd = ln_scratch(ph)
        block = ph.block()

        @block.vector
        def _(dve):
            own = Own(dve, ph["dve_own"])
            layernorm_stats(nc, dve, own, S.QF, stats, mv, rstd, ph["eps_done"], ph["sqrt_done"])
            for t in range(NODE_TILES):
                nc.vector.tensor_scalar(S.XN[:, t, :], S.QF[:, t, :], mv[:, t, 0:1], rstd[:, t:t + 1],
                                        ALU.subtract, ALU.mult).then_inc(ph["xn_ready"], 1)

        @block.scalar
        def _(act):
            ln_root(nc, ph, act, rstd)

        @block.sync
        def _(sp):
            for k in range(T5):
                sp.wait_ge(ph["xn_ready"], RING * (k + 1))
                sp.dma_start(S.xn_dram[k * RING * P:(k + 1) * RING * P, :].rearrange("(t p) d -> p t d", p=P),
                             S.XN[:, k * RING:(k + 1) * RING, :]).then_inc(ph["table_out"], 16)
            sp.wait_ge(ph["table_out"], 16 * T5)


def experts(nc, S, A):
    HC = HID // P
    with Phase(nc, "experts") as ph:
        ph.for_gathers("x_in0", "x_in1")
        xs = ph.sb("slot_rows", [P, 2, D])
        idx = ph.sb("node_idx", [P, 2], I32)
        small = ph.sb("g_b_b1", [P, 2, 4 + HC])
        W1 = ph.sb("expert_w1", [P, 2, 2, HID])
        W2 = ph.sb("expert_w2", [P, 2, HC, D])
        xT = ph.sb("xe_T", [P, 2, 2, P])
        hT = ph.sb("hidden_T", [P, 2, HC, P])
        ys = ph.sb("y_rows", [P, 2, D])
        block = ph.block()

        def pairs(eng, body):
            with eng.Fori(0, SLOT_TILES // 2) as i:
                for h in range(2):
                    body(i, h, i * 2 + h, i * 2 + (h + 1))

        @block.sync
        def _(sp):
            def load(i, h, t, n):
                e = sp.value_load(S.expertI[0:1, bass.ds(t, 1)], min_val=0, max_val=E0 - 1)
                sp.wait_ge(ph["h_psum"], n)
                sp.dma_start(W1[:, h, :, :], A["eW1"][bass.ds(e * D, D), :].rearrange("(c p) n -> p c n", p=P)
                             ).then_inc(ph[f"w1_in{h}"], 16)
                sp.wait_ge(ph["hidden"], n * 2)
                sp.dma_start(small[:, h, :], A["eSmall"][bass.ds(e, 1), :, :].squeeze(0)
                             ).then_inc(ph[f"small_in{h}"], 16)
                sp.wait_ge(ph["y_psum"], n)
                sp.dma_start(W2[:, h, :, :], A["eW2"][bass.ds(e * HID, HID), :].rearrange("(c p) n -> p c n", p=P)
                             ).then_inc(ph[f"w2_in{h}"], 16)
            pairs(sp, load)

        @block.gpsimd
        def _(pool):
            def gather(i, h, t, n):
                pool.wait_ge(ph["xT_psum"], n)
                nc.gpsimd.tensor_copy(idx[:, h:h + 1], S.slot_node[:, bass.ds(t, 1)]).then_inc(ph["idx_ready"], 1)
                pool.wait_ge(ph["idx_ready"], n)
                pool.sem_inc(ph["gather_gate"], 1)
                nc.gpsimd.indirect_dma_start(xs[:, h, :], None, S.xn_dram,
                                             bass.IndirectOffsetOnAxis(ap=idx[:, h:h + 1], axis=0)
                                             ).then_inc(ph[f"x_in{h}"], 16)
            pairs(pool, gather)

        @block.vector
        def _(dve):
            dve.sem_inc(ph["xT_ready"], 2)
            dve.sem_inc(ph["y_ready"], 2)

            def xe(h, i, n):
                dve.wait_ge(ph["xT_psum"], n + 2)
                dve.wait_ge(ph[f"small_in{h}"], i * 16 + 16)
                dve.wait_ge(ph["h_psum"], n)
                for c in range(2):
                    ins = nc.vector.tensor_scalar(xT[:, h, c, :], S.ps[:, 0, c * P:(c + 1) * P], small[:, h, c:c + 1],
                                                  small[:, h, 2 + c:3 + c], ALU.mult, ALU.add)
                ins.then_inc(ph["xT_ready"], 1)

            def y(h, i, n):
                dve.wait_ge(ph["y_psum"], n + 2)
                dve.wait_ge(ph[f"y_out{h}"], i * 16 + 16)
                nc.vector.tensor_copy(ys[:, h, :], S.ps[:, 1, 0:D]).then_inc(ph["y_ready"], 1)

            xe(0, 0, 1)
            with dve.Fori(0, SLOT_TILES // 2 - 1) as i:
                xe(1, i, i * 2 + 2)
                y(0, i, i * 2 + 1)
                xe(0, i + 1, i * 2 + 3)
                y(1, i, i * 2 + 2)
            last = SLOT_TILES // 2 - 1
            xe(1, last, last * 2 + 2)
            y(0, last, last * 2 + 1)
            y(1, last, last * 2 + 2)

        @block.scalar
        def _(act):
            act.sem_inc(ph["hidden"], 2 * 2)
            for h in range(2):
                act.sem_inc(ph[f"y_out{h}"], 16)

            def gelu(i, h, t, n):
                act.wait_ge(ph["y_psum"], n)
                for m in range(HC):
                    if m % 4 == 0:
                        act.wait_ge(ph["h_half"], n * 2 + (m // 4 - 1))
                    ins = nc.scalar.activation(hT[:, h, m, :], S.ps[:, 2 + 2 * h + m // 4, (m % 4) * P:(m % 4 + 1) * P],
                                               ACT.Gelu, bias=small[:, h, 4 + m:5 + m])
                    if m % 4 == 3:
                        ins.then_inc(ph["hidden"], 1)
            def out(i, h, t, n):
                act.wait_ge(ph["y_ready"], n + 2)
                act.dma_start(S.y_dram[bass.ds(t * P, P), :], ys[:, h, :]).then_inc(ph[f"y_out{h}"], 16)

            def step(i, h, t, n):
                gelu(i, h, t, n)
            gelu(0, 0, 0, 1)
            with act.Fori(0, SLOT_TILES // 2 - 1) as i:
                gelu(i, 1, None, i * 2 + 2)
                out(i, 0, i * 2, i * 2 + 1)
                gelu(i, 0, None, i * 2 + 3)
                out(i, 1, i * 2 + 1, i * 2 + 2)
            last = SLOT_TILES // 2 - 1
            gelu(last, 1, None, last * 2 + 2)
            out(last, 0, last * 2, last * 2 + 1)
            out(last, 1, last * 2 + 1, last * 2 + 2)
            for h in range(2):
                act.wait_ge(ph[f"y_out{h}"], 16 * (SLOT_TILES // 2) + 16)

        @block.tensor
        def _(pe):
            for name in ("xT_psum", "h_psum", "y_psum"):
                pe.sem_inc(ph[name], 2)

            def up(h, i, n):
                pe.wait_ge(ph[f"x_in{h}"], i * 16 + 16)
                pe.wait_ge(ph["xT_ready"], n + 1)
                for c in range(2):
                    ins = nc.tensor.transpose(S.ps[:, 0, c * P:(c + 1) * P], xs[:, h, c * P:(c + 1) * P], S.ident[:, :])
                ins.then_inc(ph["xT_psum"], 1)
                pe.wait_ge(ph["xT_ready"], n + 2)
                pe.wait_ge(ph[f"w1_in{h}"], i * 16 + 16)
                pe.wait_ge(ph["hidden"], n * 2)
                for m in range(HC):
                    for c in range(2):
                        ins = nc.tensor.matmul(S.ps[:, 2 + 2 * h + m // 4, (m % 4) * P:(m % 4 + 1) * P],
                                               W1[:, h, c, m * P:(m + 1) * P], xT[:, h, c, :],
                                               start=c == 0, stop=c == 1)
                    if m % 4 == 3 and m < HC - 1:
                        ins.then_inc(ph["h_half"], 1)
                ins.then_inc(ph["h_half"], 1)
                pe.wait_ge(ph["h_half"], n * 2)
                pe.sem_inc(ph["h_psum"], 1)

            def down(h, i, n):
                pe.wait_ge(ph[f"w2_in{h}"], i * 16 + 16)
                pe.wait_ge(ph["hidden"], n * 2 + 4)
                pe.wait_ge(ph["y_ready"], n + 1)
                for m in range(HC):
                    ins = nc.tensor.matmul(S.ps[:, 1, 0:D], hT[:, h, m, :], W2[:, h, m, :],
                                           start=m == 0, stop=m == HC - 1)
                ins.then_inc(ph["y_psum"], 1)

            up(0, 0, 1)
            with pe.Fori(0, SLOT_TILES // 2 - 1) as i:
                up(1, i, i * 2 + 2)
                down(0, i, i * 2 + 1)
                up(0, i + 1, i * 2 + 3)
                down(1, i, i * 2 + 2)
            last = SLOT_TILES // 2 - 1
            up(1, last, last * 2 + 2)
            down(0, last, last * 2 + 1)
            down(1, last, last * 2 + 2)


def combine(nc, S, A):
    with Phase(nc, "combine") as ph:
        ph.for_gathers(*[f"y_in{j}" for j in range(RING)])
        yr = ph.sb("y_of_slots", [P, RING, 2, D])
        idx = ph.sb("slot_ring", [P, RING, 2], I32)
        wr = ph.sb("weights_ring", [P, RING, E0])
        wT = ph.sb("weights_T", [E0, RING, P])
        b2 = ph.sb("expert_b2", [E0, D])
        block = ph.block()

        @block.sync
        def _(sp):
            sp.dma_start(b2[:, :], A["eb2"]).then_inc(ph["b2_in"], 16)

        @block.gpsimd
        def _(pool):
            pool.sem_inc(ph["w_staged"], RING)
            for i, t, j, n in tiles(pool):
                again(pool, ph["x_done"], n)
                nc.gpsimd.tensor_copy(idx[:, j, :], S.posI[:, :, bass.ds(t, 1)].squeeze(2))
                nc.gpsimd.tensor_copy(wr[:, j, :], S.wexp[:, bass.ds(t, 1), :].squeeze(1)).then_inc(ph["w_staged"], 1)
                after(pool, ph["w_staged"], n)
                pool.sem_inc(ph["gather_gate"], 1)
                for m in range(2):
                    nc.gpsimd.indirect_dma_start(yr[:, j, m, :], None, S.y_dram,
                                                 bass.IndirectOffsetOnAxis(ap=idx[:, j, m:m + 1], axis=0)
                                                 ).then_inc(ph[f"y_in{j}"], 16)

        @block.scalar
        def _(act):
            act.sem_inc(ph["wT_ready"], RING)
            for i, t, j, n in tiles(act):
                after(act, ph["wT_psum"], n)
                again(act, ph["b_psum"], n)
                nc.scalar.activation(wT[:, j, :], S.ps[0:E0, 2 + j % 2, 0:P], ACT.Copy).then_inc(ph["wT_ready"], 1)

        @block.tensor
        def _(pe):
            pe.wait_ge(ph["b2_in"], 16)
            pe.sem_inc(ph["wT_psum"], RING)
            pe.sem_inc(ph["b_psum"], RING)
            for i, t, j, n in tiles(pe):
                after(pe, ph["w_staged"], n)
                bank_again(pe, ph["wT_ready"], j, n)
                nc.tensor.transpose(S.ps[0:E0, 2 + j % 2, 0:P], wr[:, j, :], S.ident[:, :]).then_inc(ph["wT_psum"], 1)
                after(pe, ph["wT_ready"], n)
                bank_again(pe, ph["b_added"], j, n)
                nc.tensor.matmul(S.ps[:, j % 2, 0:D], wT[:, j, :], b2[:, :], start=True, stop=True
                                 ).then_inc(ph["b_psum"], 1)

        @block.vector
        def _(dve):
            v = nc.vector
            for name in ("b_added", "y1_added", "x_done"):
                dve.sem_inc(ph[name], RING)
            for i, t, j, n in tiles(dve):
                x = S.X[:, bass.ds(t, 1), :].squeeze(1)
                after(dve, ph["b_psum"], n)
                v.tensor_tensor(x, S.ps[:, j % 2, 0:D], x, ALU.add).then_inc(ph["b_added"], 1)
                dve.wait_ge(ph[f"y_in{j}"], i * 32 + 32)
                after(dve, ph["b_added"], n)
                v.scalar_tensor_tensor(x, yr[:, j, 0, :], S.w1[:, bass.ds(t, 1)], x, ALU.mult, ALU.add
                                       ).then_inc(ph["y1_added"], 1)
                after(dve, ph["y1_added"], n)
                v.scalar_tensor_tensor(x, yr[:, j, 1, :], S.w2[:, bass.ds(t, 1)], x, ALU.mult, ALU.add
                                       ).then_inc(ph["x_done"], 1)


E1, EH1, EH2, SH2 = 4, 128, 64, 128


def project_layer1(nc, S, A):
    with Phase(nc, "project_layer1") as ph:
        ph.ps = S.ps
        W = ph.sb("w_src_dst", [P, 2, 2, D])
        rows = ph.sb("b_src_dst_kw_kb_vw_vb", [P, 6, D])
        stats, mv, rstd = ln_scratch(ph)
        xn = ph.sb("xn_ring", [P, RING, D])
        xT = ph.sb("xn_T", [P, RING, 2, P])
        el = ph.sb("el_rows", [P, RING, D])
        dn = ph.sb("head_centred", [P, RING * HEADS, HD])
        sq = ph.sb("head_squares", [P, RING * HEADS, HD])
        hm = ph.sb("head_mean", [P, RING * HEADS])
        hr = ph.sb("head_rstd", [P, RING * HEADS])
        kf = ph.sb("k_rows", [P, RING, D])
        vf = ph.sb("v_rows", [P, RING, D])
        block = ph.block()
        five_rows = lambda m: rows[:, m, :].unsqueeze(1).broadcast_to([P, RING, D])
        per_head = lambda x: x.unsqueeze(2).broadcast_to([P, RING * HEADS, HD])
        heads = lambda x: x.rearrange("p r (h m) -> p (r h) m", m=HD)

        @block.sync
        def _(sp):
            for m, src in enumerate(("Ws", "Wd")):
                sp.dma_start(W[:, :, m, :], A[src].rearrange("(c p) n -> p c n", p=P)).then_inc(ph["weights_in"], 16)
            for m, src in enumerate(("bs", "bd", "kw", "kb", "vw", "vb")):
                sp.dma_start(rows[:, m, :], bcast(A[src])).then_inc(ph["weights_in"], 16)
            with sp.Fori(0, T5) as i:
                sp.wait_ge(ph["el_five"], i + 1)
                sp.dma_start(S.eltab_dram[bass.ds(i * (RING * P), RING * P), :].rearrange("(t p) d -> p t d", p=P),
                             el[:, :, :]).then_inc(ph["el_out"], 16)
            sp.wait_ge(ph["el_out"], 16 * T5 + 16)

        @block.gpsimd
        def _(pool):
            g = nc.gpsimd
            pool.sem_inc(ph["xn_kept"], RING)
            pool.sem_inc(ph["v_scaled"], 1)
            pool.wait_ge(ph["weights_in"], 128)
            with pool.Fori(0, T5) as i:
                for j in range(RING):
                    after(pool, ph["xn_ready"], i * RING + (j + 1))
                    g.tensor_copy(S.XN[:, bass.ds(i * RING + j, 1), :], xn[:, j:j + 1, :]
                                  ).then_inc(ph["xn_kept"], 1)
                pool.wait_ge(ph["normed"], i + 1)
                pool.wait_ge(ph["kv_used"], i * RING + RING)
                g.tensor_tensor(vf[:, :, :], dn[:, :, :].rearrange("p (r h) m -> p r (h m)", r=RING), five_rows(4),
                                ALU.mult).then_inc(ph["v_scaled"], 1)
                pool.wait_ge(ph["v_scaled"], i + 2)
                g.tensor_tensor(vf[:, :, :], vf[:, :, :], five_rows(5), ALU.add).then_inc(ph["v_ready"], 1)

        @block.vector
        def _(dve):
            v, own = nc.vector, Own(dve, ph["dve_own"])
            layernorm_stats(nc, dve, own, S.X, stats, mv, rstd, ph["eps_done"], ph["sqrt_done"])
            dve.wait_ge(ph["weights_in"], 128)
            for name in ("xn_ready", "er_done"):
                dve.sem_inc(ph[name], RING)
            dve.sem_inc(ph["el_out"], 16)
            with dve.Fori(0, T5) as i:
                norm_five(nc, ph, dve, S.X, mv, rstd, xn, i)
                after(dve, ph["xn_ready"], i * RING + RING)
                v.tensor_reduce(hm[:, :], heads(xn[:, :, :]), AX.X, ALU.add).then_inc(ph["head_sums"], 1)
                dve.wait_ge(ph["el_out"], i * 16 + 16)
                for j in range(RING):
                    n = i * RING + (j + 1)
                    after(dve, ph["p_psum"], n)
                    v.tensor_tensor(el[:, j, :], S.ps[:, j % 2, 0:D], rows[:, 0, :], ALU.add)
                    ins = v.tensor_tensor(S.QF[:, bass.ds(i * RING + j, 1), :].squeeze(1), S.ps[:, j % 2, D:2 * D],
                                          rows[:, 1, :], ALU.add)
                    ins.then_inc(ph["er_done"], 1)
                dve.wait_ge(ph["head_sums"], i + 1)
                v.tensor_scalar(hm[:, :], hm[:, :], 1.0 / HD, None, ALU.mult).then_inc(ph["el_five"], 1)
                dve.wait_ge(ph["el_five"], i + 1)
                dve.wait_ge(ph["v_scaled"], i + 1)
                v.tensor_tensor(dn[:, :, :], heads(xn[:, :, :]), per_head(hm[:, :]), ALU.subtract
                                ).then_inc(ph["centred"], 1)
                dve.wait_ge(ph["squared"], i + 1)
                v.tensor_reduce(hr[:, :], sq[:, :, :], AX.X, ALU.add).then_inc(ph["square_sums"], 1)
                dve.wait_ge(ph["stds"], i + 1)
                v.tensor_scalar_add(hr[:, :], hr[:, :], 1e-5).then_inc(ph["std_eps"], 1)
                dve.wait_ge(ph["std_eps"], i + 1)
                v.reciprocal(hr[:, :], hr[:, :]).then_inc(ph["std_inv"], 1)
                dve.wait_ge(ph["std_inv"], i + 1)
                v.tensor_tensor(dn[:, :, :], dn[:, :, :], per_head(hr[:, :]), ALU.mult).then_inc(ph["normed"], 1)
                dve.wait_ge(ph["normed"], i + 1)
                dve.wait_ge(ph["kv_used"], i * RING + RING)
                v.tensor_tensor(kf[:, :, :], dn[:, :, :].rearrange("p (r h) m -> p r (h m)", r=RING), five_rows(2),
                                ALU.mult).then_inc(ph["k_scaled"], 1)
                dve.wait_ge(ph["k_scaled"], i + 1)
                v.tensor_tensor(kf[:, :, :], kf[:, :, :], five_rows(3), ALU.add).then_inc(ph["k_ready"], 1)
            dve.wait_ge(ph["kv_used"], NODE_TILES + RING)
            for c in range(2):
                own(v.scalar_tensor_tensor(S.kvbd[:, c, 0:P], S.ps[:, 6 + c, 0:P], 1.0 / NODES, S.head_blocks[:, :],
                                           ALU.mult, ALU.mult))
            own.wait()

        @block.scalar
        def _(act):
            ln_root(nc, ph, act, rstd)
            act.sem_inc(ph["xT_ready"], RING)
            with act.Fori(0, T5) as i:
                for j in range(RING):
                    n = i * RING + (j + 1)
                    again(act, ph["p_psum"], n)
                    copy_transposed(nc, ph, act, j, n, 4 + j % 2, xT)
                act.wait_ge(ph["centred"], i + 1)
                nc.scalar.activation(sq[:, :, :], dn[:, :, :], ACT.Square).then_inc(ph["squared"], 1)
                act.wait_ge(ph["square_sums"], i + 1)
                nc.scalar.activation(hr[:, :], hr[:, :], ACT.Sqrt, scale=1.0 / (HD - 1)).then_inc(ph["stds"], 1)

        @block.tensor
        def _(pe):
            pe.wait_ge(ph["weights_in"], 128)
            for name in ("xT_psum", "p_psum", "kv_used"):
                pe.sem_inc(ph[name], RING)

            def group(i, first, last):
                for j in range(RING):
                    n = i * RING + (j + 1)
                    after(pe, ph["xn_ready"], n)
                    bank_again(pe, ph["xT_ready"], j, n)
                    transpose_tile(nc, ph, pe, xn, j, 4 + j % 2, S.ident)
                    after(pe, ph["xT_ready"], n)
                    bank_again(pe, ph["er_done"], j, n)
                    for c in range(2):
                        ins = nc.tensor.matmul(S.ps[:, j % 2, :], xT[:, j, c, :],
                                               W[:, c, :, :].rearrange("p a n -> p (a n)"), start=c == 0, stop=c == 1)
                    ins.then_inc(ph["p_psum"], 1)
                pe.wait_ge(ph["k_ready"], i + 1)
                pe.wait_ge(ph["v_ready"], i + 1)
                for j in range(RING):
                    rows_ = LAST_ROWS if last and j == RING - 1 else P
                    for c in range(2):
                        ins = nc.tensor.matmul(S.ps[:, 6 + c, 0:P], kf[0:rows_, j, c * P:(c + 1) * P],
                                               vf[0:rows_, j, c * P:(c + 1) * P], start=first and j == 0,
                                               stop=last and j == RING - 1)
                    ins.then_inc(ph["kv_used"], 1)
            group(0, True, False)
            with pe.Fori(1, T5 - 1) as i:
                group(i, False, False)
            group(T5 - 1, False, True)


def score_layer1(nc, S, A):
    N = GROUP * D
    with Phase(nc, "score_layer1") as ph:
        idx = ph.sb("gather_idx", [P, HALVES, GROUP], I32)
        got = ph.sb("el_of_sources", [P, HALVES, GROUP, D])
        relB = ph.sb("rel_bcast", [P, HALVES, GROUP * P])
        hot = ph.sb("dst_onehot_T", [P, HALVES, GROUP * P])
        attn = ph.sb("attn_rows", [P, D])
        fifth = ph.sb("fifth_of_z", [P, N])
        dots = ph.sb("dots", [P, GROUP])
        ps2 = S.ps[:, :, :].rearrange("p b n -> p (b n)")
        z = lambda h: ps2[:, h * 1536:h * 1536 + N]
        block = ph.block()
        gather_edges(nc, S, ph, block, S.eltab_dram, idx, got, relB,
                     before=lambda sp: sp.dma_start(attn[:, :], bcast(A["attn"])).then_inc(ph["attn_in"], 16),
                     slope=lambda act, i, h, k, n: (
                         act.wait_ge(ph["rows_used"], n + HALVES),
                         act.wait_ge(ph["dotted"], n + HALVES - 1),
                         nc.scalar.activation(fifth[:, :], z(h), ACT.Copy, scale=0.2).then_inc(ph["sloped"], 1)))

        @block.vector
        def _(dve):
            v = nc.vector
            dve.wait_ge(ph["attn_in"], 16)
            for name in ("hot_ready", "rows_used", "dotted"):
                dve.sem_inc(ph[name], HALVES)
            for i, h, k, n in groups(dve):
                onehot_T(nc, S, ph, dve, hot, relB, i, h, n)
                dve.wait_ge(ph[f"gathered{h}"], i * (16 * GROUP) + 16 * GROUP)
                dve.wait_ge(ph["dst_psum"], n + HALVES)
                v.tensor_tensor(z(h), z(h), got[:, h, :, :].rearrange("p g d -> p (g d)"), ALU.add
                                ).then_inc(ph["rows_used"], 1)
                dve.wait_ge(ph["sloped"], n)
                v.tensor_tensor(z(h), z(h), fifth[:, :], ALU.max).then_inc(ph["leaky"], 1)
                dve.wait_ge(ph["leaky"], n)
                for j in range(GROUP):
                    ins = v.tensor_tensor_reduce(out=z(h)[:, j * D:(j + 1) * D], in0=z(h)[:, j * D:(j + 1) * D], in1=attn[:, :],
                                                 scale=1.0, scalar=0.0, op0=ALU.mult, op1=ALU.add,
                                                 accum_out=dots[:, j:j + 1])
                ins.then_inc(ph["dotted"], 1)
                dve.wait_ge(ph["dotted"], n + HALVES)
                v.tensor_copy(S.scoreX[:, bass.ds(k * GROUP, GROUP)], dots[:, :])

        @block.tensor
        def _(pe):
            pe.sem_inc(ph["dst_psum"], HALVES)
            for i, h, k, n in groups(pe):
                pe.wait_ge(ph["hot_ready"], n + HALVES)
                pe.wait_ge(ph["dotted"], n)
                for j in range(GROUP):
                    b = dst_block(pe, S, k, j)
                    last = nc.tensor.matmul(z(h)[:, j * D:(j + 1) * D], hot[:, h, j * P:(j + 1) * P],
                                            S.QF[:, bass.ds(b, 1), :].squeeze(1), start=True, stop=True)
                last.then_inc(ph["dst_psum"], 1)


def mix_layer1(nc, S, A):
    with Phase(nc, "mix_layer1") as ph:
        ph.ps = S.ps
        xr = ph.sb("xn_ring", [P, RING, D])
        xT = ph.sb("xn_T", [P, RING, 2, P])
        block = ph.block()

        @block.gpsimd
        def _(pool):
            stage_tiles(nc, ph, pool, S.XN, xr, "x_staged", "xT_psum")

        @block.scalar
        def _(act):
            act.sem_inc(ph["xT_ready"], RING)
            for i, t, j, n in tiles(act):
                again(act, ph["m_psum"], n)
                copy_transposed(nc, ph, act, j, n, 4 + j % 2, xT)

        @block.tensor
        def _(pe):
            pe.sem_inc(ph["xT_psum"], RING)
            pe.sem_inc(ph["m_psum"], RING)
            for i, t, j, n in tiles(pe):
                after(pe, ph["x_staged"], n)
                bank_again(pe, ph["xT_ready"], j, n)
                transpose_tile(nc, ph, pe, xr, j, 4 + j % 2, S.ident)
                after(pe, ph["xT_ready"], n)
                bank_again(pe, ph["added"], j, n)
                for c in range(2):
                    ins = nc.tensor.matmul(S.ps[:, j % 2, c * P:(c + 1) * P], xT[:, j, c, :], S.kvbd[:, c, 0:P],
                                           start=True, stop=True)
                ins.then_inc(ph["m_psum"], 1)

        @block.vector
        def _(dve):
            v = nc.vector
            add_edge_sums(nc, ph, S, dve)
            dve.sem_inc(ph["added"], RING)
            dve.sem_inc(ph["xn_added"], RING)
            for i, t, j, n in tiles(dve):
                x = S.X[:, bass.ds(t, 1), :].squeeze(1)
                after(dve, ph["m_psum"], n)
                v.tensor_tensor(x, S.ps[:, j % 2, 0:D], x, ALU.add).then_inc(ph["added"], 1)
                after(dve, ph["added"], n)
                v.tensor_tensor(x, x, S.XN[:, bass.ds(t, 1), :].squeeze(1), ALU.add)


def gates_layer1(nc, S, A):
    with Phase(nc, "gates_layer1") as ph:
        ph.ps = S.ps
        gW = ph.sb("w_gate", [P, 2, E1])
        gb = ph.sb("b_gate", [P, E1])
        stats, mv, rstd = ln_scratch(ph)
        xf = ph.sb("xf_ring", [P, RING, D])
        xT = ph.sb("xf_T", [P, RING, 2, P])
        lg = ph.sb("logits4", [P, NODE_TILES, E1])
        mx = ph.sb("logit_max", [P, NODE_TILES])
        top = ph.sb("top8", [P, NODE_TILES, 8])
        idx = ph.sb("top8_idx", [P, NODE_TILES, 8], U32)
        idxf = ph.sb("top8_idx_f", [P, NODE_TILES, 8])
        hot1 = ph.sb("hot1", [P, NODE_TILES, E1])
        hot2 = ph.sb("hot2", [P, NODE_TILES, E1])
        block = ph.block()
        wide = lambda x: x.unsqueeze(2).broadcast_to([P, NODE_TILES, E1])

        @block.sync
        def _(sp):
            sp.dma_start(gW[:, :, :], A["gW"].rearrange("(c p) n -> p c n", p=P)).then_inc(ph["weights_in"], 16)
            sp.dma_start(gb[:, :], bcast(A["gb"])).then_inc(ph["weights_in"], 16)
            sp.wait_ge(ph["weights_in"], 32)

        @block.gpsimd
        def _(pool):
            keep_tiles(nc, ph, pool, xf, S.QF)

        @block.vector
        def _(dve):
            v, own = nc.vector, Own(dve, ph["dve_own"])
            layernorm_stats(nc, dve, own, S.X, stats, mv, rstd, ph["eps_done"], ph["sqrt_done"])
            dve.wait_ge(ph["weights_in"], 32)
            for name in ("xn_ready", "logits"):
                dve.sem_inc(ph[name], RING)
            for i, t, j, n in tiles(dve):
                if j == 0:
                    norm_five(nc, ph, dve, S.X, mv, rstd, xf, i)
                after(dve, ph["l_psum"], n)
                v.tensor_tensor(lg[:, bass.ds(t, 1), :].squeeze(1), S.ps[:, j % 2, 0:E1], gb[:, :], ALU.add
                                ).then_inc(ph["logits"], 1)
            after(dve, ph["logits"], NODE_TILES)
            own(v.memset(S.logits[:, :, :], -1.0))
            own(v.tensor_reduce(mx[:, :], lg[:, :, :], AX.X, ALU.max))
            own.wait()
            v.tensor_tensor(lg[:, :, :], lg[:, :, :], wide(mx[:, :]), ALU.subtract).then_inc(ph["shifted"], 1)
            dve.wait_ge(ph["exps"], 1)
            own(v.tensor_reduce(mx[:, :], lg[:, :, :], AX.X, ALU.add))
            own.wait()
            own(v.reciprocal(mx[:, :], mx[:, :]))
            own.wait()
            own(v.tensor_tensor(S.logits[:, :, 0:E1], lg[:, :, :], wide(mx[:, :]), ALU.mult))
            own.wait()
            top_two(nc, own, S.logits, top, idx, idxf, hot1, hot2, S.iota_row, 8)
            v.tensor_tensor(S.w2[:, :], top[:, :, 1], top[:, :, 0], ALU.subtract).then_inc(ph["gap"], 1)
            dve.wait_ge(ph["gap_exp"], 1)
            own(v.tensor_scalar_add(S.w1[:, :], S.w2[:, :], 1.0))
            own.wait()
            own(v.reciprocal(S.w1[:, :], S.w1[:, :]))
            own.wait()
            own(v.tensor_tensor(S.w2[:, :], S.w2[:, :], S.w1[:, :], ALU.mult))
            own.wait()
            own(v.tensor_tensor(hot1[:, :, :], hot1[:, :, :], wide(S.w1[:, :]), ALU.mult))
            own(v.tensor_tensor(hot2[:, :, :], hot2[:, :, :], wide(S.w2[:, :]), ALU.mult))
            own.wait()
            own(v.memset(S.wexp[:, :, :], 1.0))
            own.wait()
            own(v.tensor_tensor(S.wexp[:, :, 0:E1], hot1[:, :, :], hot2[:, :, :], ALU.add))
            own.wait()

        @block.scalar
        def _(act):
            ln_root(nc, ph, act, rstd)
            act.sem_inc(ph["xT_ready"], RING)
            for i, t, j, n in tiles(act):
                again(act, ph["l_psum"], n)
                copy_transposed(nc, ph, act, j, n, 4 + j % 2, xT)
            act.wait_ge(ph["shifted"], 1)
            nc.scalar.activation(lg[:, :, :], lg[:, :, :], ACT.Exp).then_inc(ph["exps"], 1)
            act.wait_ge(ph["gap"], 1)
            nc.scalar.activation(S.w2[:, :], S.w2[:, :], ACT.Exp).then_inc(ph["gap_exp"], 1)

        @block.tensor
        def _(pe):
            pe.wait_ge(ph["weights_in"], 32)
            for name in ("xT_psum", "l_psum"):
                pe.sem_inc(ph[name], RING)
            for i, t, j, n in tiles(pe):
                after(pe, ph["xn_ready"], n)
                bank_again(pe, ph["xT_ready"], j, n)
                transpose_tile(nc, ph, pe, xf, j, 4 + j % 2, S.ident)
                after(pe, ph["xT_ready"], n)
                bank_again(pe, ph["logits"], j, n)
                for c in range(2):
                    ins = nc.tensor.matmul(S.ps[:, j % 2, 0:E1], xT[:, j, c, :], gW[:, c, :],
                                           start=c == 0, stop=c == 1)
                ins.then_inc(ph["l_psum"], 1)


def ffn_layer1(nc, S, A):
    with Phase(nc, "ffn_layer1") as ph:
        ph.ps = S.ps
        sW1 = ph.sb("shared_w1", [P, 2, D])
        sW2 = ph.sb("shared_w2", [P, 2, SH2])
        sW3 = ph.sb("shared_w3", [P, D])
        eW1 = ph.sb("expert_w1", [P, E1, 2, EH1])
        eW2 = ph.sb("expert_w2", [P, E1, EH2])
        eW3 = ph.sb("expert_w3", [EH2, E1, D])
        b3 = ph.sb("output_biases", [E1 + 1, D])
        bT = ph.sb("hidden_biases", [P, 3 + E1])
        bE2 = ph.sb("expert_b2", [EH2, E1])
        xr = ph.sb("xf_ring", [P, RING, D])
        wr = ph.sb("weights_ring", [P, RING, E1 + 1])
        xT = ph.sb("xf_T", [P, RING, 2, P])
        wT = ph.sb("weights_T", [E1 + 1, RING, P])
        s1 = ph.sb("shared_h1_T", [P, RING, 2, P])
        s2 = ph.sb("shared_h2_T", [P, RING, P])
        e1 = ph.sb("expert_h1_T", [P, RING, E1, P])
        e2 = ph.sb("expert_h2_T", [EH2, RING, E1, P])
        block = ph.block()
        ps = S.ps

        @block.sync
        def _(sp):
            for dst, src in ((sW1[:, :, :], A["sW1"].rearrange("(c p) n -> p c n", p=P)),
                             (sW2[:, :, :], A["sW2"].rearrange("(c p) n -> p c n", p=P)), (sW3[:, :], A["sW3"]),
                             (eW2[:, :, :], A["eW2b"].rearrange("e p n -> p e n")),
                             (eW3[:, :, :], A["eW3b"].rearrange("e p n -> p e n")), (b3[:, :], A["b3"]),
                             (bT[:, :], A["bT"]), (bE2[:, :], A["bE2"])):
                sp.dma_start(dst, src).then_inc(ph["weights_in"], 16)
            for e in range(E1):
                sp.dma_start(eW1[:, e, :, :], A["eW1b"][e, :, :].rearrange("(c p) n -> p c n", p=P)
                             ).then_inc(ph["weights_in"], 16)
            sp.wait_ge(ph["weights_in"], 16 * (8 + E1))

        @block.gpsimd
        def _(pool):
            pool.sem_inc(ph["staged"], RING)
            for i, t, j, n in tiles(pool):
                again(pool, ph["xT_psum"], n)
                nc.gpsimd.tensor_copy(wr[:, j, :], S.wexp[:, bass.ds(t, 1), 0:E1 + 1].squeeze(1))
                nc.gpsimd.tensor_copy(xr[:, j:j + 1, :], S.QF[:, bass.ds(t, 1), :]).then_inc(ph["staged"], 1)

        @block.tensor
        def _(pe):
            mm = nc.tensor.matmul
            pe.wait_ge(ph["weights_in"], 16 * (8 + E1))
            for name in ("xT_psum", "h1_psum", "h2_psum", "o_psum"):
                pe.sem_inc(ph[name], RING)
            for i, t, j, n in tiles(pe):
                after(pe, ph["staged"], n)
                pe.wait_ge(ph["xT_ready"], n + RING - 1)
                nc.tensor.transpose(ps[0:E1 + 1, 0, D:D + P], wr[:, j, :], S.ident[:, :])
                transpose_tile(nc, ph, pe, xr, j, 0, S.ident)
                after(pe, ph["xT_ready"], n)
                pe.wait_ge(ph["h1_ready"], n + RING - 1)
                for m in range(2):
                    for c in range(2):
                        mm(ps[:, 1, m * P:(m + 1) * P], sW1[:, c, m * P:(m + 1) * P], xT[:, j, c, :],
                           start=c == 0, stop=c == 1)
                for e in range(E1):
                    for c in range(2):
                        ins = mm(ps[:, 2, e * P:(e + 1) * P], eW1[:, e, c, :], xT[:, j, c, :],
                                 start=c == 0, stop=c == 1)
                ins.then_inc(ph["h1_psum"], 1)
                after(pe, ph["h1_ready"], n)
                pe.wait_ge(ph["h2_ready"], n + RING - 1)
                for c in range(2):
                    mm(ps[:, 3, 0:P], sW2[:, c, :], s1[:, j, c, :], start=c == 0, stop=c == 1)
                for e in range(E1):
                    ins = mm(ps[0:EH2, 4, e * P:(e + 1) * P], eW2[:, e, :], e1[:, j, e, :], start=True, stop=True)
                ins.then_inc(ph["h2_psum"], 1)
                after(pe, ph["h2_ready"], n)
                pe.wait_ge(ph["x_done"], n + RING - 1)
                mm(ps[:, 5, 0:D], s2[:, j, :], sW3[:, :], start=True, stop=False)
                mm(ps[:, 5, 0:D], wT[:, j, :], b3[:, :], start=False, stop=True)
                for e in range(E1):
                    ins = mm(ps[:, 6 + e // 2, (e % 2) * D:(e % 2 + 1) * D], e2[:, j, e, :], eW3[:, e, :],
                             start=True, stop=True)
                ins.then_inc(ph["o_psum"], 1)

        @block.scalar
        def _(act):
            a = nc.scalar
            act.wait_ge(ph["weights_in"], 16 * (8 + E1))
            for name in ("xT_ready", "h1_ready", "h2_ready"):
                act.sem_inc(ph[name], RING)
            for i, t, j, n in tiles(act):
                again(act, ph["o_psum"], n)
                after(act, ph["xT_psum"], n)
                a.activation(wT[:, j, :], ps[0:E1 + 1, 0, D:D + P], ACT.Copy)
                copy_transposed(nc, ph, act, j, n, 0, xT)
                after(act, ph["h1_psum"], n)
                for m in range(2):
                    a.activation(s1[:, j, m, :], ps[:, 1, m * P:(m + 1) * P], ACT.Relu, bias=bT[:, m:m + 1])
                for e in range(E1):
                    ins = a.activation(e1[:, j, e, :], ps[:, 2, e * P:(e + 1) * P], ACT.Relu, bias=bT[:, 3 + e:4 + e])
                ins.then_inc(ph["h1_ready"], 1)
                after(act, ph["h2_psum"], n)
                a.activation(s2[:, j, :], ps[:, 3, 0:P], ACT.Relu, bias=bT[:, 2:3])
                for e in range(E1):
                    ins = a.activation(e2[:, j, e, :], ps[0:EH2, 4, e * P:(e + 1) * P], ACT.Relu, bias=bE2[:, e:e + 1])
                ins.then_inc(ph["h2_ready"], 1)

        @block.vector
        def _(dve):
            v = nc.vector
            dve.sem_inc(ph["x_done"], RING)
            dve.sem_inc(ph["x_step"], 1)
            for i, t, j, n in tiles(dve):
                x = S.X[:, bass.ds(t, 1), :].squeeze(1)
                after(dve, ph["o_psum"], n)
                v.tensor_tensor(x, ps[:, 5, 0:D], x, ALU.add).then_inc(ph["x_step"], 1)
                for e in range(E1):
                    dve.wait_ge(ph["x_step"], i * (RING * E1) + (j * E1 + e + 2))
                    ins = v.scalar_tensor_tensor(x, ps[:, 6 + e // 2, (e % 2) * D:(e % 2 + 1) * D],
                                                 S.wexp[:, bass.ds(t, 1), e], x, ALU.mult, ALU.add)
                    ins.then_inc(ph["x_step"] if e < E1 - 1 else ph["x_done"], 1)


def reset_semaphores(nc):
    with Phase(nc, "reset") as ph:
        numbers = sorted(Phase.numbers)
        block = ph.block()

        @block.gpsimd
        def _(pool):
            while numbers:
                first = last = numbers.pop(0)
                while numbers and numbers[0] == last + 1:
                    last = numbers.pop(0)
                pool.sem_clear(range(first, last + 1))
        Phase.numbers.clear()


def write_out(nc, S, out):
    with Phase(nc, "write_out") as ph:
        block = ph.block()

        @block.sync
        def _(sp):
            sp.dma_start(out[0:NODES_PAD - P, :].rearrange("(t p) d -> p t d", p=P),
                         S.X[:, 0:NODE_TILES - 1, :]).then_inc(ph["out"], 16)
            sp.dma_start(out[NODES_PAD - P:NODES, :], S.X[0:LAST_ROWS, NODE_TILES - 1, :]).then_inc(ph["out"], 16)
            sp.wait_ge(ph["out"], 32)


def build(nc, A, out):
    S = State()
    Phase.numbers.clear()
    with ExitStack() as ctx:
        Phase.lasting = ctx

        def sb(name, shape, dt=F32):
            return ctx.enter_context(nc.sbuf_tensor(name, shape, dt))

        def dram(name, shape, dt=F32):
            return nc.dram_tensor(name, shape, dt, kind="Internal").ap()
        S.ps = ctx.enter_context(nc.psum_tensor("ps", [P, 8, 512], F32))
        S.ident = sb("ident", [P, P])
        S.ones = sb("ones", [P, P])
        S.iota_row = sb("iota_row", [P, P])
        S.iota_col = sb("iota_col", [P, 1])
        S.srcX = sb("src_by_step", [P, STEPS], I32)
        S.relX = sb("rel_by_step", [P, STEPS])
        S.validX = sb("valid_by_step", [P, STEPS])
        S.penX = sb("penalty_by_step", [P, STEPS])
        S.scoreX = sb("score_by_step", [P, STEPS])
        S.weightX = sb("weight_by_step", [P, STEPS])
        S.blockI = sb("block_by_step", [1, STEPS], I32)
        S.cut = sb("segment_cuts", [GROUPS, 2, GROUP * P])
        S.row_cut = sb("row_has_cut", [GROUPS, 2])
        S.X = sb("x", [P, NODE_TILES, D])
        S.XN = sb("xn", [P, NODE_TILES, D])
        S.QF = sb("q_features", [P, NODE_TILES, D])
        S.acc = sb("edge_sums", [P, NODE_TILES, D + 1])
        S.qk = sb("q_k_scalars", [P, 2, NODE_TILES])
        S.kvbd = sb("kv_blocks", [P, 2, P + 4])
        S.inv_sum = sb("inv_softmax_sum", [P, NODE_TILES])
        S.node_mask = sb("node_mask", [P, NODE_TILES])
        S.logits = sb("logits", [P, NODE_TILES, E0])
        S.wexp = sb("expert_weights", [P, NODE_TILES, E0])
        S.w1 = sb("first_weight", [P, NODE_TILES])
        S.w2 = sb("second_weight", [P, NODE_TILES])
        S.posI = sb("slots_of_node", [P, 2, NODE_TILES], I32)
        S.slot_node = sb("node_of_slot", [P, SLOT_TILES], I32)
        S.expertI = sb("expert_of_tile", [1, SLOT_TILES], I32)
        S.head_blocks = sb("head_blocks", [P, P])
        S.rel_dram = dram("rel_by_step_rows", (STEPS, P))
        S.key_dram = dram("keys", (STEPS * P + 2,))
        S.htab_dram = dram("h_table", (NODES_PAD, D + 1))
        S.step_dram = dram("rows_by_step", (GROUPS, P, GROUP * D))
        S.xn_dram = dram("xn_table", (NODES_PAD, D))
        S.eltab_dram = dram("el_table", (NODES_PAD, D))
        S.y_dram = dram("y_by_slot", (SLOT_ROWS, D))
        S.layer = 0
        prepare_edges(nc, S, A)
        project_layer0(nc, S, A)
        score_layer0(nc, S, A)
        softmax_weights(nc, S, A, True)
        aggregate(nc, S, A)
        linear_attention(nc, S, A)
        mix_mlp(nc, S, A)
        router(nc, S, A)
        dispatch_plan(nc, S, A)
        expert_inputs(nc, S, A)
        experts(nc, S, A)
        combine(nc, S, A)
        S.layer = 1
        reset_semaphores(nc)
        project_layer1(nc, S, A)
        score_layer1(nc, S, A)
        softmax_weights(nc, S, A, False)
        aggregate(nc, S, A)
        mix_layer1(nc, S, A)
        gates_layer1(nc, S, A)
        ffn_layer1(nc, S, A)
        write_out(nc, S, out)


def layout(inputs):
    import numpy as np
    c = np.ascontiguousarray
    a = {}
    x = np.zeros((NODES_PAD, D), np.float32)
    x[:NODES] = inputs["x"]
    src = np.zeros(EDGE_TILES * P, np.int32)
    src[:EDGES] = inputs["src"]
    dst = np.full(EDGE_TILES * P, PAD_NODE, np.int32)
    dst[:EDGES] = inputs["dst"]
    dst = dst.reshape(EDGE_TILES, P)
    before = np.zeros(EDGE_TILES, np.int32)
    before[1:] = dst[:-1, P - 1]
    a.update(x=x, src=src.reshape(EDGE_TILES, P), dst=dst, dst_before=c(before.reshape(EDGE_CHUNKS, EDGE_ROWS).T))
    a["Wv"] = c(inputs["L0_gnn_Wv"])
    a["bv"] = c(inputs["L0_gnn_bv"])
    a["wq"] = c(inputs["L0_gnn_wq"])
    a["wk"] = c(inputs["L0_gnn_wk"])
    a["bq"] = c(inputs["L0_gnn_bq"]).reshape(1)
    a["bk"] = c(inputs["L0_gnn_bk"]).reshape(1)
    a["WqkvT"] = c(np.asarray(inputs["L0_mix_Wqkv"]).T)
    for name in ("ln1_g", "ln1_b", "ln2_g", "ln2_b"):
        a[name] = c(inputs["L0_mix_" + name])
    a["mW1T"], a["mW2T"] = c(np.asarray(inputs["L0_mix_W1"]).T), c(np.asarray(inputs["L0_mix_W2"]).T)
    a["mb1"] = c(np.asarray(inputs["L0_mix_b1"]).reshape(2, P).T)
    a["mb2"] = c(inputs["L0_mix_b2"])
    a["Wr"], a["br"] = c(inputs["L0_ffn_Wr"]), c(inputs["L0_ffn_br"])
    a["eW1"] = c(inputs["L0_ffn_W1"]).reshape(E0 * D, HID)
    a["eW2"] = c(inputs["L0_ffn_W2"]).reshape(E0 * HID, D)
    a["eb2"] = c(inputs["L0_ffn_b2"])
    a["eSmall"] = c(np.concatenate([np.asarray(inputs["L0_ffn_" + n]).reshape(E0, -1, P).transpose(0, 2, 1)
                                    for n in ("ln_g", "ln_b", "b1")], axis=2))
    for name, key in (("Ws", "W_src"), ("bs", "b_src"), ("Wd", "W_dst"), ("bd", "b_dst"), ("attn", "attn")):
        a[name] = c(inputs["L1_gnn_" + key])
    for name, key in (("kw", "kln_weight"), ("kb", "kln_bias"), ("vw", "vln_weight"), ("vb", "vln_bias")):
        a[name] = c(inputs["L1_mix_" + key]).reshape(D)
    f = {k[7:]: np.asarray(v) for k, v in inputs.items() if k.startswith("L1_ffn_")}
    a.update(sW1=c(f["sW1"]), sW2=c(f["sW2"]), sW3=c(f["sW3"]), eW1b=c(f["eW1"]), eW2b=c(f["eW2"]), eW3b=c(f["eW3"]),
             gW=c(f["gW"]), gb=c(f["gb"]), b3=c(np.concatenate([f["eb3"], f["sb3"][None]], axis=0)),
             bT=c(np.concatenate([f["sb1"].reshape(2, P), f["sb2"].reshape(1, P), f["eb1"]], axis=0).T),
             bE2=c(f["eb2"].T))
    return a


def kernel(**inputs):
    import numpy as np
    import concourse.bacc as bacc
    from concourse.bass_utils import run_bass_kernel_spmd
    nc = bacc.Bacc("TRN2", target_bir_lowering=False, num_devices=1)
    arrays = {f"in_{k}": v for k, v in layout(inputs).items()}
    A = {k[3:]: nc.dram_tensor(k, v.shape, mybir.dt.from_np(v.dtype), kind="ExternalInput").ap()
         for k, v in arrays.items()}
    out = nc.dram_tensor("out", (NODES, D), F32, kind="ExternalOutput").ap()
    build(nc, A, out)
    return run_bass_kernel_spmd(nc, [arrays], core_ids=[0]).results[0]["out"]
```

```python
import concourse.bass as bass
from concourse import mybir
from contextlib import ExitStack

F32 = mybir.dt.float32
I32 = mybir.dt.int32
U32 = mybir.dt.uint32
ALU = mybir.AluOpType
ACT = mybir.ActivationFunctionType
AX = mybir.AxisListType

P = 128
NODES, D = 3125, 256
NODE_TILES = -(-NODES // P)
NODES_PAD = NODE_TILES * P
LAST_ROWS = NODES - (NODE_TILES - 1) * P
PAD_NODE = NODES_PAD - 1
EDGES = 50000
EDGE_CHUNKS = 4
EDGE_ROWS = 98
EDGE_TILES = EDGE_CHUNKS * EDGE_ROWS
GROUP = 5
GROUPS = 84
STEPS = GROUP * GROUPS
HEADS, HD = 8, 32
E0, HID = 8, 1024
SLOT_TILES = 56
SLOTS = SLOT_TILES * P
SLOT_ROWS = SLOTS + P
BIG = 1e30
T5 = NODE_TILES // 5


class Own:

    def __init__(self, eng, sem):
        self.eng, self.sem = eng, sem
        self.total = 0
        self.i = None

    def __call__(self, ins):
        ins.then_inc(self.sem, 1)
        self.total += 1
        return ins

    def wait(self):
        if self.i is None:
            self.eng.wait_ge(self.sem, self.total)
        else:
            self.eng.wait_ge(self.sem, self.i * self.per + (self.total - self.first * self.per))

    def loop(self, i, per, first=0):
        self.i, self.per, self.first, self.at = i, per, first, self.total

    def end(self, last):
        assert self.total - self.at == self.per, (self.total - self.at, self.per)
        self.total += (last - self.first - 1) * self.per
        self.i = None


class State:
    pass


class Phase:

    numbers = set()
    lasting = None

    def __init__(self, nc, tag):
        self.nc, self.tag, self.ctx, self.sems = nc, tag, ExitStack(), {}

    def __enter__(self):
        self.ctx.__enter__()
        return self

    def __exit__(self, *a):
        return self.ctx.__exit__(*a)

    def sb(self, name, shape, dt=F32):
        return self.ctx.enter_context(self.nc.sbuf_tensor(f"{self.tag}_{name}", shape, dt))

    def sem(self, name):
        sem = self.ctx.enter_context(self.nc.semaphore(f"{self.tag}_{name}"))
        self.numbers.add(sem.num)
        return sem

    def __getitem__(self, name):
        if name not in self.sems:
            self.sems[name] = self.sem(name)
        return self.sems[name]

    def for_gathers(self, *names):
        for name in names:
            self.sems[name] = self.lasting.enter_context(self.nc.semaphore(f"{self.tag}_{name}"))

    def block(self):
        return self.ctx.enter_context(self.nc.Block())


def bcast(vec):
    return vec.partition_broadcast(P)


def layernorm_stats(nc, dve, own, src, stats, mv, rstd, eps_done, sqrt_done, eps=1e-5):
    for t in range(NODE_TILES):
        own(nc.vector.bn_stats(stats[:, t, :], src[:, t, :]))
    own.wait()
    for t in range(NODE_TILES):
        own(nc.vector.bn_aggr(mv[:, t, :], stats[:, t, :]))
    own.wait()
    nc.vector.tensor_scalar_add(rstd[:, :], mv[:, :, 1], eps).then_inc(eps_done, 1)
    dve.wait_ge(sqrt_done, 1)
    own(nc.vector.reciprocal(rstd[:, :], rstd[:, :]))
    own.wait()


def prepare_edges(nc, S, A):
    with Phase(nc, "prepare_edges") as ph:
        srcI = ph.sb("src_rows_i", [EDGE_ROWS, EDGE_CHUNKS, P], I32)
        dstI = ph.sb("dst_rows_i", [EDGE_ROWS, EDGE_CHUNKS, P], I32)
        startI = ph.sb("dst_before_tile_i", [EDGE_ROWS, EDGE_CHUNKS], I32)
        blkI = ph.sb("block_i", [EDGE_ROWS, 2, EDGE_CHUNKS], I32)
        srcF = ph.sb("src_rows", [EDGE_ROWS, EDGE_CHUNKS, P])
        dstF = ph.sb("dst_rows", [EDGE_ROWS, EDGE_CHUNKS, P])
        first = ph.sb("first_step", [EDGE_ROWS, 2, EDGE_CHUNKS])
        tile_no = ph.sb("tile_no", [EDGE_ROWS, 2, EDGE_CHUNKS])
        step_row = ph.sb("step_row", [P, STEPS])
        step_col = ph.sb("step_col", [GROUPS, GROUP])
        reached = ph.sb("reached", [EDGE_ROWS, EDGE_CHUNKS, STEPS])
        pick = ph.sb("pick", [EDGE_ROWS, EDGE_CHUNKS, STEPS])
        blk = ph.sb("block_of_step", [P, STEPS])
        blkT = ph.sb("block_of_step_col", [GROUPS, GROUP])
        relR = ph.sb("rel_rows_sb", [GROUPS, GROUP, P])
        keyR = ph.sb("key_rows_sb", [GROUPS, GROUP, P])
        tmpR = ph.sb("tmp_rows", [GROUPS, GROUP, P])
        edge = ph.sb("key_ends", [1, 2])
        keyS = ph.sb("key_scan", [GROUPS, 3, GROUP * P])
        zero = ph.sb("zeros", [P, D])
        loaded, made, own_s, got, rows_out, ends_out, keys_in, zs = (ph.sem(n) for n in (
            "edge_loads", "pool_made", "dve_own", "pe_done", "rows_out", "ends_out", "keys_in", "zero_out"))
        block = ph.block()

        @block.vector
        def _(dve):
            v, own = nc.vector, Own(dve, own_s)
            dve.wait_ge(loaded, 64)
            dve.wait_ge(made, 6)
            own(v.tensor_copy(srcF[:, :, :], srcI[:, :, :]))
            own(v.tensor_copy(dstF[:, :, :], dstI[:, :, :]))
            own(v.tensor_scalar(blkI[:, 0, :], startI[:, :], 7, None, ALU.arith_shift_right))
            own(v.tensor_scalar(blkI[:, 1, :], dstI[:, :, P - 1], 7, None, ALU.arith_shift_right))
            own.wait()
            own(v.tensor_copy(first[:, :, :], blkI[:, :, :]))
            own.wait()
            own(v.tensor_tensor(first[:, :, :], first[:, :, :], tile_no[:, :, :], ALU.add))
            own.wait()
            for c in range(EDGE_CHUNKS):
                own(v.tensor_scalar(reached[:, c, :], step_row[0:EDGE_ROWS, :], first[:, 0, c:c + 1], None, ALU.is_ge))
            own.wait()
            for c in range(EDGE_CHUNKS):
                own(v.scalar_tensor_tensor(pick[:, c, :], step_row[0:EDGE_ROWS, :], first[:, 1, c:c + 1],
                                           reached[:, c, :], ALU.is_lt, ALU.mult))
            own.wait()
            S.picked = own.total
            dve.wait_ge(got, 1)
            own(v.tensor_copy(S.srcX[:, :], S.ps[:, 0, 0:STEPS]))
            own(v.scalar_tensor_tensor(blk[:, :], step_row[:, :], 1.0, S.ps[:, 2, 0:STEPS], ALU.add, ALU.subtract))
            own(v.scalar_tensor_tensor(blkT[:, :], step_col[:, :], 1.0, S.ps[0:GROUPS, 5, 0:GROUP], ALU.add,
                                       ALU.subtract))
            own.wait()
            own(v.tensor_scalar_min(blk[:, :], blk[:, :], float(NODE_TILES - 1)))
            own(v.tensor_scalar_min(blkT[:, :], blkT[:, :], float(NODE_TILES - 1)))
            own.wait()
            own(v.tensor_copy(S.blockI[:, :, 0:GROUP], blk[0:1, :].rearrange("p (k j) -> p k j", j=GROUP)))
            own(v.scalar_tensor_tensor(S.relX[:, :], blk[:, :], -float(P), S.ps[:, 1, 0:STEPS], ALU.mult, ALU.add))
            for k in range(GROUP):
                src = S.ps[0:GROUPS, 3 + k // 4, (k % 4) * P:(k % 4 + 1) * P]
                own(v.tensor_scalar(blkT[:, k:k + 1], blkT[:, k:k + 1], -float(P), None, ALU.mult))
                own.wait()
                own(v.tensor_scalar(relR[:, k, :], src, blkT[:, k:k + 1], None, ALU.add))
            own.wait()
            own(v.tensor_scalar(S.validX[:, :], S.relX[:, :], 0.0, None, ALU.is_ge))
            own(v.tensor_scalar(keyR[:, :, :], relR[:, :, :], 0.0, None, ALU.is_ge))
            own.wait()
            own(v.scalar_tensor_tensor(S.validX[:, :], S.relX[:, :], float(P - 1), S.validX[:, :], ALU.is_le, ALU.mult))
            own(v.scalar_tensor_tensor(keyR[:, :, :], relR[:, :, :], float(P - 1), keyR[:, :, :], ALU.is_le, ALU.mult))
            own.wait()
            own(v.tensor_scalar(S.penX[:, :], S.validX[:, :], BIG, -BIG, ALU.mult, ALU.add))
            own(v.scalar_tensor_tensor(tmpR[:, :, :], relR[:, :, :], 1.0, keyR[:, :, :], ALU.add, ALU.mult))
            own.wait()
            own(v.tensor_scalar(keyR[:, :, :], tmpR[:, :, :], -1.0, None, ALU.add))
            S.rows_ready = own.total
            dve.wait_ge(keys_in, 48)
            for n, o in ((0, 0), (1, 2)):
                own(v.tensor_tensor(S.cut[:, n, :], keyS[:, 1, :], keyS[:, o, :], ALU.not_equal))
            own.wait()
            own(v.tensor_scalar(S.cut[:, :, :], S.cut[:, :, :], -BIG, None, ALU.mult))
            own.wait()
            for n in range(2):
                own(v.tensor_reduce(S.row_cut[:, n:n + 1], S.cut[:, n, :], AX.X, ALU.min))
            own.wait()

        @block.sync
        def _(sp):
            sp.dma_start(srcI[:, :, :], A["src"].rearrange("(c p) e -> p c e", p=EDGE_ROWS)).then_inc(loaded, 16)
            sp.dma_start(dstI[:, :, :], A["dst"].rearrange("(c p) e -> p c e", p=EDGE_ROWS)).then_inc(loaded, 16)
            sp.dma_start(startI[:, :], A["dst_before"]).then_inc(loaded, 16)
            sp.dma_start(S.X[:, :, :], A["x"].rearrange("(t p) d -> p t d", p=P)).then_inc(loaded, 16)
            sp.wait_ge(own_s, S.rows_ready)
            sp.dma_start(S.rel_dram.rearrange("(k p) e -> p k e", p=GROUPS), relR[:, :, :]).then_inc(rows_out, 16)
            key_rows = S.key_dram[1:1 + STEPS * P].rearrange("(k p e) -> p k e", p=GROUPS, e=P)
            sp.dma_start(key_rows, keyR[:, :, :]).then_inc(rows_out, 16)
            sp.wait_ge(made, 6)
            sp.dma_start(S.key_dram[0:1].rearrange("(a b) -> a b", a=1), edge[0:1, 0:1]).then_inc(ends_out, 16)
            sp.dma_start(S.key_dram[1 + STEPS * P:2 + STEPS * P].rearrange("(a b) -> a b", a=1),
                         edge[0:1, 1:2]).then_inc(ends_out, 16)
            sp.wait_ge(rows_out, 32)
            sp.wait_ge(ends_out, 32)
            for o in range(3):
                sp.dma_start(keyS[:, o, :], S.key_dram[o:o + STEPS * P].rearrange("(p e) -> p e", p=GROUPS)
                             ).then_inc(keys_in, 16)
            sp.wait_ge(zs, 16)

        @block.scalar
        def _(act):
            act.wait_ge(made, 6)
            act.dma_start(S.y_dram[SLOTS:SLOT_ROWS, :], zero[:, :]).then_inc(zs, 16)

        @block.gpsimd
        def _(pool):
            g = nc.gpsimd
            g.memset(S.ident[:, :], 0.0).then_inc(made, 1)
            pool.wait_ge(made, 1)
            g.affine_select(out=S.ident[:, :], in_=S.ident[:, :], compare_op=ALU.not_equal, fill=1.0, base=0,
                            pattern=[[-1, P]], channel_multiplier=1).then_inc(made, 1)
            g.iota(S.iota_row[:, :], [[1, P]], base=0, channel_multiplier=0, allow_small_or_imprecise_dtypes=True)
            g.iota(S.iota_col[:, :], [[0, 1]], base=0, channel_multiplier=1, allow_small_or_imprecise_dtypes=True)
            g.iota(step_row[:, :], [[1, STEPS]], base=0, channel_multiplier=0, allow_small_or_imprecise_dtypes=True)
            g.iota(step_col[:, :], [[GROUPS, GROUP]], base=0, channel_multiplier=1,
                   allow_small_or_imprecise_dtypes=True)
            g.iota(tile_no[:, :, :], [[1, 2], [EDGE_ROWS, EDGE_CHUNKS]], base=0, channel_multiplier=1,
                   allow_small_or_imprecise_dtypes=True).then_inc(made, 1)
            g.memset(edge[:, :], -2.0).then_inc(made, 1)
            g.memset(zero[:, :], 0.0).then_inc(made, 1)
            g.memset(S.ones[:, :], 1.0).then_inc(made, 1)

        @block.tensor
        def _(pe):
            t = nc.tensor
            pe.wait_ge(own_s, S.picked)
            for c in range(EDGE_CHUNKS):
                st, sp = c == 0, c == EDGE_CHUNKS - 1
                t.matmul(S.ps[:, 0, 0:STEPS], srcF[:, c, :], pick[:, c, :], start=st, stop=sp)
                t.matmul(S.ps[:, 1, 0:STEPS], dstF[:, c, :], pick[:, c, :], start=st, stop=sp)
                t.matmul(S.ps[:, 2, 0:STEPS], S.ones[0:EDGE_ROWS, :], reached[:, c, :], start=st, stop=sp)
            for k in range(GROUP):
                for c in range(EDGE_CHUNKS):
                    st, sp = c == 0, c == EDGE_CHUNKS - 1
                    t.matmul(S.ps[0:GROUPS, 3 + k // 4, (k % 4) * P:(k % 4 + 1) * P],
                             pick[:, c, k * GROUPS:(k + 1) * GROUPS], dstF[:, c, :], start=st, stop=sp)
                for c in range(EDGE_CHUNKS):
                    st, sp = c == 0, c == EDGE_CHUNKS - 1
                    last = t.matmul(S.ps[0:GROUPS, 5, k:k + 1], reached[:, c, k * GROUPS:(k + 1) * GROUPS],
                                    S.ones[0:EDGE_ROWS, 0:1], start=st, stop=sp)
            last.then_inc(got, 1)


RING = 5


def tiles(eng):
    with eng.Fori(0, T5) as i:
        for j in range(RING):
            yield i, i * RING + j, j, i * RING + (j + 1)


def after(eng, sem, n):
    eng.wait_ge(sem, n + RING)


def again(eng, sem, n):
    eng.wait_ge(sem, n)


def bank_again(eng, sem, j, n):
    eng.wait_ge(sem, n + RING - (1 if j == 0 else 2))


def norm_five(nc, ph, dve, src, mv, rstd, ring, i):
    for j in range(RING):
        t, n = i * RING + j, i * RING + (j + 1)
        again(dve, ph["xT_psum"], n)
        again(dve, ph["xn_kept"], n)
        nc.vector.tensor_scalar(ring[:, j, :], src[:, bass.ds(t, 1), :].squeeze(1), mv[:, bass.ds(t, 1), 0],
                                rstd[:, bass.ds(t, 1)], ALU.subtract, ALU.mult).then_inc(ph["xn_ready"], 1)


def keep_tiles(nc, ph, pool, ring, dst):
    pool.sem_inc(ph["xn_kept"], RING)
    for i, t, j, n in tiles(pool):
        after(pool, ph["xn_ready"], n)
        nc.gpsimd.tensor_copy(dst[:, bass.ds(t, 1), :], ring[:, j:j + 1, :]).then_inc(ph["xn_kept"], 1)


def copy_transposed(nc, ph, act, j, n, bank, xT, name="xT"):
    after(act, ph[name + "_psum"], n)
    nc.scalar.activation(xT[:, j, :, :], ph.ps[:, bank, 0:D].rearrange("p (c n) -> p c n", c=2),
                         ACT.Copy).then_inc(ph[name + "_ready"], 1)


def transpose_tile(nc, ph, pe, src, j, bank, ident, name="xT"):
    for c in range(2):
        last = nc.tensor.transpose(ph.ps[:, bank, c * P:(c + 1) * P], src[:, j, c * P:(c + 1) * P], ident[:, :])
    last.then_inc(ph[name + "_psum"], 1)


def project_layer0(nc, S, A):
    with Phase(nc, "project_layer0") as ph:
        ph.ps = S.ps
        W = ph.sb("w_proj", [P, 2, 4 * D])
        bv = ph.sb("bv_rows", [P, D])
        wqk = ph.sb("wqk_rows", [P, 2, D])
        bqk = ph.sb("bqk_rows", [P, 2])
        stats = ph.sb("ln_stats", [P, NODE_TILES, 6])
        mv = ph.sb("ln_mean_var", [P, NODE_TILES, 2])
        rstd = ph.sb("ln_rstd", [P, NODE_TILES])
        xn = ph.sb("xn_ring", [P, RING, D])
        xT = ph.sb("xn_T", [P, RING, 2, P])
        hrow = ph.sb("h_rows", [P, RING, D + 1])
        prod = ph.sb("h_times_w", [P, RING, 2, D])
        qk5 = ph.sb("q_k_of_five", [P, 2, RING])
        neg = ph.sb("neg_part", [P, RING, 2, D])
        kf = ph.sb("k_feature", [P, RING, D])
        vf = ph.sb("v_feature", [P, RING, 2, P + 1])
        mask4 = ph.sb("head_mask", [P, 4])
        kvs = ph.sb("kv_raw", [P, 2, P + 1])
        hq_bank = lambda j: j % 2
        kv_bank = lambda j: 2 + j % 2
        block = ph.block()

        @block.sync
        def _(sp):
            sp.dma_start(W[:, :, 0:D], A["Wv"].rearrange("(c p) n -> p c n", p=P)).then_inc(ph["weights_in"], 16)
            sp.dma_start(W[:, :, D:4 * D], A["WqkvT"].rearrange("(c p) n -> p c n", p=P)
                         ).then_inc(ph["weights_in"], 16)
            for dst, src in ((bv[:, :], "bv"), (wqk[:, 0, :], "wq"), (wqk[:, 1, :], "wk"), (bqk[:, 0:1], "bq"),
                             (bqk[:, 1:2], "bk")):
                sp.dma_start(dst, bcast(A[src])).then_inc(ph["rows_in"], 16)
            with sp.Fori(0, T5) as i:
                sp.wait_ge(ph["h_done"], i + 1)
                sp.dma_start(S.htab_dram[bass.ds(i * (RING * P), RING * P), :].rearrange("(t p) d -> p t d", p=P),
                             hrow[:, :, :]).then_inc(ph["h_table_out"], 16)
            sp.wait_ge(ph["h_table_out"], 16 * T5 + 16)

        @block.gpsimd
        def _(pool):
            g, made = nc.gpsimd, ph["pool_made"]
            g.memset(vf[:, :, :, P:P + 1], 1.0).then_inc(made, 1)
            g.memset(mask4[:, :], 1.0).then_inc(made, 1)
            pool.wait_ge(made, 2)
            g.affine_select(out=mask4[:, :], in_=mask4[:, :], compare_op=ALU.is_ge, fill=0.0, base=0,
                            pattern=[[-HD, 4]], channel_multiplier=1).then_inc(made, 1)
            pool.wait_ge(made, 3)
            g.affine_select(out=mask4[:, :], in_=mask4[:, :], compare_op=ALU.is_ge, fill=0.0, base=HD - 1,
                            pattern=[[HD, 4]], channel_multiplier=-1).then_inc(made, 1)
            pool.wait_ge(made, 4)
            g.tensor_copy(S.head_blocks[:, :].rearrange("p (h m) -> p h m", m=HD),
                          mask4[:, :].unsqueeze(2).broadcast_to([P, 4, HD])).then_inc(made, 1)
            keep_tiles(nc, ph, pool, xn, S.XN)

        @block.vector
        def _(dve):
            v, own = nc.vector, Own(dve, ph["dve_own"])
            layernorm_stats(nc, dve, own, S.X, stats, mv, rstd, ph["eps_done"], ph["sqrt_done"])
            dve.wait_ge(ph["rows_in"], 80)

            dve.sem_inc(ph["h_table_out"], 16)
            for name in ("xn_ready", "h_biased", "q_feature", "k_feature", "qk_dots"):
                dve.sem_inc(ph[name], RING)
            for i, t, j, n in tiles(dve):
                if j == 0:
                    norm_five(nc, ph, dve, S.X, mv, rstd, xn, i)
                    dve.wait_ge(ph["h_table_out"], i * 16 + 16)
                after(dve, ph["q_exp"], n)
                v.tensor_tensor(hrow[:, j, 0:D], S.ps[:, hq_bank(j), 0:D], bv[:, :], ALU.add
                                ).then_inc(ph["h_biased"], 1)
                v.scalar_tensor_tensor(S.QF[:, bass.ds(t, 1), :], S.ps[:, hq_bank(j):hq_bank(j) + 1, D:2 * D], 0.0,
                                       neg[:, j:j + 1, 0, :], ALU.max, ALU.add).then_inc(ph["q_feature"], 1)
                after(dve, ph["k_exp"], n)
                again(dve, ph["kv_used"], n)
                v.scalar_tensor_tensor(kf[:, j, :], S.ps[:, kv_bank(j), 0:D], 0.0, neg[:, j, 1, :], ALU.max,
                                       ALU.add).then_inc(ph["k_feature"], 1)
                after(dve, ph["h_biased"], n)
                for m in range(2):
                    ins = v.tensor_tensor_reduce(out=prod[:, j, m, :], in0=hrow[:, j, 0:D], in1=wqk[:, m, :],
                                                 scale=1.0, scalar=0.0, op0=ALU.mult, op1=ALU.add,
                                                 accum_out=qk5[:, m, j:j + 1])
                ins.then_inc(ph["qk_dots"], 1)
                if j == RING - 1:
                    after(dve, ph["qk_dots"], n)
                    v.tensor_copy(S.qk[:, :, bass.ds(i * RING, RING)], qk5[:, :, :])
                    v.tensor_scalar(hrow[:, :, D], qk5[:, 0, :], bqk[:, 0:1], None, ALU.add
                                    ).then_inc(ph["h_done"], 1)
            dve.wait_ge(ph["h_done"], T5)
            own(v.tensor_scalar(S.qk[:, 1, :], S.qk[:, 1, :], bqk[:, 1:2], None, ALU.add))
            after(dve, ph["kv_used"], NODE_TILES)
            dve.wait_ge(ph["pool_made"], 5)
            own(v.tensor_copy(kvs[:, :, :], S.ps[:, 6:8, 0:P + 1]))
            own.wait()
            for c in range(2):
                own(v.tensor_tensor(S.kvbd[:, c, 0:P], kvs[:, c, 0:P], S.head_blocks[:, :], ALU.mult))
                own(v.tensor_scalar(S.kvbd[:, c, P:P + 4], mask4[:, :], kvs[:, c, P:P + 1], None, ALU.mult))
            own.wait()

        @block.scalar
        def _(act):
            a = nc.scalar
            act.wait_ge(ph["eps_done"], 1)
            a.activation(rstd[:, :], rstd[:, :], ACT.Sqrt).then_inc(ph["sqrt_done"], 1)
            for name in ("xT_ready", "q_neg", "q_exp", "k_neg", "k_exp", "v_feature"):
                act.sem_inc(ph[name], RING)
            act.wait_ge(ph["pool_made"], 1)
            for i, t, j, n in tiles(act):
                again(act, ph["kv_psum"], n)
                copy_transposed(nc, ph, act, j, n, 4 + j % 2, xT)
                for m, (psum, neg_s, exp_s, used, bank, off) in enumerate((
                        ("hq_psum", "q_neg", "q_exp", "q_feature", hq_bank(j), D),
                        ("kv_psum", "k_neg", "k_exp", "k_feature", kv_bank(j), 0))):
                    after(act, ph[psum], n)
                    again(act, ph[used], n)
                    a.activation(neg[:, j, m, :], S.ps[:, bank, off:off + D], ACT.Relu, scale=-1.0
                                 ).then_inc(ph[neg_s], 1)
                    if m == 1:
                        again(act, ph["kv_used"], n)
                        a.activation(vf[:, j, :, 0:P], S.ps[:, bank, D:2 * D].rearrange("p (c n) -> p c n", c=2),
                                     ACT.Copy).then_inc(ph["v_feature"], 1)
                        after(act, ph["v_feature"], n)
                    after(act, ph[neg_s], n)
                    a.activation(neg[:, j, m, :], neg[:, j, m, :], ACT.Exp, scale=-1.0).then_inc(ph[exp_s], 1)

        @block.tensor
        def _(pe):
            t_ = nc.tensor
            pe.wait_ge(ph["weights_in"], 32)
            for name in ("xT_psum", "hq_psum", "kv_psum", "kv_used"):
                pe.sem_inc(ph[name], RING)

            def products(j, n):
                after(pe, ph["xn_ready"], n)
                bank_again(pe, ph["xT_ready"], j, n)
                transpose_tile(nc, ph, pe, xn, j, 4 + j % 2, S.ident)
                after(pe, ph["xT_ready"], n)
                for half, (psum, bank) in enumerate((("hq_psum", hq_bank(j)), ("kv_psum", kv_bank(j)))):
                    for used in (("h_biased", "q_feature") if half == 0 else ("k_feature", "v_feature")):
                        bank_again(pe, ph[used], j, n)
                    for c in range(2):
                        ins = t_.matmul(S.ps[:, bank, :], xT[:, j, c, :], W[:, c, half * 512:(half + 1) * 512],
                                        start=c == 0, stop=c == 1)
                    ins.then_inc(ph[psum], 1)

            def group(i, first, last):
                for j in range(RING):
                    products(j, i * RING + (j + 1))
                for j in range(RING):
                    after(pe, ph["k_feature"], i * RING + (j + 1))
                    after(pe, ph["v_feature"], i * RING + (j + 1))
                    rows = LAST_ROWS if last and j == RING - 1 else P
                    for c in range(2):
                        ins = t_.matmul(S.ps[:, 6 + c, 0:P + 1], kf[0:rows, j, c * P:(c + 1) * P],
                                        vf[0:rows, j, c, :], start=first and j == 0, stop=last and j == RING - 1)
                    ins.then_inc(ph["kv_used"], 1)

            group(0, True, False)
            with pe.Fori(1, T5 - 1) as i:
                group(i, False, False)
            group(T5 - 1, False, True)


LANES = 4
AHEAD = 2
AGG_LANES = 3
ON_ACT = 3
MIX_LANES = 5


def group_at(i, h, lanes):
    i, h = i + h // lanes, h % lanes
    return i, h, i * lanes + h, i * lanes + (h + 1)


def groups(eng, lanes=LANES):
    for i, h, k, n, later in groups_ahead(eng, 0, lanes):
        yield i, h, k, n


def groups_ahead(eng, ahead, lanes=LANES):
    loops = GROUPS // lanes - (ahead > GROUPS % lanes)
    with eng.Fori(0, loops) as i:
        for h in range(lanes):
            yield *group_at(i, h, lanes), group_at(i, h + ahead, lanes)
    for h in range(GROUPS - loops * lanes):
        yield (*group_at(loops, h, lanes),
               group_at(loops, h + ahead, lanes) if loops * lanes + h + ahead < GROUPS else None)


def dst_blocks(eng, S, k):
    S.loads += 1
    regs = [eng.alloc_register(f"dst_block{j}_{S.loads}") for j in range(GROUP)]
    eng.load(regs, S.blockI[0:1, bass.ds(k, 1), 0:GROUP].squeeze(1))
    return [bass.RuntimeValue.of_register_unchecked(r).with_bounds(min_val=0, max_val=NODE_TILES - 1) for r in regs]


def gather_edges(nc, S, ph, block, table, idx, got, relB, lanes, items, before=None):
    ph.for_gathers(*[f"gathered{h}" for h in range(lanes)])

    @block.gpsimd
    def _(pool):
        def indices(i, h, k, n):
            pool.wait_ge(ph["rows_used"], n)
            nc.gpsimd.tensor_copy(idx[:, h, :], S.srcX[:, bass.ds(k * GROUP, GROUP)]).then_inc(ph["idx_ready"], 1)

        indices(0, 0, 0, 1)
        for i, h, k, n, later in groups_ahead(pool, 1, lanes):
            if later:
                indices(*later)
            pool.wait_ge(ph[f"kept{h}"], i * 16 + 16)
            pool.wait_ge(ph["idx_ready"], n)
            pool.sem_inc(ph["gather_gate"], 1)
            for j in range(GROUP):
                nc.gpsimd.indirect_dma_start(got[:, h, j, :], None, table,
                                             bass.IndirectOffsetOnAxis(ap=idx[:, h, j:j + 1], axis=0)
                                             ).then_inc(ph[f"gathered{h}"], 16)

    @block.sync
    def _(sp):
        if before:
            before(sp)
        for i, h, k, n in groups(sp, lanes):
            sp.wait_ge(ph["hot_ready"], n)
            sp.dma_start(relB[:, h, :], S.rel_dram[bass.ds(k * GROUP, GROUP), :].rearrange("g e -> (g e)")
                         .partition_broadcast(P)).then_inc(ph[f"rel_in{h}"], 16)

    @block.scalar
    def _(act):
        for h in range(lanes):
            act.sem_inc(ph[f"kept{h}"], 16)
        for i, h, k, n in items(act):
            act.wait_ge(ph[f"gathered{h}"], i * (16 * GROUP) + 16 * GROUP)
            act.dma_start(S.step_dram[bass.ds(k, 1), :, :].rearrange("a p (g d) -> (a p) g d", d=D),
                          got[:, h, :, 0:D]).then_inc(ph[f"kept{h}"], 16)
        for h in range(lanes):
            act.wait_ge(ph[f"kept{h}"], 16 * ((GROUPS - 1 - h) // lanes + 1) + 16)


def onehot_T(nc, S, ph, dve, hot, relB, i, h, n):
    dve.wait_ge(ph[f"rel_in{h}"], i * 16 + 16)
    dve.wait_ge(ph["dst_psum"], n)
    nc.vector.tensor_scalar(hot[:, h, :], relB[:, h, :], S.iota_col[:, 0:1], None, ALU.is_equal
                            ).then_inc(ph["hot_ready"], 1)


def score_and_mix_layer0(nc, S, A):
    lanes = MIX_LANES
    with Phase(nc, "score_mix") as ph:
        ph.ps = S.ps
        idx = ph.sb("gather_idx", [P, lanes, GROUP], I32)
        got = ph.sb("h_of_sources", [P, lanes, GROUP, D + 1])
        relB = ph.sb("rel_bcast", [P, lanes, GROUP * P])
        hot = ph.sb("dst_onehot_T", [P, lanes, GROUP * P])
        qr = ph.sb("q_ring", [P, RING, D])
        qT = ph.sb("q_T", [P, RING, 2, P])
        z = ph.sb("inv_den", [P, RING, 2, 4])
        tt = ph.sb("attended", [P, RING, 2, P])
        W1 = ph.sb("w1", [P, 2, D])
        W2 = ph.sb("w2", [P, 2, D])
        b1 = ph.sb("b1", [P, 2])
        rows = ph.sb("ln1_g_b_b2", [P, 3, D])
        stats, mv, rstd = ln_scratch(ph)
        x1, xT, hT = qr, qT, tt
        xs = ph.sb("x1_scaled", [P, RING, D])
        edge_k = lambda h: S.ps[:, 2 + h % 2, 0:GROUP]
        block = ph.block()

        def paced(eng, attend, between, mlp):
            with eng.Fori(0, T5) as i:
                for j in range(RING):
                    attend(i, i * RING + j, j, i * RING + (j + 1))
                    yield group_at(i, j, lanes)
            between()
            with eng.Fori(0, T5) as i:
                for j in range(RING):
                    mlp(i, i * RING + j, j, i * RING + (j + 1))
                    yield group_at(i * 2 + T5, 2 * j, lanes)
                    yield group_at(i * 2 + T5, 2 * j + 1, lanes)
            for h in range(GROUPS - 3 * NODE_TILES):
                yield group_at(3 * T5, h, lanes)

        def act_items(act):
            def attend(i, t, j, n):
                again(act, ph["qT_psum"], n)
                nc.scalar.activation(qr[:, j:j + 1, :], S.QF[:, bass.ds(t, 1), :], ACT.Copy
                                     ).then_inc(ph["q_staged"], 1)
                again(act, ph["num_psum"], n)
                copy_transposed(nc, ph, act, j, n, 4 + j % 2, qT, "qT")

            def between():
                ln_root(nc, ph, act, rstd)
                act.sem_inc(ph["xT_ready"], RING)
                act.sem_inc(ph["hidden"], RING)
                act.wait_ge(ph["weights_in"], 96)

            def mlp(i, t, j, n):
                again(act, ph["h_psum"], n)
                copy_transposed(nc, ph, act, j, n, 4 + j % 2, xT)
                after(act, ph["h_psum"], n)
                again(act, ph["y_psum"], n)
                for m in range(2):
                    ins = nc.scalar.activation(hT[:, j, m, :], S.ps[:, j % 2, m * P:(m + 1) * P], ACT.Gelu,
                                               bias=b1[:, m:m + 1])
                ins.then_inc(ph["hidden"], 1)

            act.sem_inc(ph["qT_ready"], RING)
            act.sem_inc(ph["q_staged"], RING)
            yield from paced(act, attend, between, mlp)

        def weights(sp):
            for dst, src in ((W1, "mW1T"), (W2, "mW2T")):
                sp.dma_start(dst[:, :, :], A[src].rearrange("(c p) n -> p c n", p=P)).then_inc(ph["weights_in"], 16)
            sp.dma_start(b1[:, :], A["mb1"]).then_inc(ph["weights_in"], 16)
            for m, src in enumerate(("ln1_g", "ln1_b", "mb2")):
                sp.dma_start(rows[:, m, :], bcast(A[src])).then_inc(ph["weights_in"], 16)

        gather_edges(nc, S, ph, block, S.htab_dram, idx, got, relB, lanes, act_items, weights)

        @block.vector
        def _(dve):
            v, own = nc.vector, Own(dve, ph["dve_own"])

            def attend(i, t, j, n):
                both = S.ps[:, j % 2, 0:2 * (P + 4)].rearrange("p (c n) -> p c n", c=2)
                after(dve, ph["num_psum"], n)
                v.tensor_scalar_add(z[:, j, :, :], both[:, :, P:P + 4], 1e-6).then_inc(ph["den_eps"], 1)
                after(dve, ph["den_eps"], n)
                v.reciprocal(z[:, j, :, :], z[:, j, :, :]).then_inc(ph["den_inv"], 1)
                after(dve, ph["den_inv"], n)
                for c in range(2):
                    ins = v.tensor_tensor(tt[:, j, c, :].rearrange("p (h m) -> p h m", h=4),
                                          both[:, c, 0:P].rearrange("p (h m) -> p h m", h=4),
                                          z[:, j, c, :].unsqueeze(2).broadcast_to([P, 4, HD]), ALU.mult)
                ins.then_inc(ph["attended"], 1)
                after(dve, ph["attended"], n)
                v.tensor_tensor(S.QF[:, bass.ds(t, 1), :], tt[:, j:j + 1, :, :].rearrange("p a c n -> p a (c n)"),
                                S.XN[:, bass.ds(t, 1), :], ALU.add).then_inc(ph["residual"], 1)

            def between():
                dve.wait_ge(ph["residual"], NODE_TILES)
                layernorm_stats(nc, dve, own, S.QF, stats, mv, rstd, ph["eps_done"], ph["sqrt_done"])
                dve.wait_ge(ph["weights_in"], 96)
                for name in ("xn_ready", "x1_scaled", "y_biased", "y_done"):
                    dve.sem_inc(ph[name], RING)

            def mlp(i, t, j, n):
                if j == 0:
                    for jj in range(RING):
                        tt, nn = i * RING + jj, i * RING + (jj + 1)
                        again(dve, ph["xT_psum"], nn)
                        v.scalar_tensor_tensor(xs[:, jj, :], S.QF[:, bass.ds(tt, 1), :].squeeze(1),
                                               mv[:, bass.ds(tt, 1), 0], rows[:, 0, :], ALU.subtract, ALU.mult
                                               ).then_inc(ph["x1_scaled"], 1)
                    for jj in range(RING):
                        tt, nn = i * RING + jj, i * RING + (jj + 1)
                        after(dve, ph["x1_scaled"], nn)
                        v.scalar_tensor_tensor(x1[:, jj, :], xs[:, jj, :], rstd[:, bass.ds(tt, 1)], rows[:, 1, :],
                                               ALU.mult, ALU.add).then_inc(ph["xn_ready"], 1)
                after(dve, ph["y_psum"], n)
                v.tensor_tensor(S.QF[:, bass.ds(t, 1), :].squeeze(1), S.ps[:, 6 + j % 2, 0:D], x1[:, j, :], ALU.add
                                ).then_inc(ph["y_done"], 1)
                after(dve, ph["y_done"], n)
                v.tensor_tensor(S.QF[:, bass.ds(t, 1), :].squeeze(1), S.QF[:, bass.ds(t, 1), :].squeeze(1),
                                rows[:, 2, :], ALU.add).then_inc(ph["y_biased"], 1)

            for name in ("hot_ready", "rows_used"):
                dve.sem_inc(ph[name], lanes)
            for name in ("attended", "den_eps", "den_inv"):
                dve.sem_inc(ph[name], RING)
            for h in range(AHEAD):
                onehot_T(nc, S, ph, dve, hot, relB, 0, h, h + 1)
            for i, h, k, n in paced(dve, attend, between, mlp):
                if not (isinstance(k, int) and k + AHEAD >= GROUPS):
                    i2, h2, _, n2 = group_at(i, h + AHEAD, lanes)
                    onehot_T(nc, S, ph, dve, hot, relB, i2, h2, n2)
                dve.wait_ge(ph[f"gathered{h}"], i * (16 * GROUP) + 16 * GROUP)
                dve.wait_ge(ph["dst_psum"], n + lanes)
                v.tensor_tensor(S.scoreX[:, bass.ds(k * GROUP, GROUP)], edge_k(h), got[:, h, :, D], ALU.add
                                ).then_inc(ph["rows_used"], 1)

        @block.tensor
        def _(pe):
            def attend(i, t, j, n):
                after(pe, ph["q_staged"], n)
                bank_again(pe, ph["qT_ready"], j, n)
                transpose_tile(nc, ph, pe, qr, j, 4 + j % 2, S.ident, "qT")
                after(pe, ph["qT_ready"], n)
                bank_again(pe, ph["attended"], j, n)
                for c in range(2):
                    ins = nc.tensor.matmul(S.ps[:, j % 2, c * (P + 4):(c + 1) * (P + 4)], qT[:, j, c, :],
                                           S.kvbd[:, c, :], start=True, stop=True)
                ins.then_inc(ph["num_psum"], 1)

            def between():
                pe.wait_ge(ph["weights_in"], 96)
                pe.wait_ge(ph["attended"], NODE_TILES + RING)
                for name in ("xT_psum", "h_psum", "y_psum"):
                    pe.sem_inc(ph[name], RING)

            def mlp(i, t, j, n):
                after(pe, ph["xn_ready"], n)
                bank_again(pe, ph["xT_ready"], j, n)
                transpose_tile(nc, ph, pe, x1, j, 4 + j % 2, S.ident)
                after(pe, ph["xT_ready"], n)
                bank_again(pe, ph["hidden"], j, n)
                for m in range(2):
                    for c in range(2):
                        ins = nc.tensor.matmul(S.ps[:, j % 2, m * P:(m + 1) * P], W1[:, c, m * P:(m + 1) * P],
                                               xT[:, j, c, :], start=c == 0, stop=c == 1)
                ins.then_inc(ph["h_psum"], 1)
                after(pe, ph["hidden"], n)
                bank_again(pe, ph["y_done"], j, n)
                for c in range(2):
                    ins = nc.tensor.matmul(S.ps[:, 6 + j % 2, 0:D], hT[:, j, c, :], W2[:, c, :],
                                           start=c == 0, stop=c == 1)
                ins.then_inc(ph["y_psum"], 1)

            pe.sem_inc(ph["dst_psum"], lanes)
            pe.sem_inc(ph["qT_psum"], RING)
            pe.sem_inc(ph["num_psum"], RING)
            for i, h, k, n in paced(pe, attend, between, mlp):
                blocks = dst_blocks(pe, S, k)
                pe.wait_ge(ph["hot_ready"], n + lanes)
                pe.wait_ge(ph["rows_used"], n + lanes - (1 if h == 0 else 2))
                for j, b in enumerate(blocks):
                    last = nc.tensor.matmul(edge_k(h)[:, j:j + 1], hot[:, h, j * P:(j + 1) * P],
                                            S.qk[:, 1, bass.ds(b, 1)], start=True, stop=True)
                last.then_inc(ph["dst_psum"], 1)


def softmax_weights(nc, S, A, leaky):
    N = GROUP * P
    with Phase(nc, f"softmax_weights_{S.layer}") as ph:
        score = ph.sb("score_scan", [GROUPS, N])
        fwd = ph.sb("max_forward", [GROUPS, N])
        bwd = ph.sb("max_backward", [GROUPS, N])
        ends = ph.sb("row_ends", [GROUPS, 2])
        rows = ph.sb("row_ends_T", [1, 4, GROUPS])
        carry = ph.sb("carry_rows", [1, 2, GROUPS + 1])
        carryT = ph.sb("carry_cols", [GROUPS, 2])
        ps2 = S.ps[:, :, :].rearrange("p b n -> p (b n)")
        block = ph.block()

        @block.vector
        def _(dve):
            v, own = nc.vector, Own(dve, ph["dve_own"])
            if leaky:
                own(v.tensor_scalar(S.weightX[:, :], S.scoreX[:, :], 0.2, None, ALU.mult))
                own.wait()
                own(v.tensor_tensor(S.scoreX[:, :], S.scoreX[:, :], S.weightX[:, :], ALU.max))
                own.wait()
            own(v.tensor_tensor(S.scoreX[:, :], S.scoreX[:, :], S.validX[:, :], ALU.mult))
            own.wait()
            v.tensor_tensor(S.scoreX[:, :], S.scoreX[:, :], S.penX[:, :], ALU.add).then_inc(ph["score_ready"], 1)
            own(v.memset(carry[:, :, :], -BIG))
            dve.wait_ge(ph["score_psum"], 1)
            own(v.tensor_copy(score[:, :], ps2[0:GROUPS, 0:N]))
            own.wait()
            own(v.tensor_tensor_scan(fwd[:, :], S.cut[:, 0, :], score[:, :], -BIG, ALU.add, ALU.max))
            own(v.tensor_tensor_scan(bwd[:, ::-1], S.cut[:, 1, ::-1], score[:, ::-1], -BIG, ALU.add, ALU.max))
            own.wait()
            own(v.tensor_copy(ends[:, 0:1], fwd[:, N - 1:N]))
            v.tensor_copy(ends[:, 1:2], bwd[:, 0:1]).then_inc(ph["ends_ready"], 1)
            dve.wait_ge(ph["ends_psum"], 1)
            own(v.tensor_copy(rows[:, :, :], ps2[0:1, 1024:1024 + 4 * GROUPS].rearrange("p (a n) -> p a n", a=4)))
            own.wait()
            own(v.tensor_tensor_scan(carry[:, 0, 1:GROUPS + 1], rows[:, 2, :], rows[:, 0, :], -BIG, ALU.add, ALU.max))
            own(v.tensor_tensor_scan(carry[:, 1, 0:GROUPS][:, ::-1], rows[:, 3, ::-1], rows[:, 1, ::-1], -BIG, ALU.add,
                                     ALU.max))
            own.wait()
            S.carry_ready = own.total
            dve.wait_ge(ph["carry_psum"], 1)
            own(v.tensor_copy(carryT[:, :], ps2[0:GROUPS, 1536:1538]))
            own.wait()
            own(v.tensor_tensor_scan(fwd[:, :], S.cut[:, 0, :], score[:, :], carryT[:, 0:1], ALU.add, ALU.max))
            own(v.tensor_tensor_scan(bwd[:, ::-1], S.cut[:, 1, ::-1], score[:, ::-1], carryT[:, 1:2], ALU.add,
                                     ALU.max))
            own.wait()
            own(v.tensor_tensor(fwd[:, :], fwd[:, :], bwd[:, :], ALU.max))
            own.wait()
            v.tensor_tensor(score[:, :], score[:, :], fwd[:, :], ALU.subtract).then_inc(ph["shifted"], 1)
            dve.wait_ge(ph["weight_psum"], 1)
            own(v.tensor_tensor(S.weightX[:, :].rearrange("p (q g) -> p q g", g=GROUP),
                                ps2[:, 2048:2048 + STEPS].rearrange("p (g q) -> p q g", g=GROUP),
                                S.validX[:, :].rearrange("p (q g) -> p q g", g=GROUP), ALU.mult))
            own.wait()

        @block.scalar
        def _(act):
            act.wait_ge(ph["shifted"], 1)
            nc.scalar.activation(score[:, :], score[:, :], ACT.Exp).then_inc(ph["exps"], 1)

        @block.tensor
        def _(pe):
            t = nc.tensor
            pe.wait_ge(ph["score_ready"], 1)
            for g in range(GROUP):
                ins = t.transpose(ps2[0:GROUPS, g * P:(g + 1) * P], S.scoreX[:, g::GROUP], S.ident[:, :])
            ins.then_inc(ph["score_psum"], 1)
            pe.wait_ge(ph["ends_ready"], 1)
            idg = S.ident[0:GROUPS, 0:GROUPS]
            for m, col in enumerate((ends[:, 0:1], ends[:, 1:2], S.row_cut[:, 0:1], S.row_cut[:, 1:2])):
                ins = t.transpose(ps2[0:1, 1024 + m * GROUPS:1024 + (m + 1) * GROUPS], col, idg)
            ins.then_inc(ph["ends_psum"], 1)
            pe.wait_ge(ph["dve_own"], S.carry_ready)
            t.transpose(ps2[0:GROUPS, 1536:1537], carry[0:1, 0, 0:GROUPS], S.ident[0:1, 0:1])
            t.transpose(ps2[0:GROUPS, 1537:1538], carry[0:1, 1, 1:GROUPS + 1], S.ident[0:1, 0:1]
                        ).then_inc(ph["carry_psum"], 1)
            pe.wait_ge(ph["exps"], 1)
            for g in range(GROUP):
                ins = t.transpose(ps2[:, 2048 + g * GROUPS:2048 + (g + 1) * GROUPS], score[:, g * P:(g + 1) * P], idg)
            ins.then_inc(ph["weight_psum"], 1)


def aggregate(nc, S, A):
    with Phase(nc, f"aggregate_{S.layer}") as ph:
        rowsB = ph.sb("step_rows", [P, AGG_LANES, GROUP, D + 1])
        hotw = ph.sb("weighted_onehot", [P, AGG_LANES, GROUP, P])
        relw = ph.sb("rel_and_weight", [P, AGG_LANES, 3, GROUP])
        negw = ph.sb("minus_weight", [P, STEPS])
        far = ph.sb("distance", [P, AGG_LANES, ON_ACT, P])
        odd = ph.sb("odd_edge_sums", [P, NODE_TILES, D + 1])
        block = ph.block()

        @block.gpsimd
        def _(pool):
            g = nc.gpsimd

            def columns(i, h, k, n):
                pool.wait_ge(ph["sums_psum"], n * GROUP)
                g.tensor_copy(relw[:, h, 0, :], S.relX[:, bass.ds(k * GROUP, GROUP)])
                g.tensor_copy(relw[:, h, 1, :], S.weightX[:, bass.ds(k * GROUP, GROUP)])
                g.tensor_copy(relw[:, h, 2, :], negw[:, bass.ds(k * GROUP, GROUP)]).then_inc(ph["columns"], 1)

            g.memset(rowsB[:, :, :, D:D + 1], 1.0).then_inc(ph["ones_made"], 1)
            pool.wait_ge(ph["negated"], 1)
            columns(0, 0, 0, 1)
            for i, h, k, n, later in groups_ahead(pool, 1, AGG_LANES):
                if later:
                    columns(*later)
                pool.wait_ge(ph["columns"], n)
                pool.sem_inc(ph["weigh_gate"], 1)
                for j in range(ON_ACT, GROUP):
                    ins = g.tensor_scalar(hotw[:, h, j, :], S.iota_row[:, :], relw[:, h, 0, j:j + 1],
                                          relw[:, h, 1, j:j + 1], ALU.is_equal, ALU.mult)
                ins.then_inc(ph["hotw_ready"], 1)

        @block.scalar
        def _(act):
            a = nc.scalar
            for i, h, k, n in groups(act, AGG_LANES):
                act.wait_ge(ph["columns"], n)
                for j in range(ON_ACT):
                    ins = a.activation(far[:, h, j, :], S.iota_row[:, :], ACT.Abs, scale=-1.0, bias=relw[:, h, 0, j:j + 1])
                ins.then_inc(ph["distances"], 1)
                act.wait_ge(ph["distances"], n)
                for j in range(ON_ACT):
                    ins = a.activation(hotw[:, h, j, :], far[:, h, j, :], ACT.Relu, scale=relw[:, h, 2, j:j + 1],
                                       bias=relw[:, h, 1, j:j + 1])
                ins.then_inc(ph["hotw_by_act"], 1)

        @block.sync
        def _(sp):
            for i, h, k, n in groups(sp, AGG_LANES):
                sp.wait_ge(ph["sums_psum"], n * GROUP)
                sp.dma_start(rowsB[:, h, :, 0:D], S.step_dram[bass.ds(k, 1), :, :].rearrange(
                    "a p (g d) -> (a p) g d", d=D)).then_inc(ph[f"rows_in{h}"], 16)

        @block.vector
        def _(dve):
            v = nc.vector
            v.tensor_scalar(negw[:, :], S.weightX[:, :], -1.0, None, ALU.mult).then_inc(ph["negated"], 1)
            v.memset(S.acc[:, :, :], 0.0).then_inc(ph["cleared"], 1)
            v.memset(odd[:, :, :], 0.0).then_inc(ph["cleared"], 1)
            dve.wait_ge(ph["cleared"], 2)
            dve.sem_inc(ph["added"], GROUP)
            for i, h, k, n in groups(dve, AGG_LANES):
                for j, b in enumerate(dst_blocks(dve, S, k)):
                    m = n * GROUP + (j + 1 - GROUP)
                    sums = S.acc if j % 2 == 0 else odd
                    dve.wait_ge(ph["sums_psum"], m + AGG_LANES * GROUP)
                    dve.wait_ge(ph["added"], m + GROUP - (1 if j == 0 else 2))
                    v.tensor_tensor(sums[:, bass.ds(b, 1), :], S.ps[:, j:j + 1, 0:D + 1],
                                    sums[:, bass.ds(b, 1), :], ALU.add).then_inc(ph["added"], 1)
            dve.wait_ge(ph["added"], STEPS + GROUP)
            v.tensor_tensor(S.acc[:, :, :], S.acc[:, :, :], odd[:, :, :], ALU.add)

        @block.tensor
        def _(pe):
            pe.sem_inc(ph["sums_psum"], AGG_LANES * GROUP)
            pe.wait_ge(ph["ones_made"], 1)
            for i, h, k, n in groups(pe, AGG_LANES):
                pe.wait_ge(ph["hotw_ready"], n)
                pe.wait_ge(ph["hotw_by_act"], n)
                pe.wait_ge(ph[f"rows_in{h}"], i * 16 + 16)
                for j in range(GROUP):
                    pe.wait_ge(ph["added"], n * GROUP + (j + 1 - GROUP))
                    nc.tensor.matmul(S.ps[:, j, 0:D + 1], hotw[:, h, j, :], rowsB[:, h, j, :],
                                     start=True, stop=True).then_inc(ph["sums_psum"], 1)


def ln_scratch(ph):
    return (ph.sb("ln_stats", [P, NODE_TILES, 6]), ph.sb("ln_mean_var", [P, NODE_TILES, 2]),
            ph.sb("ln_rstd", [P, NODE_TILES]))


def ln_root(nc, ph, act, rstd):
    act.wait_ge(ph["eps_done"], 1)
    nc.scalar.activation(rstd[:, :], rstd[:, :], ACT.Sqrt).then_inc(ph["sqrt_done"], 1)


def stage_tiles(nc, ph, pool, src, ring, name, used):
    pool.sem_inc(ph[name], RING)
    for i, t, j, n in tiles(pool):
        again(pool, ph[used], n)
        nc.gpsimd.tensor_copy(ring[:, j:j + 1, :], src[:, bass.ds(t, 1), :]).then_inc(ph[name], 1)


def add_edge_sums(nc, ph, S, dve):
    v, own = nc.vector, Own(dve, ph["dve_own_sums"])
    inv = S.inv_sum
    own(v.tensor_scalar_max(inv[:, :], S.acc[:, :, D], 1e-30))
    own.wait()
    own(v.reciprocal(inv[:, :], inv[:, :]))
    own.wait()
    for t in range(NODE_TILES):
        own(v.scalar_tensor_tensor(S.X[:, t, :], S.acc[:, t, 0:D], inv[:, t:t + 1], S.X[:, t, :],
                                   ALU.mult, ALU.add))
    own.wait()


def router(nc, S, A):
    with Phase(nc, "router") as ph:
        ph.ps = S.ps
        Wr = ph.sb("w_router", [P, 2, E0])
        br = ph.sb("b_router", [P, E0])
        rows = ph.sb("ln2_g_b", [P, 2, D])
        stats, mv, rstd = ln_scratch(ph)
        mv2 = ph.sb("ln_mean_var_x", [P, NODE_TILES, 2])
        rstd2 = ph.sb("ln_rstd_x", [P, NODE_TILES])
        xt = ph.sb("xt_ring", [P, RING, D])
        xT = ph.sb("xt_T", [P, RING, 2, P])
        block = ph.block()

        @block.sync
        def _(sp):
            sp.dma_start(Wr[:, :, :], A["Wr"].rearrange("(c p) n -> p c n", p=P)).then_inc(ph["weights_in"], 16)
            sp.dma_start(br[:, :], bcast(A["br"])).then_inc(ph["weights_in"], 16)
            for m, src in enumerate(("ln2_g", "ln2_b")):
                sp.dma_start(rows[:, m, :], bcast(A[src])).then_inc(ph["weights_in"], 16)
            sp.wait_ge(ph["weights_in"], 64)

        @block.vector
        def _(dve):
            v, own = nc.vector, Own(dve, ph["dve_own"])
            layernorm_stats(nc, dve, own, S.QF, stats, mv, rstd, ph["eps_done"], ph["sqrt_done"])
            dve.wait_ge(ph["weights_in"], 64)
            add_edge_sums(nc, ph, S, dve)
            for t in range(NODE_TILES):
                own(v.scalar_tensor_tensor(S.QF[:, t, :], S.QF[:, t, :], mv[:, t, 0:1], rows[:, 0, :],
                                           ALU.subtract, ALU.mult))
            own.wait()
            for t in range(NODE_TILES):
                own(v.scalar_tensor_tensor(S.QF[:, t, :], S.QF[:, t, :], rstd[:, t:t + 1], rows[:, 1, :],
                                           ALU.mult, ALU.add))
            own.wait()
            for t in range(NODE_TILES):
                own(v.tensor_tensor(S.X[:, t, :], S.X[:, t, :], S.QF[:, t, :], ALU.add))
            own.wait()
            layernorm_stats(nc, dve, own, S.X, stats, mv2, rstd2, ph["eps_done2"], ph["sqrt_done2"])
            for name in ("xn_ready", "logits"):
                dve.sem_inc(ph[name], RING)
            for i, t, j, n in tiles(dve):
                if j == 0:
                    norm_five(nc, ph, dve, S.X, mv2, rstd2, xt, i)
                after(dve, ph["l_psum"], n)
                v.tensor_tensor(S.logits[:, bass.ds(t, 1), :].squeeze(1), S.ps[:, j % 2, 0:E0], br[:, :], ALU.add
                                ).then_inc(ph["logits"], 1)
            after(dve, ph["logits"], NODE_TILES)

        @block.gpsimd
        def _(pool):
            pool.wait_ge(ph["qf_free"], 1)
            keep_tiles(nc, ph, pool, xt, S.QF)

        @block.scalar
        def _(act):
            ln_root(nc, ph, act, rstd)
            act.wait_ge(ph["eps_done2"], 1)
            act.sem_inc(ph["qf_free"], 1)
            nc.scalar.activation(rstd2[:, :], rstd2[:, :], ACT.Sqrt).then_inc(ph["sqrt_done2"], 1)
            act.sem_inc(ph["xT_ready"], RING)
            for i, t, j, n in tiles(act):
                again(act, ph["l_psum"], n)
                copy_transposed(nc, ph, act, j, n, 4 + j % 2, xT)

        @block.tensor
        def _(pe):
            pe.wait_ge(ph["weights_in"], 64)
            for name in ("xT_psum", "l_psum"):
                pe.sem_inc(ph[name], RING)
            for i, t, j, n in tiles(pe):
                after(pe, ph["xn_ready"], n)
                bank_again(pe, ph["xT_ready"], j, n)
                transpose_tile(nc, ph, pe, xt, j, 4 + j % 2, S.ident)
                after(pe, ph["xT_ready"], n)
                bank_again(pe, ph["logits"], j, n)
                for c in range(2):
                    ins = nc.tensor.matmul(S.ps[:, j % 2, 0:E0], xT[:, j, c, :], Wr[:, c, :],
                                           start=c == 0, stop=c == 1)
                ins.then_inc(ph["l_psum"], 1)


def top_two(nc, own, logits, top, idx, idxf, hot1, hot2, iota8, width):
    v = nc.vector
    for t in range(NODE_TILES):
        own(v.max(top[:, t, :], logits[:, t, :]))
    own.wait()
    for t in range(NODE_TILES):
        own(v.max_index(idx[:, t, :], top[:, t, :], logits[:, t, :]))
    own.wait()
    own(v.tensor_copy(idxf[:, :, :], idx[:, :, :]))
    own.wait()
    for m, hot in enumerate((hot1, hot2)):
        w = hot.shape[2]
        own(v.tensor_tensor(hot[:, :, :], iota8[:, 0:w].unsqueeze(1).broadcast_to([P, NODE_TILES, w]),
                            idxf[:, :, m:m + 1].broadcast_to([P, NODE_TILES, w]), ALU.is_equal))
    own.wait()


def dispatch_plan(nc, S, A):
    with Phase(nc, "dispatch_plan") as ph:
        top = ph.sb("top8", [P, NODE_TILES, 8])
        idx = ph.sb("top8_idx", [P, NODE_TILES, 8], U32)
        idxf = ph.sb("top8_idx_f", [P, NODE_TILES, 8])
        hot1 = ph.sb("hot1", [P, NODE_TILES, E0])
        hot2 = ph.sb("hot2", [P, NODE_TILES, E0])
        both = ph.sb("hot_both", [P, NODE_TILES, E0])
        tri = ph.sb("strictly_before", [P, P])
        tot = ph.sb("tile_totals", [P, NODE_TILES, E0])
        cum = ph.sb("totals_up_to", [P, NODE_TILES, E0])
        one = ph.sb("one_row", [P, NODE_TILES])
        tl = ph.sb("tiles_of_expert", [P, E0])
        tlI = ph.sb("tiles_of_expert_i", [P, E0], I32)
        end = ph.sb("end_tile", [P, E0])
        base = ph.sb("first_slot", [P, E0])
        posf = ph.sb("slot_f", [P, 2, NODE_TILES])
        trash = ph.sb("padding_slot", [P, 1])
        step = ph.sb("slot_tile_no", [P, SLOT_TILES])
        ex = ph.sb("expert_of_tile_f", [P, SLOT_TILES])
        partI = ph.sb("slot_parts_i", [P, 2, 2, NODE_TILES], I32)
        part = ph.sb("slot_parts", [P, 2, 2, NODE_TILES])
        node_no = ph.sb("node_no", [P, NODE_TILES])
        hot_row = ph.sb("slot_row_onehot", [P, RING, 2, P])
        hot_tile = ph.sb("slot_tile_onehot", [P, RING, 2, SLOT_TILES])
        block = ph.block()

        @block.gpsimd
        def _(pool):
            g, made = nc.gpsimd, ph["pool_made"]
            g.memset(tri[:, :], 1.0).then_inc(made, 1)
            g.memset(one[:, :], 1.0).then_inc(made, 1)
            g.memset(S.node_mask[:, :], 1.0).then_inc(made, 1)
            g.iota(trash[:, :], [[0, 1]], base=SLOTS, channel_multiplier=1,
                   allow_small_or_imprecise_dtypes=True).then_inc(made, 1)
            g.iota(step[:, :], [[1, SLOT_TILES]], base=0, channel_multiplier=0,
                   allow_small_or_imprecise_dtypes=True).then_inc(made, 1)
            g.iota(node_no[:, :], [[P, NODE_TILES]], base=0, channel_multiplier=1,
                   allow_small_or_imprecise_dtypes=True).then_inc(made, 1)
            pool.wait_ge(made, 6)
            g.affine_select(out=tri[:, :], in_=tri[:, :], compare_op=ALU.is_gt, fill=0.0, base=0,
                            pattern=[[1, P]], channel_multiplier=-1).then_inc(made, 1)
            g.affine_select(out=S.node_mask[:, NODE_TILES - 1:], in_=S.node_mask[:, NODE_TILES - 1:],
                            compare_op=ALU.is_ge, fill=0.0, base=LAST_ROWS - 1, pattern=[[0, 1]],
                            channel_multiplier=-1).then_inc(made, 1)

        @block.vector
        def _(dve):
            v, own = nc.vector, Own(dve, ph["dve_own"])
            top_two(nc, own, S.logits, top, idx, idxf, hot1, hot2, S.iota_row, E0)
            v.tensor_tensor(S.w2[:, :], top[:, :, 1], top[:, :, 0], ALU.subtract).then_inc(ph["gap"], 1)
            own(v.tensor_tensor(both[:, :, :], hot1[:, :, :], hot2[:, :, :], ALU.add))
            dve.wait_ge(ph["pool_made"], 8)
            own.wait()
            own(v.tensor_tensor(both[:, :, :], both[:, :, :],
                                S.node_mask[:, :].unsqueeze(2).broadcast_to([P, NODE_TILES, E0]), ALU.mult))
            dve.wait_ge(ph["gap_exp"], 1)
            own(v.tensor_scalar_add(S.w1[:, :], S.w2[:, :], 1.0))
            own.wait()
            S.both_ready = own.total
            own(v.reciprocal(S.w1[:, :], S.w1[:, :]))
            own.wait()
            own(v.tensor_tensor(S.w2[:, :], S.w2[:, :], S.w1[:, :], ALU.mult))
            own.wait()
            for w, hot, dst in ((S.w1, hot1, S.wexp), (S.w2, hot2, tot)):
                own(v.tensor_tensor(dst[:, :, :], hot[:, :, :], w[:, :].unsqueeze(2).broadcast_to(
                    [P, NODE_TILES, E0]), ALU.mult))
            own.wait()
            own(v.tensor_tensor(S.wexp[:, :, :], S.wexp[:, :, :], tot[:, :, :], ALU.add))
            own.wait()
            dve.wait_ge(ph["counts"], 1)
            flat = NODE_TILES * E0
            own(v.tensor_copy(tot[:, :, :], S.ps[:, 1, 0:flat].rearrange("p (t e) -> p t e", e=E0)))
            own.wait()
            for e in range(E0):
                own(v.tensor_tensor_scan(cum[:, :, e], one[:, :], tot[:, :, e], 0.0, ALU.mult, ALU.add))
            own.wait()
            own(v.tensor_scalar_add(tlI[:, :], cum[:, NODE_TILES - 1, :], float(P - 1)))
            own.wait()
            own(v.tensor_scalar(tlI[:, :], tlI[:, :], 7, None, ALU.arith_shift_right))
            own.wait()
            own(v.tensor_copy(tl[:, :], tlI[:, :]))
            own.wait()
            own(v.tensor_tensor_scan(end[:, :], one[:, 0:E0], tl[:, :], 0.0, ALU.mult, ALU.add))
            own.wait()
            own(v.tensor_tensor(base[:, :], end[:, :], tl[:, :], ALU.subtract))
            own(v.memset(ex[:, :], 0.0))
            own(v.tensor_tensor(cum[:, :, :], cum[:, :, :], tot[:, :, :], ALU.subtract))
            own.wait()
            own(v.tensor_scalar(base[:, :], base[:, :], float(P), None, ALU.mult))
            own(v.tensor_tensor(cum[:, :, :], cum[:, :, :],
                                S.ps[:, 0, 0:flat].rearrange("p (t e) -> p t e", e=E0), ALU.add))
            for e in range(E0 - 1):
                own.wait()
                own(v.scalar_tensor_tensor(ex[:, :], step[:, :], end[:, e:e + 1], ex[:, :], ALU.is_ge, ALU.add))
            own.wait()
            own(v.tensor_copy(S.expertI[:, :], ex[0:1, :]))
            own(v.tensor_tensor(cum[:, :, :], cum[:, :, :],
                                base[:, :].unsqueeze(1).broadcast_to([P, NODE_TILES, E0]), ALU.add))
            own.wait()
            for m, hot in enumerate((hot1, hot2)):
                own(v.tensor_tensor(tot[:, :, :], cum[:, :, :], hot[:, :, :], ALU.mult))
                own.wait()
                own(v.tensor_reduce(posf[:, m, :], tot[:, :, :], AX.X, ALU.add))
                own.wait()
            own(v.tensor_scalar(posf[:, :, :], posf[:, :, :], trash[:, 0:1], None, ALU.subtract))
            own.wait()
            own(v.tensor_tensor(posf[:, :, :], posf[:, :, :],
                                S.node_mask[:, :].unsqueeze(1).broadcast_to([P, 2, NODE_TILES]), ALU.mult))
            own.wait()
            own(v.tensor_scalar(S.posI[:, :, :], posf[:, :, :], trash[:, 0:1], None, ALU.add))
            own.wait()
            own(v.tensor_scalar(partI[:, 0, :, :], S.posI[:, :, :], P - 1, None, ALU.bitwise_and))
            own(v.tensor_scalar(partI[:, 1, :, :], S.posI[:, :, :], 7, None, ALU.arith_shift_right))
            own.wait()
            own(v.tensor_copy(part[:, :, :, :], partI[:, :, :, :]))
            own.wait()
            dve.sem_inc(ph["places"], RING)
            for i, t, j, n in tiles(dve):
                again(dve, ph["listed"], n)
                for m in range(2):
                    v.tensor_scalar(hot_row[:, j, m, :], S.iota_row[:, :], part[:, 0, m, bass.ds(t, 1)], None,
                                    ALU.is_equal)
                    ins = v.tensor_scalar(hot_tile[:, j, m, :], step[:, :], part[:, 1, m, bass.ds(t, 1)],
                                          node_no[:, bass.ds(t, 1)], ALU.is_equal, ALU.mult)
                ins.then_inc(ph["places"], 1)
            after(dve, ph["listed"], NODE_TILES)
            own(v.tensor_copy(S.slot_node[:, :], S.ps[:, 2, 0:SLOT_TILES]))
            own.wait()

        @block.scalar
        def _(act):
            act.wait_ge(ph["gap"], 1)
            nc.scalar.activation(S.w2[:, :], S.w2[:, :], ACT.Exp).then_inc(ph["gap_exp"], 1)

        @block.tensor
        def _(pe):
            flat = NODE_TILES * E0
            rhs = both[:, :, :].rearrange("p t e -> p (t e)")
            pe.wait_ge(ph["dve_own"], S.both_ready)
            nc.tensor.matmul(S.ps[:, 0, 0:flat], tri[:, :], rhs, start=True, stop=True)
            nc.tensor.matmul(S.ps[:, 1, 0:flat], S.ones[:, :], rhs, start=True, stop=True).then_inc(ph["counts"], 1)
            pe.sem_inc(ph["listed"], RING)

            def five(i, first, last):
                for j in range(RING):
                    after(pe, ph["places"], i * RING + (j + 1))
                    for m in range(2):
                        ins = nc.tensor.matmul(S.ps[:, 2, 0:SLOT_TILES], hot_row[:, j, m, :], hot_tile[:, j, m, :],
                                               start=first and j + m == 0, stop=last and j == RING - 1 and m == 1)
                    ins.then_inc(ph["listed"], 1)
            five(0, True, False)
            with pe.Fori(1, T5 - 1) as i:
                five(i, False, False)
            five(T5 - 1, False, True)


def expert_inputs(nc, S, A):
    with Phase(nc, "expert_inputs") as ph:
        stats, mv, rstd = ln_scratch(ph)
        block = ph.block()

        @block.vector
        def _(dve):
            own = Own(dve, ph["dve_own"])
            layernorm_stats(nc, dve, own, S.QF, stats, mv, rstd, ph["eps_done"], ph["sqrt_done"])
            for t in range(NODE_TILES):
                nc.vector.tensor_scalar(S.XN[:, t, :], S.QF[:, t, :], mv[:, t, 0:1], rstd[:, t:t + 1],
                                        ALU.subtract, ALU.mult).then_inc(ph["xn_ready"], 1)

        @block.scalar
        def _(act):
            ln_root(nc, ph, act, rstd)

        @block.sync
        def _(sp):
            for k in range(T5):
                sp.wait_ge(ph["xn_ready"], RING * (k + 1))
                sp.dma_start(S.xn_dram[k * RING * P:(k + 1) * RING * P, :].rearrange("(t p) d -> p t d", p=P),
                             S.XN[:, k * RING:(k + 1) * RING, :]).then_inc(ph["table_out"], 16)
            sp.wait_ge(ph["table_out"], 16 * T5)


def experts(nc, S, A):
    HC = HID // P
    with Phase(nc, "experts") as ph:
        ph.for_gathers("x_in0", "x_in1")
        xs = ph.sb("slot_rows", [P, 2, D])
        idx = ph.sb("node_idx", [P, 2], I32)
        small = ph.sb("g_b_b1", [P, 2, 4 + HC])
        W1 = ph.sb("expert_w1", [P, 2, 2, HID])
        W2 = ph.sb("expert_w2", [P, 2, HC, D])
        xT = ph.sb("xe_T", [P, 2, 2, P])
        hT = ph.sb("hidden_T", [P, 2, HC, P])
        ys = ph.sb("y_rows", [P, 2, D])
        block = ph.block()

        def pairs(eng, body):
            with eng.Fori(0, SLOT_TILES // 2) as i:
                for h in range(2):
                    body(i, h, i * 2 + h, i * 2 + (h + 1))

        @block.sync
        def _(sp):
            def load(i, h, t, n):
                e = sp.value_load(S.expertI[0:1, bass.ds(t, 1)], min_val=0, max_val=E0 - 1)
                sp.wait_ge(ph["h_psum"], n)
                sp.dma_start(W1[:, h, :, :], A["eW1"][bass.ds(e * D, D), :].rearrange("(c p) n -> p c n", p=P)
                             ).then_inc(ph[f"w1_in{h}"], 16)
                sp.wait_ge(ph["hidden"], n * 2)
                sp.dma_start(small[:, h, :], A["eSmall"][bass.ds(e, 1), :, :].squeeze(0)
                             ).then_inc(ph[f"small_in{h}"], 16)
                sp.wait_ge(ph["y_psum"], n)
                sp.dma_start(W2[:, h, :, :], A["eW2"][bass.ds(e * HID, HID), :].rearrange("(c p) n -> p c n", p=P)
                             ).then_inc(ph[f"w2_in{h}"], 16)
            pairs(sp, load)

        @block.gpsimd
        def _(pool):
            def gather(i, h, t, n):
                pool.wait_ge(ph["xT_psum"], n)
                nc.gpsimd.tensor_copy(idx[:, h:h + 1], S.slot_node[:, bass.ds(t, 1)]).then_inc(ph["idx_ready"], 1)
                pool.wait_ge(ph["idx_ready"], n)
                pool.sem_inc(ph["gather_gate"], 1)
                nc.gpsimd.indirect_dma_start(xs[:, h, :], None, S.xn_dram,
                                             bass.IndirectOffsetOnAxis(ap=idx[:, h:h + 1], axis=0)
                                             ).then_inc(ph[f"x_in{h}"], 16)
            pairs(pool, gather)

        @block.vector
        def _(dve):
            dve.sem_inc(ph["xT_ready"], 2)
            dve.sem_inc(ph["y_ready"], 2)

            def xe(h, i, n):
                dve.wait_ge(ph["xT_psum"], n + 2)
                dve.wait_ge(ph[f"small_in{h}"], i * 16 + 16)
                dve.wait_ge(ph["h_psum"], n)
                for c in range(2):
                    ins = nc.vector.tensor_scalar(xT[:, h, c, :], S.ps[:, 0, c * P:(c + 1) * P], small[:, h, c:c + 1],
                                                  small[:, h, 2 + c:3 + c], ALU.mult, ALU.add)
                ins.then_inc(ph["xT_ready"], 1)

            def y(h, i, n):
                dve.wait_ge(ph["y_psum"], n + 2)
                dve.wait_ge(ph[f"y_out{h}"], i * 16 + 16)
                nc.vector.tensor_copy(ys[:, h, :], S.ps[:, 1, 0:D]).then_inc(ph["y_ready"], 1)

            xe(0, 0, 1)
            with dve.Fori(0, SLOT_TILES // 2 - 1) as i:
                xe(1, i, i * 2 + 2)
                y(0, i, i * 2 + 1)
                xe(0, i + 1, i * 2 + 3)
                y(1, i, i * 2 + 2)
            last = SLOT_TILES // 2 - 1
            xe(1, last, last * 2 + 2)
            y(0, last, last * 2 + 1)
            y(1, last, last * 2 + 2)

        @block.scalar
        def _(act):
            act.sem_inc(ph["hidden"], 2 * 2)
            for h in range(2):
                act.sem_inc(ph[f"y_out{h}"], 16)

            def gelu(i, h, t, n):
                act.wait_ge(ph["y_psum"], n)
                for m in range(HC):
                    if m % 4 == 0:
                        act.wait_ge(ph["h_half"], n * 2 + (m // 4 - 1))
                    ins = nc.scalar.activation(hT[:, h, m, :], S.ps[:, 2 + 2 * h + m // 4, (m % 4) * P:(m % 4 + 1) * P],
                                               ACT.Gelu, bias=small[:, h, 4 + m:5 + m])
                    if m % 4 == 3:
                        ins.then_inc(ph["hidden"], 1)
            def out(i, h, t, n):
                act.wait_ge(ph["y_ready"], n + 2)
                act.dma_start(S.y_dram[bass.ds(t * P, P), :], ys[:, h, :]).then_inc(ph[f"y_out{h}"], 16)

            def step(i, h, t, n):
                gelu(i, h, t, n)
            gelu(0, 0, 0, 1)
            with act.Fori(0, SLOT_TILES // 2 - 1) as i:
                gelu(i, 1, None, i * 2 + 2)
                out(i, 0, i * 2, i * 2 + 1)
                gelu(i, 0, None, i * 2 + 3)
                out(i, 1, i * 2 + 1, i * 2 + 2)
            last = SLOT_TILES // 2 - 1
            gelu(last, 1, None, last * 2 + 2)
            out(last, 0, last * 2, last * 2 + 1)
            out(last, 1, last * 2 + 1, last * 2 + 2)
            for h in range(2):
                act.wait_ge(ph[f"y_out{h}"], 16 * (SLOT_TILES // 2) + 16)

        @block.tensor
        def _(pe):
            for name in ("xT_psum", "h_psum", "y_psum"):
                pe.sem_inc(ph[name], 2)

            def up(h, i, n):
                pe.wait_ge(ph[f"x_in{h}"], i * 16 + 16)
                pe.wait_ge(ph["xT_ready"], n + 1)
                for c in range(2):
                    ins = nc.tensor.transpose(S.ps[:, 0, c * P:(c + 1) * P], xs[:, h, c * P:(c + 1) * P], S.ident[:, :])
                ins.then_inc(ph["xT_psum"], 1)
                pe.wait_ge(ph["xT_ready"], n + 2)
                pe.wait_ge(ph[f"w1_in{h}"], i * 16 + 16)
                pe.wait_ge(ph["hidden"], n * 2)
                for m in range(HC):
                    for c in range(2):
                        ins = nc.tensor.matmul(S.ps[:, 2 + 2 * h + m // 4, (m % 4) * P:(m % 4 + 1) * P],
                                               W1[:, h, c, m * P:(m + 1) * P], xT[:, h, c, :],
                                               start=c == 0, stop=c == 1)
                    if m % 4 == 3 and m < HC - 1:
                        ins.then_inc(ph["h_half"], 1)
                ins.then_inc(ph["h_half"], 1)
                pe.wait_ge(ph["h_half"], n * 2)
                pe.sem_inc(ph["h_psum"], 1)

            def down(h, i, n):
                pe.wait_ge(ph[f"w2_in{h}"], i * 16 + 16)
                pe.wait_ge(ph["hidden"], n * 2 + 4)
                pe.wait_ge(ph["y_ready"], n + 1)
                for m in range(HC):
                    ins = nc.tensor.matmul(S.ps[:, 1, 0:D], hT[:, h, m, :], W2[:, h, m, :],
                                           start=m == 0, stop=m == HC - 1)
                ins.then_inc(ph["y_psum"], 1)

            up(0, 0, 1)
            with pe.Fori(0, SLOT_TILES // 2 - 1) as i:
                up(1, i, i * 2 + 2)
                down(0, i, i * 2 + 1)
                up(0, i + 1, i * 2 + 3)
                down(1, i, i * 2 + 2)
            last = SLOT_TILES // 2 - 1
            up(1, last, last * 2 + 2)
            down(0, last, last * 2 + 1)
            down(1, last, last * 2 + 2)


def combine(nc, S, A):
    with Phase(nc, "combine") as ph:
        ph.for_gathers(*[f"y_in{j}" for j in range(RING)])
        yr = ph.sb("y_of_slots", [P, RING, 2, D])
        idx = ph.sb("slot_ring", [P, RING, 2], I32)
        wr = ph.sb("weights_ring", [P, RING, E0])
        wT = ph.sb("weights_T", [E0, RING, P])
        b2 = ph.sb("expert_b2", [E0, D])
        block = ph.block()

        @block.sync
        def _(sp):
            sp.dma_start(b2[:, :], A["eb2"]).then_inc(ph["b2_in"], 16)

        @block.gpsimd
        def _(pool):
            pool.sem_inc(ph["w_staged"], RING)
            for i, t, j, n in tiles(pool):
                again(pool, ph["x_done"], n)
                nc.gpsimd.tensor_copy(idx[:, j, :], S.posI[:, :, bass.ds(t, 1)].squeeze(2))
                nc.gpsimd.tensor_copy(wr[:, j, :], S.wexp[:, bass.ds(t, 1), :].squeeze(1)).then_inc(ph["w_staged"], 1)
                after(pool, ph["w_staged"], n)
                pool.sem_inc(ph["gather_gate"], 1)
                for m in range(2):
                    nc.gpsimd.indirect_dma_start(yr[:, j, m, :], None, S.y_dram,
                                                 bass.IndirectOffsetOnAxis(ap=idx[:, j, m:m + 1], axis=0)
                                                 ).then_inc(ph[f"y_in{j}"], 16)

        @block.scalar
        def _(act):
            act.sem_inc(ph["wT_ready"], RING)
            for i, t, j, n in tiles(act):
                after(act, ph["wT_psum"], n)
                again(act, ph["b_psum"], n)
                nc.scalar.activation(wT[:, j, :], S.ps[0:E0, 2 + j % 2, 0:P], ACT.Copy).then_inc(ph["wT_ready"], 1)

        @block.tensor
        def _(pe):
            pe.wait_ge(ph["b2_in"], 16)
            pe.sem_inc(ph["wT_psum"], RING)
            pe.sem_inc(ph["b_psum"], RING)
            for i, t, j, n in tiles(pe):
                after(pe, ph["w_staged"], n)
                bank_again(pe, ph["wT_ready"], j, n)
                nc.tensor.transpose(S.ps[0:E0, 2 + j % 2, 0:P], wr[:, j, :], S.ident[:, :]).then_inc(ph["wT_psum"], 1)
                after(pe, ph["wT_ready"], n)
                bank_again(pe, ph["b_added"], j, n)
                nc.tensor.matmul(S.ps[:, j % 2, 0:D], wT[:, j, :], b2[:, :], start=True, stop=True
                                 ).then_inc(ph["b_psum"], 1)

        @block.vector
        def _(dve):
            v = nc.vector
            for name in ("b_added", "y1_added", "x_done"):
                dve.sem_inc(ph[name], RING)
            for i, t, j, n in tiles(dve):
                x = S.X[:, bass.ds(t, 1), :].squeeze(1)
                after(dve, ph["b_psum"], n)
                v.tensor_tensor(x, S.ps[:, j % 2, 0:D], x, ALU.add).then_inc(ph["b_added"], 1)
                dve.wait_ge(ph[f"y_in{j}"], i * 32 + 32)
                after(dve, ph["b_added"], n)
                v.scalar_tensor_tensor(x, yr[:, j, 0, :], S.w1[:, bass.ds(t, 1)], x, ALU.mult, ALU.add
                                       ).then_inc(ph["y1_added"], 1)
                after(dve, ph["y1_added"], n)
                v.scalar_tensor_tensor(x, yr[:, j, 1, :], S.w2[:, bass.ds(t, 1)], x, ALU.mult, ALU.add
                                       ).then_inc(ph["x_done"], 1)


E1, EH1, EH2, SH2 = 4, 128, 64, 128


def project_layer1(nc, S, A):
    with Phase(nc, "project_layer1") as ph:
        ph.ps = S.ps
        W = ph.sb("w_src_dst", [P, 2, 2, D])
        rows = ph.sb("b_src_dst_kw_kb_vw_vb", [P, 6, D])
        stats, mv, rstd = ln_scratch(ph)
        xn = ph.sb("xn_ring", [P, RING, D])
        xT = ph.sb("xn_T", [P, RING, 2, P])
        el = ph.sb("el_rows", [P, RING, D + 1])
        er = ph.sb("er_rows", [P, RING, D])
        prod = ph.sb("attn_times_row", [P, 2, RING, D])
        dots5 = ph.sb("attn_dots_of_five", [P, 2, RING])
        dn = ph.sb("head_centred", [P, RING * HEADS, HD])
        sq = ph.sb("head_squares", [P, RING * HEADS, HD])
        hm = ph.sb("head_mean", [P, RING * HEADS])
        hr = ph.sb("head_rstd", [P, RING * HEADS])
        kf = ph.sb("k_rows", [P, RING, D])
        vf = ph.sb("v_rows", [P, RING, D])
        block = ph.block()
        five_rows = lambda m: rows[:, m, :].unsqueeze(1).broadcast_to([P, RING, D])
        per_head = lambda x: x.unsqueeze(2).broadcast_to([P, RING * HEADS, HD])
        heads = lambda x: x.rearrange("p r (h m) -> p (r h) m", m=HD)

        @block.sync
        def _(sp):
            for m, src in enumerate(("Ws", "Wd")):
                sp.dma_start(W[:, :, m, :], A[src].rearrange("(c p) n -> p c n", p=P)).then_inc(ph["weights_in"], 16)
            for m, src in enumerate(("bs", "bd", "kw", "kb", "vw", "vb")):
                sp.dma_start(rows[:, m, :], bcast(A[src])).then_inc(ph["weights_in"], 16)
            sp.dma_start(S.attn[:, :], bcast(A["attn"])).then_inc(ph["weights_in"], 16)
            with sp.Fori(0, T5) as i:
                sp.wait_ge(ph["el_five"], i + 1)
                sp.dma_start(S.eltab_dram[bass.ds(i * (RING * P), RING * P), :].rearrange("(t p) d -> p t d", p=P),
                             el[:, :, :]).then_inc(ph["el_out"], 16)
            sp.wait_ge(ph["el_out"], 16 * T5 + 16)

        @block.gpsimd
        def _(pool):
            g = nc.gpsimd
            pool.sem_inc(ph["xn_kept"], RING)
            pool.sem_inc(ph["er_kept"], RING)
            pool.sem_inc(ph["v_scaled"], 1)
            pool.wait_ge(ph["weights_in"], 144)
            with pool.Fori(0, T5) as i:
                for j in range(RING):
                    after(pool, ph["xn_ready"], i * RING + (j + 1))
                    g.tensor_copy(S.XN[:, bass.ds(i * RING + j, 1), :], xn[:, j:j + 1, :]
                                  ).then_inc(ph["xn_kept"], 1)
                for j in range(RING):
                    after(pool, ph["er_done"], i * RING + (j + 1))
                    g.tensor_copy(S.QF[:, bass.ds(i * RING + j, 1), :], er[:, j:j + 1, :]).then_inc(ph["er_kept"], 1)
                pool.wait_ge(ph["normed"], i + 1)
                pool.wait_ge(ph["kv_used"], i * RING + RING)
                g.tensor_tensor(vf[:, :, :], dn[:, :, :].rearrange("p (r h) m -> p r (h m)", r=RING), five_rows(4),
                                ALU.mult).then_inc(ph["v_scaled"], 1)
                pool.wait_ge(ph["v_scaled"], i + 2)
                g.tensor_tensor(vf[:, :, :], vf[:, :, :], five_rows(5), ALU.add).then_inc(ph["v_ready"], 1)

        @block.vector
        def _(dve):
            v, own = nc.vector, Own(dve, ph["dve_own"])
            layernorm_stats(nc, dve, own, S.X, stats, mv, rstd, ph["eps_done"], ph["sqrt_done"])
            dve.wait_ge(ph["weights_in"], 144)
            own(v.tensor_scalar(S.attn[:, :], S.attn[:, :], 0.6, None, ALU.mult))
            own.wait()
            for name in ("xn_ready", "er_done"):
                dve.sem_inc(ph[name], RING)
            dve.sem_inc(ph["el_out"], 16)
            with dve.Fori(0, T5) as i:
                norm_five(nc, ph, dve, S.X, mv, rstd, xn, i)
                after(dve, ph["xn_ready"], i * RING + RING)
                v.tensor_reduce(hm[:, :], heads(xn[:, :, :]), AX.X, ALU.add).then_inc(ph["head_sums"], 1)
                dve.wait_ge(ph["el_out"], i * 16 + 16)
                for j in range(RING):
                    n = i * RING + (j + 1)
                    after(dve, ph["p_psum"], n)
                    v.tensor_tensor(el[:, j, 0:D], S.ps[:, j % 2, 0:D], rows[:, 0, :], ALU.add)
                    again(dve, ph["er_kept"], n)
                    ins = v.tensor_tensor(er[:, j, :], S.ps[:, j % 2, D:2 * D], rows[:, 1, :], ALU.add)
                    ins.then_inc(ph["er_done"], 1)
                after(dve, ph["er_done"], i * RING + RING)
                for j in range(RING):
                    for m, row in enumerate((el[:, j, 0:D], er[:, j, :])):
                        ins = v.tensor_tensor_reduce(out=prod[:, m, j, :], in0=row, in1=S.attn[:, :], scale=1.0,
                                                     scalar=0.0, op0=ALU.mult, op1=ALU.add,
                                                     accum_out=dots5[:, m, j:j + 1])
                ins.then_inc(ph["attn_dots"], 1)
                dve.wait_ge(ph["attn_dots"], i + 1)
                v.tensor_copy(el[:, :, D], dots5[:, 0, :])
                v.tensor_copy(S.qk[:, 1, bass.ds(i * RING, RING)], dots5[:, 1, :])
                dve.wait_ge(ph["head_sums"], i + 1)
                v.tensor_scalar(hm[:, :], hm[:, :], 1.0 / HD, None, ALU.mult).then_inc(ph["el_five"], 1)
                dve.wait_ge(ph["el_five"], i + 1)
                dve.wait_ge(ph["v_scaled"], i + 1)
                v.tensor_tensor(dn[:, :, :], heads(xn[:, :, :]), per_head(hm[:, :]), ALU.subtract
                                ).then_inc(ph["centred"], 1)
                dve.wait_ge(ph["squared"], i + 1)
                v.tensor_reduce(hr[:, :], sq[:, :, :], AX.X, ALU.add).then_inc(ph["square_sums"], 1)
                dve.wait_ge(ph["stds"], i + 1)
                v.tensor_scalar_add(hr[:, :], hr[:, :], 1e-5).then_inc(ph["std_eps"], 1)
                dve.wait_ge(ph["std_eps"], i + 1)
                v.reciprocal(hr[:, :], hr[:, :]).then_inc(ph["std_inv"], 1)
                dve.wait_ge(ph["std_inv"], i + 1)
                v.tensor_tensor(dn[:, :, :], dn[:, :, :], per_head(hr[:, :]), ALU.mult).then_inc(ph["normed"], 1)
                dve.wait_ge(ph["normed"], i + 1)
                dve.wait_ge(ph["kv_used"], i * RING + RING)
                v.tensor_tensor(kf[:, :, :], dn[:, :, :].rearrange("p (r h) m -> p r (h m)", r=RING), five_rows(2),
                                ALU.mult).then_inc(ph["k_scaled"], 1)
                dve.wait_ge(ph["k_scaled"], i + 1)
                v.tensor_tensor(kf[:, :, :], kf[:, :, :], five_rows(3), ALU.add).then_inc(ph["k_ready"], 1)
            dve.wait_ge(ph["kv_used"], NODE_TILES + RING)
            for c in range(2):
                own(v.scalar_tensor_tensor(S.kvbd[:, c, 0:P], S.ps[:, 6 + c, 0:P], 1.0 / NODES, S.head_blocks[:, :],
                                           ALU.mult, ALU.mult))
            own.wait()

        @block.scalar
        def _(act):
            ln_root(nc, ph, act, rstd)
            act.sem_inc(ph["xT_ready"], RING)
            with act.Fori(0, T5) as i:
                for j in range(RING):
                    n = i * RING + (j + 1)
                    again(act, ph["p_psum"], n)
                    copy_transposed(nc, ph, act, j, n, 4 + j % 2, xT)
                act.wait_ge(ph["centred"], i + 1)
                nc.scalar.activation(sq[:, :, :], dn[:, :, :], ACT.Square).then_inc(ph["squared"], 1)
                act.wait_ge(ph["square_sums"], i + 1)
                nc.scalar.activation(hr[:, :], hr[:, :], ACT.Sqrt, scale=1.0 / (HD - 1)).then_inc(ph["stds"], 1)

        @block.tensor
        def _(pe):
            pe.wait_ge(ph["weights_in"], 144)
            for name in ("xT_psum", "p_psum", "kv_used"):
                pe.sem_inc(ph[name], RING)

            def group(i, first, last):
                for j in range(RING):
                    n = i * RING + (j + 1)
                    after(pe, ph["xn_ready"], n)
                    bank_again(pe, ph["xT_ready"], j, n)
                    transpose_tile(nc, ph, pe, xn, j, 4 + j % 2, S.ident)
                    after(pe, ph["xT_ready"], n)
                    bank_again(pe, ph["er_done"], j, n)
                    for c in range(2):
                        ins = nc.tensor.matmul(S.ps[:, j % 2, :], xT[:, j, c, :],
                                               W[:, c, :, :].rearrange("p a n -> p (a n)"), start=c == 0, stop=c == 1)
                    ins.then_inc(ph["p_psum"], 1)
                pe.wait_ge(ph["k_ready"], i + 1)
                pe.wait_ge(ph["v_ready"], i + 1)
                for j in range(RING):
                    rows_ = LAST_ROWS if last and j == RING - 1 else P
                    for c in range(2):
                        ins = nc.tensor.matmul(S.ps[:, 6 + c, 0:P], kf[0:rows_, j, c * P:(c + 1) * P],
                                               vf[0:rows_, j, c * P:(c + 1) * P], start=first and j == 0,
                                               stop=last and j == RING - 1)
                    ins.then_inc(ph["kv_used"], 1)
            group(0, True, False)
            with pe.Fori(1, T5 - 1) as i:
                group(i, False, False)
            group(T5 - 1, False, True)


def score_layer1(nc, S, A):
    N = GROUP * D
    with Phase(nc, "score_layer1") as ph:
        idx = ph.sb("gather_idx", [P, LANES, GROUP], I32)
        got = ph.sb("el_of_sources", [P, LANES, GROUP, D + 1])
        relB = ph.sb("rel_bcast", [P, LANES, GROUP * P])
        hot = ph.sb("dst_onehot_T", [P, LANES, GROUP * P])
        attn = ph.sb("attn_rows", [P, D])
        linear = ph.sb("linear_part", [P, 2, GROUP])
        dots = ph.sb("dots", [P, GROUP])
        ps2 = S.ps[:, :, :].rearrange("p b n -> p (b n)")
        z = lambda h: ps2[:, (h % 2) * 1536:(h % 2) * 1536 + N]
        lin = lambda h: ps2[:, (h % 2) * 1536 + N:(h % 2) * 1536 + N + GROUP]
        block = ph.block()

        def act_items(act):
            for i, h, k, n in groups(act):
                yield i, h, k, n
                act.wait_ge(ph["rows_used"], n + LANES)
                nc.scalar.activation(z(h), z(h), ACT.Abs).then_inc(ph["abs_ready"], 1)

        gather_edges(nc, S, ph, block, S.eltab_dram, idx, got, relB, LANES, act_items)

        @block.vector
        def _(dve):
            v = nc.vector
            for name in ("hot_ready", "rows_used", "dotted"):
                dve.sem_inc(ph[name], LANES)
            for h in range(AHEAD):
                onehot_T(nc, S, ph, dve, hot, relB, 0, h, h + 1)
            v.tensor_scalar(attn[:, :], S.attn[:, :], 0.4 / 0.6, None, ALU.mult).then_inc(ph["attn_scaled"], 1)
            dve.wait_ge(ph["attn_scaled"], 1)
            for i, h, k, n, later in groups_ahead(dve, AHEAD):
                dve.wait_ge(ph[f"gathered{h}"], i * (16 * GROUP) + 16 * GROUP)
                dve.wait_ge(ph["dst_psum"], n + LANES)
                v.tensor_tensor(linear[:, h % 2, :], lin(h), got[:, h, :, D], ALU.add)
                v.tensor_tensor(z(h).rearrange("p (g d) -> p g d", d=D), z(h).rearrange("p (g d) -> p g d", d=D),
                                got[:, h, :, 0:D], ALU.add).then_inc(ph["rows_used"], 1)
                if later:
                    onehot_T(nc, S, ph, dve, hot, relB, later[0], later[1], later[3])
                dve.wait_ge(ph["abs_ready"], n)
                for j in range(GROUP):
                    ins = v.tensor_tensor_reduce(out=z(h)[:, j * D:(j + 1) * D], in0=z(h)[:, j * D:(j + 1) * D],
                                                 in1=attn[:, :], scale=1.0, scalar=0.0, op0=ALU.mult, op1=ALU.add,
                                                 accum_out=dots[:, j:j + 1])
                ins.then_inc(ph["dotted"], 1)
                dve.wait_ge(ph["dotted"], n + LANES)
                v.tensor_tensor(S.scoreX[:, bass.ds(k * GROUP, GROUP)], dots[:, :], linear[:, h % 2, :], ALU.add)

        @block.tensor
        def _(pe):
            pe.sem_inc(ph["dst_psum"], LANES)
            for i, h, k, n in groups(pe):
                blocks = dst_blocks(pe, S, k)
                pe.wait_ge(ph["hot_ready"], n + LANES)
                pe.wait_ge(ph["dotted"], n + LANES - 2)
                for j, b in enumerate(blocks):
                    nc.tensor.matmul(z(h)[:, j * D:(j + 1) * D], hot[:, h, j * P:(j + 1) * P],
                                     S.QF[:, bass.ds(b, 1), :].squeeze(1), start=True, stop=True)
                    last = nc.tensor.matmul(lin(h)[:, j:j + 1], hot[:, h, j * P:(j + 1) * P],
                                            S.qk[:, 1, bass.ds(b, 1)], start=True, stop=True)
                last.then_inc(ph["dst_psum"], 1)


def mix_layer1(nc, S, A):
    with Phase(nc, "mix_layer1") as ph:
        ph.ps = S.ps
        xr = ph.sb("xn_ring", [P, RING, D])
        xT = ph.sb("xn_T", [P, RING, 2, P])
        block = ph.block()

        @block.gpsimd
        def _(pool):
            stage_tiles(nc, ph, pool, S.XN, xr, "x_staged", "xT_psum")

        @block.scalar
        def _(act):
            act.sem_inc(ph["xT_ready"], RING)
            for i, t, j, n in tiles(act):
                again(act, ph["m_psum"], n)
                copy_transposed(nc, ph, act, j, n, 4 + j % 2, xT)

        @block.tensor
        def _(pe):
            pe.sem_inc(ph["xT_psum"], RING)
            pe.sem_inc(ph["m_psum"], RING)
            for i, t, j, n in tiles(pe):
                after(pe, ph["x_staged"], n)
                bank_again(pe, ph["xT_ready"], j, n)
                transpose_tile(nc, ph, pe, xr, j, 4 + j % 2, S.ident)
                after(pe, ph["xT_ready"], n)
                bank_again(pe, ph["added"], j, n)
                for c in range(2):
                    ins = nc.tensor.matmul(S.ps[:, j % 2, c * P:(c + 1) * P], xT[:, j, c, :], S.kvbd[:, c, 0:P],
                                           start=True, stop=True)
                ins.then_inc(ph["m_psum"], 1)

        @block.vector
        def _(dve):
            v = nc.vector
            add_edge_sums(nc, ph, S, dve)
            dve.sem_inc(ph["added"], RING)
            dve.sem_inc(ph["xn_added"], RING)
            for i, t, j, n in tiles(dve):
                x = S.X[:, bass.ds(t, 1), :].squeeze(1)
                after(dve, ph["m_psum"], n)
                v.tensor_tensor(x, S.ps[:, j % 2, 0:D], x, ALU.add).then_inc(ph["added"], 1)
                after(dve, ph["added"], n)
                v.tensor_tensor(x, x, S.XN[:, bass.ds(t, 1), :].squeeze(1), ALU.add)


def gates_layer1(nc, S, A):
    with Phase(nc, "gates_layer1") as ph:
        ph.ps = S.ps
        gW = ph.sb("w_gate", [P, 2, E1])
        gb = ph.sb("b_gate", [P, E1])
        stats, mv, rstd = ln_scratch(ph)
        xf = ph.sb("xf_ring", [P, RING, D])
        xT = ph.sb("xf_T", [P, RING, 2, P])
        lg = ph.sb("logits4", [P, NODE_TILES, E1])
        mx = ph.sb("logit_max", [P, NODE_TILES])
        top = ph.sb("top8", [P, NODE_TILES, 8])
        idx = ph.sb("top8_idx", [P, NODE_TILES, 8], U32)
        idxf = ph.sb("top8_idx_f", [P, NODE_TILES, 8])
        hot1 = ph.sb("hot1", [P, NODE_TILES, E1])
        hot2 = ph.sb("hot2", [P, NODE_TILES, E1])
        block = ph.block()
        wide = lambda x: x.unsqueeze(2).broadcast_to([P, NODE_TILES, E1])

        @block.sync
        def _(sp):
            sp.dma_start(gW[:, :, :], A["gW"].rearrange("(c p) n -> p c n", p=P)).then_inc(ph["weights_in"], 16)
            sp.dma_start(gb[:, :], bcast(A["gb"])).then_inc(ph["weights_in"], 16)
            sp.wait_ge(ph["weights_in"], 32)

        @block.gpsimd
        def _(pool):
            keep_tiles(nc, ph, pool, xf, S.QF)

        @block.vector
        def _(dve):
            v, own = nc.vector, Own(dve, ph["dve_own"])
            layernorm_stats(nc, dve, own, S.X, stats, mv, rstd, ph["eps_done"], ph["sqrt_done"])
            dve.wait_ge(ph["weights_in"], 32)
            for name in ("xn_ready", "logits"):
                dve.sem_inc(ph[name], RING)
            for i, t, j, n in tiles(dve):
                if j == 0:
                    norm_five(nc, ph, dve, S.X, mv, rstd, xf, i)
                after(dve, ph["l_psum"], n)
                v.tensor_tensor(lg[:, bass.ds(t, 1), :].squeeze(1), S.ps[:, j % 2, 0:E1], gb[:, :], ALU.add
                                ).then_inc(ph["logits"], 1)
            after(dve, ph["logits"], NODE_TILES)
            own(v.memset(S.logits[:, :, :], -1.0))
            own(v.tensor_reduce(mx[:, :], lg[:, :, :], AX.X, ALU.max))
            own.wait()
            v.tensor_tensor(lg[:, :, :], lg[:, :, :], wide(mx[:, :]), ALU.subtract).then_inc(ph["shifted"], 1)
            dve.wait_ge(ph["exps"], 1)
            own(v.tensor_reduce(mx[:, :], lg[:, :, :], AX.X, ALU.add))
            own.wait()
            own(v.reciprocal(mx[:, :], mx[:, :]))
            own.wait()
            own(v.tensor_tensor(S.logits[:, :, 0:E1], lg[:, :, :], wide(mx[:, :]), ALU.mult))
            own.wait()
            top_two(nc, own, S.logits, top, idx, idxf, hot1, hot2, S.iota_row, 8)
            v.tensor_tensor(S.w2[:, :], top[:, :, 1], top[:, :, 0], ALU.subtract).then_inc(ph["gap"], 1)
            dve.wait_ge(ph["gap_exp"], 1)
            own(v.tensor_scalar_add(S.w1[:, :], S.w2[:, :], 1.0))
            own.wait()
            own(v.reciprocal(S.w1[:, :], S.w1[:, :]))
            own.wait()
            own(v.tensor_tensor(S.w2[:, :], S.w2[:, :], S.w1[:, :], ALU.mult))
            own.wait()
            own(v.tensor_tensor(hot1[:, :, :], hot1[:, :, :], wide(S.w1[:, :]), ALU.mult))
            own(v.tensor_tensor(hot2[:, :, :], hot2[:, :, :], wide(S.w2[:, :]), ALU.mult))
            own.wait()
            own(v.memset(S.wexp[:, :, :], 1.0))
            own.wait()
            own(v.tensor_tensor(S.wexp[:, :, 0:E1], hot1[:, :, :], hot2[:, :, :], ALU.add))
            own.wait()

        @block.scalar
        def _(act):
            ln_root(nc, ph, act, rstd)
            act.sem_inc(ph["xT_ready"], RING)
            for i, t, j, n in tiles(act):
                again(act, ph["l_psum"], n)
                copy_transposed(nc, ph, act, j, n, 4 + j % 2, xT)
            act.wait_ge(ph["shifted"], 1)
            nc.scalar.activation(lg[:, :, :], lg[:, :, :], ACT.Exp).then_inc(ph["exps"], 1)
            act.wait_ge(ph["gap"], 1)
            nc.scalar.activation(S.w2[:, :], S.w2[:, :], ACT.Exp).then_inc(ph["gap_exp"], 1)

        @block.tensor
        def _(pe):
            pe.wait_ge(ph["weights_in"], 32)
            for name in ("xT_psum", "l_psum"):
                pe.sem_inc(ph[name], RING)
            for i, t, j, n in tiles(pe):
                after(pe, ph["xn_ready"], n)
                bank_again(pe, ph["xT_ready"], j, n)
                transpose_tile(nc, ph, pe, xf, j, 4 + j % 2, S.ident)
                after(pe, ph["xT_ready"], n)
                bank_again(pe, ph["logits"], j, n)
                for c in range(2):
                    ins = nc.tensor.matmul(S.ps[:, j % 2, 0:E1], xT[:, j, c, :], gW[:, c, :],
                                           start=c == 0, stop=c == 1)
                ins.then_inc(ph["l_psum"], 1)


def ffn_layer1(nc, S, A):
    with Phase(nc, "ffn_layer1") as ph:
        ph.ps = S.ps
        sW1 = ph.sb("shared_w1", [P, 2, D])
        sW2 = ph.sb("shared_w2", [P, 2, SH2])
        sW3 = ph.sb("shared_w3", [P, D])
        eW1 = ph.sb("expert_w1", [P, E1, 2, EH1])
        eW2 = ph.sb("expert_w2", [P, E1, EH2])
        eW3 = ph.sb("expert_w3", [EH2, E1, D])
        b3 = ph.sb("output_biases", [E1 + 1, D])
        bT = ph.sb("hidden_biases", [P, 3 + E1])
        bE2 = ph.sb("expert_b2", [EH2, E1])
        xr = ph.sb("xf_ring", [P, RING, D])
        wr = ph.sb("weights_ring", [P, RING, E1 + 1])
        xT = ph.sb("xf_T", [P, RING, 2, P])
        wT = ph.sb("weights_T", [E1 + 1, RING, P])
        s1 = ph.sb("shared_h1_T", [P, RING, 2, P])
        s2 = ph.sb("shared_h2_T", [P, RING, P])
        e1 = ph.sb("expert_h1_T", [P, RING, E1, P])
        e2 = ph.sb("expert_h2_T", [EH2, RING, E1, P])
        block = ph.block()
        ps = S.ps

        @block.sync
        def _(sp):
            for dst, src in ((sW1[:, :, :], A["sW1"].rearrange("(c p) n -> p c n", p=P)),
                             (sW2[:, :, :], A["sW2"].rearrange("(c p) n -> p c n", p=P)), (sW3[:, :], A["sW3"]),
                             (eW2[:, :, :], A["eW2b"].rearrange("e p n -> p e n")),
                             (eW3[:, :, :], A["eW3b"].rearrange("e p n -> p e n")), (b3[:, :], A["b3"]),
                             (bT[:, :], A["bT"]), (bE2[:, :], A["bE2"])):
                sp.dma_start(dst, src).then_inc(ph["weights_in"], 16)
            for e in range(E1):
                sp.dma_start(eW1[:, e, :, :], A["eW1b"][e, :, :].rearrange("(c p) n -> p c n", p=P)
                             ).then_inc(ph["weights_in"], 16)
            sp.wait_ge(ph["weights_in"], 16 * (8 + E1))

        @block.gpsimd
        def _(pool):
            pool.sem_inc(ph["staged"], RING)
            for i, t, j, n in tiles(pool):
                again(pool, ph["xT_psum"], n)
                nc.gpsimd.tensor_copy(wr[:, j, :], S.wexp[:, bass.ds(t, 1), 0:E1 + 1].squeeze(1))
                nc.gpsimd.tensor_copy(xr[:, j:j + 1, :], S.QF[:, bass.ds(t, 1), :]).then_inc(ph["staged"], 1)

        @block.tensor
        def _(pe):
            mm = nc.tensor.matmul
            pe.wait_ge(ph["weights_in"], 16 * (8 + E1))
            for name in ("xT_psum", "h1_psum", "h2_psum", "o_psum"):
                pe.sem_inc(ph[name], RING)
            for i, t, j, n in tiles(pe):
                after(pe, ph["staged"], n)
                pe.wait_ge(ph["xT_ready"], n + RING - 1)
                nc.tensor.transpose(ps[0:E1 + 1, 0, D:D + P], wr[:, j, :], S.ident[:, :])
                transpose_tile(nc, ph, pe, xr, j, 0, S.ident)
                after(pe, ph["xT_ready"], n)
                pe.wait_ge(ph["h1_ready"], n + RING - 1)
                for m in range(2):
                    for c in range(2):
                        mm(ps[:, 1, m * P:(m + 1) * P], sW1[:, c, m * P:(m + 1) * P], xT[:, j, c, :],
                           start=c == 0, stop=c == 1)
                for e in range(E1):
                    for c in range(2):
                        ins = mm(ps[:, 2, e * P:(e + 1) * P], eW1[:, e, c, :], xT[:, j, c, :],
                                 start=c == 0, stop=c == 1)
                ins.then_inc(ph["h1_psum"], 1)
                after(pe, ph["h1_ready"], n)
                pe.wait_ge(ph["h2_ready"], n + RING - 1)
                for c in range(2):
                    mm(ps[:, 3, 0:P], sW2[:, c, :], s1[:, j, c, :], start=c == 0, stop=c == 1)
                for e in range(E1):
                    ins = mm(ps[0:EH2, 4, e * P:(e + 1) * P], eW2[:, e, :], e1[:, j, e, :], start=True, stop=True)
                ins.then_inc(ph["h2_psum"], 1)
                after(pe, ph["h2_ready"], n)
                pe.wait_ge(ph["x_done"], n + RING - 1)
                mm(ps[:, 5, 0:D], s2[:, j, :], sW3[:, :], start=True, stop=False)
                mm(ps[:, 5, 0:D], wT[:, j, :], b3[:, :], start=False, stop=True)
                for e in range(E1):
                    ins = mm(ps[:, 6 + e // 2, (e % 2) * D:(e % 2 + 1) * D], e2[:, j, e, :], eW3[:, e, :],
                             start=True, stop=True)
                ins.then_inc(ph["o_psum"], 1)

        @block.scalar
        def _(act):
            a = nc.scalar
            act.wait_ge(ph["weights_in"], 16 * (8 + E1))
            for name in ("xT_ready", "h1_ready", "h2_ready"):
                act.sem_inc(ph[name], RING)
            for i, t, j, n in tiles(act):
                again(act, ph["o_psum"], n)
                after(act, ph["xT_psum"], n)
                a.activation(wT[:, j, :], ps[0:E1 + 1, 0, D:D + P], ACT.Copy)
                copy_transposed(nc, ph, act, j, n, 0, xT)
                after(act, ph["h1_psum"], n)
                for m in range(2):
                    a.activation(s1[:, j, m, :], ps[:, 1, m * P:(m + 1) * P], ACT.Relu, bias=bT[:, m:m + 1])
                for e in range(E1):
                    ins = a.activation(e1[:, j, e, :], ps[:, 2, e * P:(e + 1) * P], ACT.Relu, bias=bT[:, 3 + e:4 + e])
                ins.then_inc(ph["h1_ready"], 1)
                after(act, ph["h2_psum"], n)
                a.activation(s2[:, j, :], ps[:, 3, 0:P], ACT.Relu, bias=bT[:, 2:3])
                for e in range(E1):
                    ins = a.activation(e2[:, j, e, :], ps[0:EH2, 4, e * P:(e + 1) * P], ACT.Relu, bias=bE2[:, e:e + 1])
                ins.then_inc(ph["h2_ready"], 1)

        @block.vector
        def _(dve):
            v = nc.vector
            dve.sem_inc(ph["x_done"], RING)
            dve.sem_inc(ph["x_step"], 1)
            for i, t, j, n in tiles(dve):
                x = S.X[:, bass.ds(t, 1), :].squeeze(1)
                after(dve, ph["o_psum"], n)
                v.tensor_tensor(x, ps[:, 5, 0:D], x, ALU.add).then_inc(ph["x_step"], 1)
                for e in range(E1):
                    dve.wait_ge(ph["x_step"], i * (RING * E1) + (j * E1 + e + 2))
                    ins = v.scalar_tensor_tensor(x, ps[:, 6 + e // 2, (e % 2) * D:(e % 2 + 1) * D],
                                                 S.wexp[:, bass.ds(t, 1), e], x, ALU.mult, ALU.add)
                    ins.then_inc(ph["x_step"] if e < E1 - 1 else ph["x_done"], 1)


def reset_semaphores(nc):
    with Phase(nc, "reset") as ph:
        numbers = sorted(Phase.numbers)
        block = ph.block()

        @block.gpsimd
        def _(pool):
            while numbers:
                first = last = numbers.pop(0)
                while numbers and numbers[0] == last + 1:
                    last = numbers.pop(0)
                pool.sem_clear(range(first, last + 1))
        Phase.numbers.clear()


def write_out(nc, S, out):
    with Phase(nc, "write_out") as ph:
        block = ph.block()

        @block.sync
        def _(sp):
            sp.dma_start(out[0:NODES_PAD - P, :].rearrange("(t p) d -> p t d", p=P),
                         S.X[:, 0:NODE_TILES - 1, :]).then_inc(ph["out"], 16)
            sp.dma_start(out[NODES_PAD - P:NODES, :], S.X[0:LAST_ROWS, NODE_TILES - 1, :]).then_inc(ph["out"], 16)
            sp.wait_ge(ph["out"], 32)


def build(nc, A, out):
    S = State()
    Phase.numbers.clear()
    with ExitStack() as ctx:
        Phase.lasting = ctx

        def sb(name, shape, dt=F32):
            return ctx.enter_context(nc.sbuf_tensor(name, shape, dt))

        def dram(name, shape, dt=F32):
            return nc.dram_tensor(name, shape, dt, kind="Internal").ap()
        S.ps = ctx.enter_context(nc.psum_tensor("ps", [P, 8, 512], F32))
        S.ident = sb("ident", [P, P])
        S.ones = sb("ones", [P, P])
        S.iota_row = sb("iota_row", [P, P])
        S.iota_col = sb("iota_col", [P, 1])
        S.srcX = sb("src_by_step", [P, STEPS], I32)
        S.relX = sb("rel_by_step", [P, STEPS])
        S.validX = sb("valid_by_step", [P, STEPS])
        S.penX = sb("penalty_by_step", [P, STEPS])
        S.scoreX = sb("score_by_step", [P, STEPS])
        S.weightX = sb("weight_by_step", [P, STEPS])
        S.blockI = sb("block_by_step", [1, GROUPS, 8], I32)
        S.cut = sb("segment_cuts", [GROUPS, 2, GROUP * P])
        S.row_cut = sb("row_has_cut", [GROUPS, 2])
        S.X = sb("x", [P, NODE_TILES, D])
        S.XN = sb("xn", [P, NODE_TILES, D])
        S.QF = sb("q_features", [P, NODE_TILES, D])
        S.acc = sb("edge_sums", [P, NODE_TILES, D + 1])
        S.qk = sb("q_k_scalars", [P, 2, NODE_TILES])
        S.attn = sb("attn_rows", [P, D])
        S.kvbd = sb("kv_blocks", [P, 2, P + 4])
        S.inv_sum = sb("inv_softmax_sum", [P, NODE_TILES])
        S.node_mask = sb("node_mask", [P, NODE_TILES])
        S.logits = sb("logits", [P, NODE_TILES, E0])
        S.wexp = sb("expert_weights", [P, NODE_TILES, E0])
        S.w1 = sb("first_weight", [P, NODE_TILES])
        S.w2 = sb("second_weight", [P, NODE_TILES])
        S.posI = sb("slots_of_node", [P, 2, NODE_TILES], I32)
        S.slot_node = sb("node_of_slot", [P, SLOT_TILES], I32)
        S.expertI = sb("expert_of_tile", [1, SLOT_TILES], I32)
        S.head_blocks = sb("head_blocks", [P, P])
        S.rel_dram = dram("rel_by_step_rows", (STEPS, P))
        S.key_dram = dram("keys", (STEPS * P + 2,))
        S.htab_dram = dram("h_table", (NODES_PAD, D + 1))
        S.step_dram = dram("rows_by_step", (GROUPS, P, GROUP * D))
        S.xn_dram = dram("xn_table", (NODES_PAD, D))
        S.eltab_dram = dram("el_table", (NODES_PAD, D + 1))
        S.y_dram = dram("y_by_slot", (SLOT_ROWS, D))
        S.layer = 0
        S.loads = 0
        prepare_edges(nc, S, A)
        project_layer0(nc, S, A)
        score_and_mix_layer0(nc, S, A)
        softmax_weights(nc, S, A, True)
        aggregate(nc, S, A)
        router(nc, S, A)
        dispatch_plan(nc, S, A)
        expert_inputs(nc, S, A)
        experts(nc, S, A)
        combine(nc, S, A)
        S.layer = 1
        reset_semaphores(nc)
        project_layer1(nc, S, A)
        score_layer1(nc, S, A)
        softmax_weights(nc, S, A, False)
        aggregate(nc, S, A)
        mix_layer1(nc, S, A)
        gates_layer1(nc, S, A)
        ffn_layer1(nc, S, A)
        write_out(nc, S, out)


def layout(inputs):
    import numpy as np
    c = np.ascontiguousarray
    a = {}
    x = np.zeros((NODES_PAD, D), np.float32)
    x[:NODES] = inputs["x"]
    src = np.zeros(EDGE_TILES * P, np.int32)
    src[:EDGES] = inputs["src"]
    dst = np.full(EDGE_TILES * P, PAD_NODE, np.int32)
    dst[:EDGES] = inputs["dst"]
    dst = dst.reshape(EDGE_TILES, P)
    before = np.zeros(EDGE_TILES, np.int32)
    before[1:] = dst[:-1, P - 1]
    a.update(x=x, src=src.reshape(EDGE_TILES, P), dst=dst, dst_before=c(before.reshape(EDGE_CHUNKS, EDGE_ROWS).T))
    a["Wv"] = c(inputs["L0_gnn_Wv"])
    a["bv"] = c(inputs["L0_gnn_bv"])
    a["wq"] = c(inputs["L0_gnn_wq"])
    a["wk"] = c(inputs["L0_gnn_wk"])
    a["bq"] = c(inputs["L0_gnn_bq"]).reshape(1)
    a["bk"] = c(inputs["L0_gnn_bk"]).reshape(1)
    a["WqkvT"] = c(np.asarray(inputs["L0_mix_Wqkv"]).T)
    for name in ("ln1_g", "ln1_b", "ln2_g", "ln2_b"):
        a[name] = c(inputs["L0_mix_" + name])
    a["mW1T"], a["mW2T"] = c(np.asarray(inputs["L0_mix_W1"]).T), c(np.asarray(inputs["L0_mix_W2"]).T)
    a["mb1"] = c(np.asarray(inputs["L0_mix_b1"]).reshape(2, P).T)
    a["mb2"] = c(inputs["L0_mix_b2"])
    a["Wr"], a["br"] = c(inputs["L0_ffn_Wr"]), c(inputs["L0_ffn_br"])
    a["eW1"] = c(inputs["L0_ffn_W1"]).reshape(E0 * D, HID)
    a["eW2"] = c(inputs["L0_ffn_W2"]).reshape(E0 * HID, D)
    a["eb2"] = c(inputs["L0_ffn_b2"])
    a["eSmall"] = c(np.concatenate([np.asarray(inputs["L0_ffn_" + n]).reshape(E0, -1, P).transpose(0, 2, 1)
                                    for n in ("ln_g", "ln_b", "b1")], axis=2))
    for name, key in (("Ws", "W_src"), ("bs", "b_src"), ("Wd", "W_dst"), ("bd", "b_dst"), ("attn", "attn")):
        a[name] = c(inputs["L1_gnn_" + key])
    for name, key in (("kw", "kln_weight"), ("kb", "kln_bias"), ("vw", "vln_weight"), ("vb", "vln_bias")):
        a[name] = c(inputs["L1_mix_" + key]).reshape(D)
    f = {k[7:]: np.asarray(v) for k, v in inputs.items() if k.startswith("L1_ffn_")}
    a.update(sW1=c(f["sW1"]), sW2=c(f["sW2"]), sW3=c(f["sW3"]), eW1b=c(f["eW1"]), eW2b=c(f["eW2"]), eW3b=c(f["eW3"]),
             gW=c(f["gW"]), gb=c(f["gb"]), b3=c(np.concatenate([f["eb3"], f["sb3"][None]], axis=0)),
             bT=c(np.concatenate([f["sb1"].reshape(2, P), f["sb2"].reshape(1, P), f["eb1"]], axis=0).T),
             bE2=c(f["eb2"].T))
    return a


def kernel(**inputs):
    import numpy as np
    import concourse.bacc as bacc
    from concourse.bass_utils import run_bass_kernel_spmd
    nc = bacc.Bacc("TRN2", target_bir_lowering=False, num_devices=1)
    arrays = {f"in_{k}": v for k, v in layout(inputs).items()}
    A = {k[3:]: nc.dram_tensor(k, v.shape, mybir.dt.from_np(v.dtype), kind="ExternalInput").ap()
         for k, v in arrays.items()}
    out = nc.dram_tensor("out", (NODES, D), F32, kind="ExternalOutput").ap()
    build(nc, A, out)
    return run_bass_kernel_spmd(nc, [arrays], core_ids=[0]).results[0]["out"]
```

```python
import concourse.bass as bass
from concourse import mybir
from contextlib import ExitStack

F32 = mybir.dt.float32
I32 = mybir.dt.int32
U32 = mybir.dt.uint32
BF16 = mybir.dt.bfloat16
ALU = mybir.AluOpType
ACT = mybir.ActivationFunctionType
AX = mybir.AxisListType

P = 128
NODES, D = 3125, 256
NODE_TILES = -(-NODES // P)
NODES_PAD = NODE_TILES * P
LAST_ROWS = NODES - (NODE_TILES - 1) * P
PAD_NODE = NODES_PAD - 1
EDGES = 50000
EDGE_CHUNKS = 4
EDGE_ROWS = 98
EDGE_TILES = EDGE_CHUNKS * EDGE_ROWS
GROUP = 5
GROUPS = 84
STEPS = GROUP * GROUPS
HEADS, HD = 8, 32
E0, HID = 8, 1024
SLOT_TILES = 56
SLOTS = SLOT_TILES * P
SLOT_ROWS = SLOTS + P
BIG = 1e30
T5 = NODE_TILES // 5


class Own:

    def __init__(self, eng, sem):
        self.eng, self.sem = eng, sem
        self.total = 0
        self.i = None

    def __call__(self, ins):
        ins.then_inc(self.sem, 1)
        self.total += 1
        return ins

    def wait(self):
        if self.i is None:
            self.eng.wait_ge(self.sem, self.total)
        else:
            self.eng.wait_ge(self.sem, self.i * self.per + (self.total - self.first * self.per))

    def loop(self, i, per, first=0):
        self.i, self.per, self.first, self.at = i, per, first, self.total

    def end(self, last):
        assert self.total - self.at == self.per, (self.total - self.at, self.per)
        self.total += (last - self.first - 1) * self.per
        self.i = None


class State:
    pass


class Phase:

    numbers = set()
    lasting = None

    def __init__(self, nc, tag):
        self.nc, self.tag, self.ctx, self.sems = nc, tag, ExitStack(), {}

    def __enter__(self):
        self.ctx.__enter__()
        return self

    def __exit__(self, *a):
        return self.ctx.__exit__(*a)

    def sb(self, name, shape, dt=F32):
        return self.ctx.enter_context(self.nc.sbuf_tensor(f"{self.tag}_{name}", shape, dt))

    def sem(self, name):
        sem = self.ctx.enter_context(self.nc.semaphore(f"{self.tag}_{name}"))
        self.numbers.add(sem.num)
        return sem

    def __getitem__(self, name):
        if name not in self.sems:
            self.sems[name] = self.sem(name)
        return self.sems[name]

    def for_gathers(self, *names):
        for name in names:
            self.sems[name] = self.lasting.enter_context(self.nc.semaphore(f"{self.tag}_{name}"))

    def block(self):
        return self.ctx.enter_context(self.nc.Block())


def bcast(vec):
    return vec.partition_broadcast(P)


def layernorm_stats(nc, dve, own, src, stats, mv, rstd, eps_done, sqrt_done, eps=1e-5):
    for t in range(NODE_TILES):
        own(nc.vector.bn_stats(stats[:, t, :], src[:, t, :]))
    own.wait()
    for t in range(NODE_TILES):
        own(nc.vector.bn_aggr(mv[:, t, :], stats[:, t, :]))
    own.wait()
    nc.vector.tensor_scalar_add(rstd[:, :], mv[:, :, 1], eps).then_inc(eps_done, 1)
    dve.wait_ge(sqrt_done, 1)
    own(nc.vector.reciprocal(rstd[:, :], rstd[:, :]))
    own.wait()


def prepare_edges(nc, S, A):
    with Phase(nc, "prepare_edges") as ph:
        srcI = ph.sb("src_rows_i", [EDGE_ROWS, EDGE_CHUNKS, P], I32)
        dstI = ph.sb("dst_rows_i", [EDGE_ROWS, EDGE_CHUNKS, P], I32)
        startI = ph.sb("dst_before_tile_i", [EDGE_ROWS, EDGE_CHUNKS], I32)
        blkI = ph.sb("block_i", [EDGE_ROWS, 2, EDGE_CHUNKS], I32)
        srcF = ph.sb("src_rows", [EDGE_ROWS, EDGE_CHUNKS, P])
        dstF = ph.sb("dst_rows", [EDGE_ROWS, EDGE_CHUNKS, P])
        first = ph.sb("first_step", [EDGE_ROWS, 2, EDGE_CHUNKS])
        tile_no = ph.sb("tile_no", [EDGE_ROWS, 2, EDGE_CHUNKS])
        step_row = ph.sb("step_row", [P, STEPS])
        step_col = ph.sb("step_col", [GROUPS, GROUP])
        reached = ph.sb("reached", [EDGE_ROWS, EDGE_CHUNKS, STEPS])
        pick = ph.sb("pick", [EDGE_ROWS, EDGE_CHUNKS, STEPS])
        blk = ph.sb("block_of_step", [P, STEPS])
        blkT = ph.sb("block_of_step_col", [GROUPS, GROUP])
        relR = ph.sb("rel_rows_sb", [GROUPS, GROUP, P])
        keyR = ph.sb("key_rows_sb", [GROUPS, GROUP, P])
        tmpR = ph.sb("tmp_rows", [GROUPS, GROUP, P])
        edge = ph.sb("key_ends", [1, 2])
        keyS = ph.sb("key_scan", [GROUPS, 3, GROUP * P])
        zero = ph.sb("zeros", [P, D])
        loaded, made, own_s, got, rows_out, ends_out, keys_in, zs = (ph.sem(n) for n in (
            "edge_loads", "pool_made", "dve_own", "pe_done", "rows_out", "ends_out", "keys_in", "zero_out"))
        block = ph.block()

        @block.vector
        def _(dve):
            v, own = nc.vector, Own(dve, own_s)
            dve.wait_ge(loaded, 48)
            dve.wait_ge(made, 6)
            own(v.tensor_copy(srcF[:, :, :], srcI[:, :, :]))
            own(v.tensor_copy(dstF[:, :, :], dstI[:, :, :]))
            own(v.tensor_scalar(blkI[:, 0, :], startI[:, :], 7, None, ALU.arith_shift_right))
            own(v.tensor_scalar(blkI[:, 1, :], dstI[:, :, P - 1], 7, None, ALU.arith_shift_right))
            own.wait()
            own(v.tensor_copy(first[:, :, :], blkI[:, :, :]))
            own.wait()
            own(v.tensor_tensor(first[:, :, :], first[:, :, :], tile_no[:, :, :], ALU.add))
            own.wait()
            for c in range(EDGE_CHUNKS):
                own(v.tensor_scalar(reached[:, c, :], step_row[0:EDGE_ROWS, :], first[:, 0, c:c + 1], None, ALU.is_ge))
            own.wait()
            for c in range(EDGE_CHUNKS):
                own(v.scalar_tensor_tensor(pick[:, c, :], step_row[0:EDGE_ROWS, :], first[:, 1, c:c + 1],
                                           reached[:, c, :], ALU.is_lt, ALU.mult))
            own.wait()
            S.picked = own.total
            dve.wait_ge(got, 1)
            own(v.tensor_copy(S.srcX[:, :], S.ps[:, 0, 0:STEPS]))
            own(v.scalar_tensor_tensor(blk[:, :], step_row[:, :], 1.0, S.ps[:, 2, 0:STEPS], ALU.add, ALU.subtract))
            own(v.scalar_tensor_tensor(blkT[:, :], step_col[:, :], 1.0, S.ps[0:GROUPS, 5, 0:GROUP], ALU.add,
                                       ALU.subtract))
            own.wait()
            own(v.tensor_scalar_min(blk[:, :], blk[:, :], float(NODE_TILES - 1)))
            own(v.tensor_scalar_min(blkT[:, :], blkT[:, :], float(NODE_TILES - 1)))
            own.wait()
            own(v.tensor_copy(S.blockI[:, :, 0:GROUP], blk[0:1, :].rearrange("p (k j) -> p k j", j=GROUP)))
            own(v.scalar_tensor_tensor(S.relX[:, :], blk[:, :], -float(P), S.ps[:, 1, 0:STEPS], ALU.mult, ALU.add))
            for k in range(GROUP):
                src = S.ps[0:GROUPS, 3 + k // 4, (k % 4) * P:(k % 4 + 1) * P]
                own(v.tensor_scalar(blkT[:, k:k + 1], blkT[:, k:k + 1], -float(P), None, ALU.mult))
                own.wait()
                own(v.tensor_scalar(relR[:, k, :], src, blkT[:, k:k + 1], None, ALU.add))
            own.wait()
            own(v.tensor_scalar(S.validX[:, :], S.relX[:, :], 0.0, None, ALU.is_ge))
            own(v.tensor_scalar(keyR[:, :, :], relR[:, :, :], 0.0, None, ALU.is_ge))
            own.wait()
            own(v.scalar_tensor_tensor(S.validX[:, :], S.relX[:, :], float(P - 1), S.validX[:, :], ALU.is_le, ALU.mult))
            own(v.scalar_tensor_tensor(keyR[:, :, :], relR[:, :, :], float(P - 1), keyR[:, :, :], ALU.is_le, ALU.mult))
            own.wait()
            own(v.tensor_scalar(S.penX[:, :], S.validX[:, :], BIG, -BIG, ALU.mult, ALU.add))
            own(v.scalar_tensor_tensor(tmpR[:, :, :], relR[:, :, :], 1.0, keyR[:, :, :], ALU.add, ALU.mult))
            own.wait()
            own(v.tensor_scalar(keyR[:, :, :], tmpR[:, :, :], -1.0, None, ALU.add))
            S.rows_ready = own.total
            dve.wait_ge(keys_in, 48)
            for n, o in ((0, 0), (1, 2)):
                own(v.tensor_tensor(S.cut[:, n, :], keyS[:, 1, :], keyS[:, o, :], ALU.not_equal))
            own.wait()
            own(v.tensor_scalar(S.cut[:, :, :], S.cut[:, :, :], -BIG, None, ALU.mult))
            own.wait()
            for n in range(2):
                own(v.tensor_reduce(S.row_cut[:, n:n + 1], S.cut[:, n, :], AX.X, ALU.min))
            own.wait()

        @block.sync
        def _(sp):
            sp.dma_start(srcI[:, :, :], A["src"].rearrange("(c p) e -> p c e", p=EDGE_ROWS)).then_inc(loaded, 16)
            sp.dma_start(dstI[:, :, :], A["dst"].rearrange("(c p) e -> p c e", p=EDGE_ROWS)).then_inc(loaded, 16)
            sp.dma_start(startI[:, :], A["dst_before"]).then_inc(loaded, 16)
            sp.dma_start(S.X[:, :, :], A["x"].rearrange("(t p) d -> p t d", p=P)).then_inc(ph["x_loaded"], 16)
            sp.wait_ge(own_s, S.rows_ready)
            sp.dma_start(S.rel_dram.rearrange("(k p) e -> p k e", p=GROUPS), relR[:, :, :]).then_inc(rows_out, 16)
            key_rows = S.key_dram[1:1 + STEPS * P].rearrange("(k p e) -> p k e", p=GROUPS, e=P)
            sp.dma_start(key_rows, keyR[:, :, :]).then_inc(rows_out, 16)
            sp.wait_ge(made, 6)
            sp.dma_start(S.key_dram[0:1].rearrange("(a b) -> a b", a=1), edge[0:1, 0:1]).then_inc(ends_out, 16)
            sp.dma_start(S.key_dram[1 + STEPS * P:2 + STEPS * P].rearrange("(a b) -> a b", a=1),
                         edge[0:1, 1:2]).then_inc(ends_out, 16)
            sp.wait_ge(rows_out, 32)
            sp.wait_ge(ends_out, 32)
            for o in range(3):
                sp.dma_start(keyS[:, o, :], S.key_dram[o:o + STEPS * P].rearrange("(p e) -> p e", p=GROUPS)
                             ).then_inc(keys_in, 16)
            sp.wait_ge(zs, 16)
            sp.wait_ge(ph["x_loaded"], 16)

        @block.scalar
        def _(act):
            act.wait_ge(made, 6)
            act.dma_start(S.y_dram[SLOTS:SLOT_ROWS, :], zero[:, :]).then_inc(zs, 16)

        @block.gpsimd
        def _(pool):
            g = nc.gpsimd
            g.memset(S.ident[:, :], 0.0).then_inc(made, 1)
            pool.wait_ge(made, 1)
            g.affine_select(out=S.ident[:, :], in_=S.ident[:, :], compare_op=ALU.not_equal, fill=1.0, base=0,
                            pattern=[[-1, P]], channel_multiplier=1).then_inc(made, 1)
            g.iota(S.iota_row[:, :], [[1, P]], base=0, channel_multiplier=0, allow_small_or_imprecise_dtypes=True)
            g.iota(S.iota_col[:, :], [[0, 1]], base=0, channel_multiplier=1, allow_small_or_imprecise_dtypes=True)
            g.iota(step_row[:, :], [[1, STEPS]], base=0, channel_multiplier=0, allow_small_or_imprecise_dtypes=True)
            g.iota(step_col[:, :], [[GROUPS, GROUP]], base=0, channel_multiplier=1,
                   allow_small_or_imprecise_dtypes=True)
            g.iota(tile_no[:, :, :], [[1, 2], [EDGE_ROWS, EDGE_CHUNKS]], base=0, channel_multiplier=1,
                   allow_small_or_imprecise_dtypes=True).then_inc(made, 1)
            g.memset(edge[:, :], -2.0).then_inc(made, 1)
            g.memset(zero[:, :], 0.0).then_inc(made, 1)
            g.memset(S.ones[:, :], 1.0).then_inc(made, 1)

        @block.tensor
        def _(pe):
            t = nc.tensor
            pe.wait_ge(own_s, S.picked)
            for c in range(EDGE_CHUNKS):
                st, sp = c == 0, c == EDGE_CHUNKS - 1
                t.matmul(S.ps[:, 0, 0:STEPS], srcF[:, c, :], pick[:, c, :], start=st, stop=sp)
                t.matmul(S.ps[:, 1, 0:STEPS], dstF[:, c, :], pick[:, c, :], start=st, stop=sp)
                t.matmul(S.ps[:, 2, 0:STEPS], S.ones[0:EDGE_ROWS, :], reached[:, c, :], start=st, stop=sp)
            for k in range(GROUP):
                for c in range(EDGE_CHUNKS):
                    st, sp = c == 0, c == EDGE_CHUNKS - 1
                    t.matmul(S.ps[0:GROUPS, 3 + k // 4, (k % 4) * P:(k % 4 + 1) * P],
                             pick[:, c, k * GROUPS:(k + 1) * GROUPS], dstF[:, c, :], start=st, stop=sp)
                for c in range(EDGE_CHUNKS):
                    st, sp = c == 0, c == EDGE_CHUNKS - 1
                    last = t.matmul(S.ps[0:GROUPS, 5, k:k + 1], reached[:, c, k * GROUPS:(k + 1) * GROUPS],
                                    S.ones[0:EDGE_ROWS, 0:1], start=st, stop=sp)
            last.then_inc(got, 1)


RING = 5


def tiles(eng):
    with eng.Fori(0, T5) as i:
        for j in range(RING):
            yield i, i * RING + j, j, i * RING + (j + 1)


def skewed(eng, *stages):
    def steps(i, js, runs):
        for j in js:
            for q, stage in enumerate(stages):
                if runs(j, q):
                    i2, j2 = i + (j - q) // RING, (j - q) % RING
                    stage(i2, i2 * RING + j2, j2, i2 * RING + (j2 + 1))
    steps(0, range(RING), lambda j, q: j >= q)
    with eng.Fori(1, T5) as i:
        steps(i, range(RING), lambda j, q: True)
    steps(T5, range(len(stages) - 1), lambda j, q: j < q)


def nothing(*tile):
    pass


def after(eng, sem, n):
    eng.wait_ge(sem, n + RING)


def again(eng, sem, n):
    eng.wait_ge(sem, n)


def bank_again(eng, sem, j, n):
    eng.wait_ge(sem, n + RING - (1 if j == 0 else 2))


def norm_five(nc, ph, dve, src, mv, rstd, ring, i):
    for j in range(RING):
        t, n = i * RING + j, i * RING + (j + 1)
        again(dve, ph["xT_psum"], n)
        again(dve, ph["xn_kept"], n)
        nc.vector.tensor_scalar(ring[:, j, :], src[:, bass.ds(t, 1), :].squeeze(1), mv[:, bass.ds(t, 1), 0],
                                rstd[:, bass.ds(t, 1)], ALU.subtract, ALU.mult).then_inc(ph["xn_ready"], 1)


def norm_tile(nc, ph, dve, src, mv, rstd, ring):
    def stage(i, t, j, n):
        again(dve, ph["xT_psum"], n)
        again(dve, ph["xn_kept"], n)
        nc.vector.tensor_scalar(ring[:, j, :], src[:, bass.ds(t, 1), :].squeeze(1), mv[:, bass.ds(t, 1), 0],
                                rstd[:, bass.ds(t, 1)], ALU.subtract, ALU.mult).then_inc(ph["xn_ready"], 1)
    return stage


def keep_tiles(nc, ph, pool, ring, dst):
    pool.sem_inc(ph["xn_kept"], RING)
    for i, t, j, n in tiles(pool):
        after(pool, ph["xn_ready"], n)
        nc.gpsimd.tensor_copy(dst[:, bass.ds(t, 1), :], ring[:, j:j + 1, :]).then_inc(ph["xn_kept"], 1)


def copy_transposed(nc, ph, act, j, n, bank, xT, name="xT"):
    after(act, ph[name + "_psum"], n)
    nc.scalar.activation(xT[:, j, :, :], ph.ps[:, bank, 0:D].rearrange("p (c n) -> p c n", c=2),
                         ACT.Copy).then_inc(ph[name + "_ready"], 1)


def transpose_tile(nc, ph, pe, src, j, bank, ident, name="xT"):
    for c in range(2):
        last = nc.tensor.transpose(ph.ps[:, bank, c * P:(c + 1) * P], src[:, j, c * P:(c + 1) * P], ident[:, :])
    last.then_inc(ph[name + "_psum"], 1)


def project_layer0(nc, S, A):
    with Phase(nc, "project_layer0") as ph:
        ph.ps = S.ps
        W = ph.sb("w_proj", [P, 2, 4 * D])
        bv = ph.sb("bv_rows", [P, D])
        wqk = ph.sb("wqk_rows", [P, 2, D])
        bqk = ph.sb("bqk_rows", [P, 2])
        stats = ph.sb("ln_stats", [P, NODE_TILES, 6])
        mv = ph.sb("ln_mean_var", [P, NODE_TILES, 2])
        rstd = ph.sb("ln_rstd", [P, NODE_TILES])
        xn = ph.sb("xn_ring", [P, RING, D])
        xT = ph.sb("xn_T", [P, RING, 2, P])
        hrow = ph.sb("h_rows", [P, RING, D + 1])
        prod = ph.sb("h_times_w", [P, RING, 2, D])
        qk5 = ph.sb("q_k_of_five", [P, 2, RING])
        neg = ph.sb("neg_part", [P, RING, 2, D])
        kf = ph.sb("k_feature", [P, RING, D])
        vf = ph.sb("v_feature", [P, RING, 2, P + 1])
        mask4 = ph.sb("head_mask", [P, 4])
        kvs = ph.sb("kv_raw", [P, 2, P + 1])
        hq_bank = lambda j: j % 2
        kv_bank = lambda j: 2 + j % 2
        block = ph.block()

        @block.sync
        def _(sp):
            sp.dma_start(W[:, :, 0:D], A["Wv"].rearrange("(c p) n -> p c n", p=P)).then_inc(ph["weights_in"], 16)
            sp.dma_start(W[:, :, D:4 * D], A["WqkvT"].rearrange("(c p) n -> p c n", p=P)
                         ).then_inc(ph["weights_in"], 16)
            for dst, src in ((bv[:, :], "bv"), (wqk[:, 0, :], "wq"), (wqk[:, 1, :], "wk"), (bqk[:, 0:1], "bq"),
                             (bqk[:, 1:2], "bk")):
                sp.dma_start(dst, bcast(A[src])).then_inc(ph["rows_in"], 16)
            with sp.Fori(0, T5) as i:
                sp.wait_ge(ph["h_done"], i + 1)
                sp.dma_start(S.htab_dram[bass.ds(i * (RING * P), RING * P), :].rearrange("(t p) d -> p t d", p=P),
                             hrow[:, :, :]).then_inc(ph["h_table_out"], 16)
            sp.wait_ge(ph["h_table_out"], 16 * T5 + 16)

        @block.gpsimd
        def _(pool):
            g, made = nc.gpsimd, ph["pool_made"]
            g.memset(vf[:, :, :, P:P + 1], 1.0).then_inc(made, 1)
            g.memset(mask4[:, :], 1.0).then_inc(made, 1)
            pool.wait_ge(made, 2)
            g.affine_select(out=mask4[:, :], in_=mask4[:, :], compare_op=ALU.is_ge, fill=0.0, base=0,
                            pattern=[[-HD, 4]], channel_multiplier=1).then_inc(made, 1)
            pool.wait_ge(made, 3)
            g.affine_select(out=mask4[:, :], in_=mask4[:, :], compare_op=ALU.is_ge, fill=0.0, base=HD - 1,
                            pattern=[[HD, 4]], channel_multiplier=-1).then_inc(made, 1)
            pool.wait_ge(made, 4)
            g.tensor_copy(S.head_blocks[:, :].rearrange("p (h m) -> p h m", m=HD),
                          mask4[:, :].unsqueeze(2).broadcast_to([P, 4, HD])).then_inc(made, 1)
            keep_tiles(nc, ph, pool, xn, S.XN)

        @block.vector
        def _(dve):
            v, own = nc.vector, Own(dve, ph["dve_own"])
            layernorm_stats(nc, dve, own, S.X, stats, mv, rstd, ph["eps_done"], ph["sqrt_done"])
            dve.wait_ge(ph["rows_in"], 80)

            dve.sem_inc(ph["h_table_out"], 16)
            for name in ("xn_ready", "h_biased", "q_feature", "k_feature", "qk_dots"):
                dve.sem_inc(ph[name], RING)

            def features(i, t, j, n):
                if j == 0:
                    dve.wait_ge(ph["h_table_out"], i * 16 + 16)
                after(dve, ph["q_exp"], n)
                v.tensor_tensor(hrow[:, j, 0:D], S.ps[:, hq_bank(j), 0:D], bv[:, :], ALU.add
                                ).then_inc(ph["h_biased"], 1)
                v.scalar_tensor_tensor(S.QF[:, bass.ds(t, 1), :], S.ps[:, hq_bank(j):hq_bank(j) + 1, D:2 * D], 0.0,
                                       neg[:, j:j + 1, 0, :], ALU.max, ALU.add).then_inc(ph["q_feature"], 1)
                after(dve, ph["k_exp"], n)
                again(dve, ph["kv_used"], n)
                v.scalar_tensor_tensor(kf[:, j, :], S.ps[:, kv_bank(j), 0:D], 0.0, neg[:, j, 1, :], ALU.max,
                                       ALU.add).then_inc(ph["k_feature"], 1)
                after(dve, ph["h_biased"], n)
                for m in range(2):
                    ins = v.tensor_tensor_reduce(out=prod[:, j, m, :], in0=hrow[:, j, 0:D], in1=wqk[:, m, :],
                                                 scale=1.0, scalar=0.0, op0=ALU.mult, op1=ALU.add,
                                                 accum_out=qk5[:, m, j:j + 1])
                ins.then_inc(ph["qk_dots"], 1)
                if j == RING - 1:
                    after(dve, ph["qk_dots"], n)
                    v.tensor_copy(S.qk[:, :, bass.ds(i * RING, RING)], qk5[:, :, :])
                    v.tensor_scalar(hrow[:, :, D], qk5[:, 0, :], bqk[:, 0:1], None, ALU.add
                                    ).then_inc(ph["h_done"], 1)

            skewed(dve, norm_tile(nc, ph, dve, S.X, mv, rstd, xn), nothing, features)
            dve.wait_ge(ph["h_done"], T5)
            own(v.tensor_scalar(S.qk[:, 1, :], S.qk[:, 1, :], bqk[:, 1:2], None, ALU.add))
            after(dve, ph["kv_used"], NODE_TILES)
            dve.wait_ge(ph["pool_made"], 5)
            own(v.tensor_copy(kvs[:, :, :], S.ps[:, 6:8, 0:P + 1]))
            own.wait()
            for c in range(2):
                own(v.tensor_tensor(S.kvbd[:, c, 0:P], kvs[:, c, 0:P], S.head_blocks[:, :], ALU.mult))
                own(v.tensor_scalar(S.kvbd[:, c, P:P + 4], mask4[:, :], kvs[:, c, P:P + 1], None, ALU.mult))
            own.wait()

        @block.scalar
        def _(act):
            a = nc.scalar
            act.wait_ge(ph["eps_done"], 1)
            a.activation(rstd[:, :], rstd[:, :], ACT.Sqrt).then_inc(ph["sqrt_done"], 1)
            for name in ("xT_ready", "q_neg", "q_exp", "k_neg", "k_exp", "v_feature"):
                act.sem_inc(ph[name], RING)
            act.wait_ge(ph["pool_made"], 1)

            def copy(i, t, j, n):
                again(act, ph["kv_psum"], n)
                copy_transposed(nc, ph, act, j, n, 4 + j % 2, xT)

            def features(i, t, j, n):
                for m, (psum, neg_s, exp_s, used, bank, off) in enumerate((
                        ("hq_psum", "q_neg", "q_exp", "q_feature", hq_bank(j), D),
                        ("kv_psum", "k_neg", "k_exp", "k_feature", kv_bank(j), 0))):
                    after(act, ph[psum], n)
                    again(act, ph[used], n)
                    a.activation(neg[:, j, m, :], S.ps[:, bank, off:off + D], ACT.Relu, scale=-1.0
                                 ).then_inc(ph[neg_s], 1)
                    if m == 1:
                        again(act, ph["kv_used"], n)
                        a.activation(vf[:, j, :, 0:P], S.ps[:, bank, D:2 * D].rearrange("p (c n) -> p c n", c=2),
                                     ACT.Copy).then_inc(ph["v_feature"], 1)
                        after(act, ph["v_feature"], n)
                    after(act, ph[neg_s], n)
                    a.activation(neg[:, j, m, :], neg[:, j, m, :], ACT.Exp, scale=-1.0).then_inc(ph[exp_s], 1)

            skewed(act, copy, features)

        @block.tensor
        def _(pe):
            t_ = nc.tensor
            pe.wait_ge(ph["weights_in"], 32)
            for name in ("xT_psum", "hq_psum", "kv_psum", "kv_used"):
                pe.sem_inc(ph[name], RING)

            def transposes(i, t, j, n):
                after(pe, ph["xn_ready"], n)
                bank_again(pe, ph["xT_ready"], j, n)
                transpose_tile(nc, ph, pe, xn, j, 4 + j % 2, S.ident)

            def products(i, t, j, n):
                after(pe, ph["xT_ready"], n)
                for half, (psum, bank) in enumerate((("hq_psum", hq_bank(j)), ("kv_psum", kv_bank(j)))):
                    for used in (("h_biased", "q_feature") if half == 0 else ("k_feature", "v_feature")):
                        bank_again(pe, ph[used], j, n)
                    for c in range(2):
                        ins = t_.matmul(S.ps[:, bank, :], xT[:, j, c, :], W[:, c, half * 512:(half + 1) * 512],
                                        start=c == 0, stop=c == 1)
                    ins.then_inc(ph[psum], 1)

            def sums(i, t, j, n):
                first, last = ((t == 0, t == NODE_TILES - 1) if isinstance(t, int) else (False, False))
                after(pe, ph["k_feature"], n)
                after(pe, ph["v_feature"], n)
                rows = LAST_ROWS if last else P
                for c in range(2):
                    ins = t_.matmul(S.ps[:, 6 + c, 0:P + 1], kf[0:rows, j, c * P:(c + 1) * P],
                                    vf[0:rows, j, c, :], start=first, stop=last)
                ins.then_inc(ph["kv_used"], 1)

            skewed(pe, transposes, products, nothing, sums)


AHEAD = 2
AGG_LANES = 4
ON_ACT = 3
MIX_LANES = 5


def group_at(i, h, lanes):
    i, h = i + h // lanes, h % lanes
    return i, h, i * lanes + h, i * lanes + (h + 1)


def groups(eng, lanes):
    for i, h, k, n, later in groups_ahead(eng, 0, lanes):
        yield i, h, k, n


def groups_ahead(eng, ahead, lanes):
    loops = GROUPS // lanes - (ahead > GROUPS % lanes)
    with eng.Fori(0, loops) as i:
        for h in range(lanes):
            yield *group_at(i, h, lanes), group_at(i, h + ahead, lanes)
    for h in range(GROUPS - loops * lanes):
        yield (*group_at(loops, h, lanes),
               group_at(loops, h + ahead, lanes) if loops * lanes + h + ahead < GROUPS else None)


def dst_blocks(eng, S, k):
    S.loads += 1
    regs = [eng.alloc_register(f"dst_block{j}_{S.loads}") for j in range(GROUP)]
    eng.load(regs, S.blockI[0:1, bass.ds(k, 1), 0:GROUP].squeeze(1))
    return [bass.RuntimeValue.of_register_unchecked(r).with_bounds(min_val=0, max_val=NODE_TILES - 1) for r in regs]


def gather_edges(nc, S, ph, block, table, idx, got, relB, lanes, items, before=None):
    ph.for_gathers(*[f"gathered{h}" for h in range(lanes)])

    @block.gpsimd
    def _(pool):
        def indices(i, h, k, n):
            pool.wait_ge(ph["rows_used"], n)
            nc.gpsimd.tensor_copy(idx[:, h, :], S.srcX[:, bass.ds(k * GROUP, GROUP)]).then_inc(ph["idx_ready"], 1)

        indices(0, 0, 0, 1)
        for i, h, k, n, later in groups_ahead(pool, 1, lanes):
            if later:
                indices(*later)
            pool.wait_ge(ph[f"kept{h}"], i * 16 + 16)
            pool.wait_ge(ph["idx_ready"], n)
            pool.sem_inc(ph["gather_gate"], 1)
            for j in range(GROUP):
                nc.gpsimd.indirect_dma_start(got[:, h, j, :], None, table,
                                             bass.IndirectOffsetOnAxis(ap=idx[:, h, j:j + 1], axis=0)
                                             ).then_inc(ph[f"gathered{h}"], 16)

    @block.sync
    def _(sp):
        if before:
            before(sp)
        for i, h, k, n in groups(sp, lanes):
            sp.wait_ge(ph["hot_ready"], n)
            sp.dma_start(relB[:, h, :], S.rel_dram[bass.ds(k * GROUP, GROUP), :].rearrange("g e -> (g e)")
                         .partition_broadcast(P)).then_inc(ph[f"rel_in{h}"], 16)

    @block.scalar
    def _(act):
        for h in range(lanes):
            act.sem_inc(ph[f"kept{h}"], 16)
        for i, h, k, n in items(act):
            act.wait_ge(ph[f"gathered{h}"], i * (16 * GROUP) + 16 * GROUP)
            act.dma_start(S.step_dram[bass.ds(k, 1), :, :].rearrange("a p (g d) -> (a p) g d", d=D),
                          got[:, h, :, 0:D]).then_inc(ph[f"kept{h}"], 16)
        for h in range(lanes):
            act.wait_ge(ph[f"kept{h}"], 16 * ((GROUPS - 1 - h) // lanes + 1) + 16)


def onehot_T(nc, S, ph, dve, hot, relB, i, h, n):
    dve.wait_ge(ph[f"rel_in{h}"], i * 16 + 16)
    dve.wait_ge(ph["dst_psum"], n)
    nc.vector.tensor_scalar(hot[:, h, :], relB[:, h, :], S.iota_col[:, 0:1], None, ALU.is_equal
                            ).then_inc(ph["hot_ready"], 1)


def score_and_mix_layer0(nc, S, A):
    lanes = MIX_LANES
    with Phase(nc, "score_mix") as ph:
        ph.ps = S.ps
        idx = ph.sb("gather_idx", [P, lanes, GROUP], I32)
        got = ph.sb("h_of_sources", [P, lanes, GROUP, D + 1])
        relB = ph.sb("rel_bcast", [P, lanes, GROUP * P])
        hot = ph.sb("dst_onehot_T", [P, lanes, GROUP * P])
        qr = ph.sb("q_ring", [P, RING, D])
        qT = ph.sb("q_T", [P, RING, 2, P])
        z = ph.sb("inv_den", [P, RING, 2, 4])
        tt = ph.sb("attended", [P, RING, 2, P])
        W1 = ph.sb("w1", [P, 2, D])
        W2 = ph.sb("w2", [P, 2, D])
        b1 = ph.sb("b1", [P, 2])
        rows = ph.sb("ln1_g_b_b2", [P, 3, D])
        stats, mv, rstd = ln_scratch(ph)
        x1, xT, hT = qr, qT, tt
        xs = ph.sb("x1_scaled", [P, RING, D])
        edge_k = lambda h: S.ps[:, 2 + h % 2, 0:GROUP]
        block = ph.block()

        def paced(eng, attend, between, mlp, behind=lambda: None):
            with eng.Fori(0, T5) as i:
                for j in range(RING):
                    attend(i, i * RING + j, j, i * RING + (j + 1))
                    yield group_at(i, j, lanes)
            between()
            with eng.Fori(0, T5) as i:
                for j in range(RING):
                    mlp(i, i * RING + j, j, i * RING + (j + 1))
                    yield group_at(i * 2 + T5, 2 * j, lanes)
                    yield group_at(i * 2 + T5, 2 * j + 1, lanes)
            behind()
            for h in range(GROUPS - 3 * NODE_TILES):
                yield group_at(3 * T5, h, lanes)

        def act_items(act):
            def attend(i, t, j, n):
                again(act, ph["qT_psum"], n)
                nc.scalar.activation(qr[:, j:j + 1, :], S.QF[:, bass.ds(t, 1), :], ACT.Copy
                                     ).then_inc(ph["q_staged"], 1)
                again(act, ph["num_psum"], n)
                copy_transposed(nc, ph, act, j, n, 4 + j % 2, qT, "qT")

            def between():
                ln_root(nc, ph, act, rstd)
                act.sem_inc(ph["xT_ready"], RING)
                act.sem_inc(ph["hidden"], RING)
                act.wait_ge(ph["weights_in"], 96)

            def mlp(i, t, j, n):
                again(act, ph["h_psum"], n)
                copy_transposed(nc, ph, act, j, n, 4 + j % 2, xT)
                after(act, ph["h_psum"], n)
                again(act, ph["y_psum"], n)
                for m in range(2):
                    ins = nc.scalar.activation(hT[:, j, m, :], S.ps[:, j % 2, m * P:(m + 1) * P], ACT.Gelu,
                                               bias=b1[:, m:m + 1])
                ins.then_inc(ph["hidden"], 1)

            def behind():
                act.wait_ge(ph["eps_done2"], 1)
                nc.scalar.activation(S.ln2_rstd[:, :], S.ln2_rstd[:, :], ACT.Sqrt).then_inc(ph["sqrt_done2"], 1)

            act.sem_inc(ph["qT_ready"], RING)
            act.sem_inc(ph["q_staged"], RING)
            yield from paced(act, attend, between, mlp, behind)

        def weights(sp):
            for dst, src in ((W1, "mW1T"), (W2, "mW2T")):
                sp.dma_start(dst[:, :, :], A[src].rearrange("(c p) n -> p c n", p=P)).then_inc(ph["weights_in"], 16)
            sp.dma_start(b1[:, :], A["mb1"]).then_inc(ph["weights_in"], 16)
            for m, src in enumerate(("ln1_g", "ln1_b", "mb2")):
                sp.dma_start(rows[:, m, :], bcast(A[src])).then_inc(ph["weights_in"], 16)

        gather_edges(nc, S, ph, block, S.htab_dram, idx, got, relB, lanes, act_items, weights)

        @block.vector
        def _(dve):
            v, own = nc.vector, Own(dve, ph["dve_own"])

            def attend(i, t, j, n):
                both = S.ps[:, j % 2, 0:2 * (P + 4)].rearrange("p (c n) -> p c n", c=2)
                after(dve, ph["num_psum"], n)
                v.tensor_scalar_add(z[:, j, :, :], both[:, :, P:P + 4], 1e-6).then_inc(ph["den_eps"], 1)
                after(dve, ph["den_eps"], n)
                v.reciprocal(z[:, j, :, :], z[:, j, :, :]).then_inc(ph["den_inv"], 1)
                after(dve, ph["den_inv"], n)
                for c in range(2):
                    ins = v.tensor_tensor(tt[:, j, c, :].rearrange("p (h m) -> p h m", h=4),
                                          both[:, c, 0:P].rearrange("p (h m) -> p h m", h=4),
                                          z[:, j, c, :].unsqueeze(2).broadcast_to([P, 4, HD]), ALU.mult)
                ins.then_inc(ph["attended"], 1)
                after(dve, ph["attended"], n)
                v.tensor_tensor(S.QF[:, bass.ds(t, 1), :], tt[:, j:j + 1, :, :].rearrange("p a c n -> p a (c n)"),
                                S.XN[:, bass.ds(t, 1), :], ALU.add).then_inc(ph["residual"], 1)

            def between():
                dve.wait_ge(ph["residual"], NODE_TILES)
                layernorm_stats(nc, dve, own, S.QF, stats, mv, rstd, ph["eps_done"], ph["sqrt_done"])
                dve.wait_ge(ph["weights_in"], 96)
                for name in ("xn_ready", "x1_scaled", "y_biased", "y_done"):
                    dve.sem_inc(ph[name], RING)

            def mlp(i, t, j, n):
                if j == 0:
                    for jj in range(RING):
                        tt, nn = i * RING + jj, i * RING + (jj + 1)
                        again(dve, ph["xT_psum"], nn)
                        v.scalar_tensor_tensor(xs[:, jj, :], S.QF[:, bass.ds(tt, 1), :].squeeze(1),
                                               mv[:, bass.ds(tt, 1), 0], rows[:, 0, :], ALU.subtract, ALU.mult
                                               ).then_inc(ph["x1_scaled"], 1)
                    for jj in range(RING):
                        tt, nn = i * RING + jj, i * RING + (jj + 1)
                        after(dve, ph["x1_scaled"], nn)
                        v.scalar_tensor_tensor(x1[:, jj, :], xs[:, jj, :], rstd[:, bass.ds(tt, 1)], rows[:, 1, :],
                                               ALU.mult, ALU.add).then_inc(ph["xn_ready"], 1)
                after(dve, ph["y_psum"], n)
                v.tensor_tensor(S.QF[:, bass.ds(t, 1), :].squeeze(1), S.ps[:, 6 + j % 2, 0:D], x1[:, j, :], ALU.add
                                ).then_inc(ph["y_done"], 1)
                after(dve, ph["y_done"], n)
                v.tensor_tensor(S.QF[:, bass.ds(t, 1), :].squeeze(1), S.QF[:, bass.ds(t, 1), :].squeeze(1),
                                rows[:, 2, :], ALU.add).then_inc(ph["y_biased"], 1)

            def behind():
                after(dve, ph["y_biased"], NODE_TILES)
                layernorm_stats(nc, dve, own, S.QF, stats, S.ln2_mv, S.ln2_rstd, ph["eps_done2"], ph["sqrt_done2"])

            for name in ("hot_ready", "rows_used"):
                dve.sem_inc(ph[name], lanes)
            for name in ("attended", "den_eps", "den_inv"):
                dve.sem_inc(ph[name], RING)
            for h in range(AHEAD):
                onehot_T(nc, S, ph, dve, hot, relB, 0, h, h + 1)
            for i, h, k, n in paced(dve, attend, between, mlp, behind):
                if not (isinstance(k, int) and k + AHEAD >= GROUPS):
                    i2, h2, _, n2 = group_at(i, h + AHEAD, lanes)
                    onehot_T(nc, S, ph, dve, hot, relB, i2, h2, n2)
                dve.wait_ge(ph[f"gathered{h}"], i * (16 * GROUP) + 16 * GROUP)
                dve.wait_ge(ph["dst_psum"], n + lanes)
                v.tensor_tensor(S.scoreX[:, bass.ds(k * GROUP, GROUP)], edge_k(h), got[:, h, :, D], ALU.add
                                ).then_inc(ph["rows_used"], 1)

        @block.tensor
        def _(pe):
            def attend(i, t, j, n):
                after(pe, ph["q_staged"], n)
                bank_again(pe, ph["qT_ready"], j, n)
                transpose_tile(nc, ph, pe, qr, j, 4 + j % 2, S.ident, "qT")
                after(pe, ph["qT_ready"], n)
                bank_again(pe, ph["attended"], j, n)
                for c in range(2):
                    ins = nc.tensor.matmul(S.ps[:, j % 2, c * (P + 4):(c + 1) * (P + 4)], qT[:, j, c, :],
                                           S.kvbd[:, c, :], start=True, stop=True)
                ins.then_inc(ph["num_psum"], 1)

            def between():
                pe.wait_ge(ph["weights_in"], 96)
                pe.wait_ge(ph["attended"], NODE_TILES + RING)
                for name in ("xT_psum", "h_psum", "y_psum"):
                    pe.sem_inc(ph[name], RING)

            def mlp(i, t, j, n):
                after(pe, ph["xn_ready"], n)
                bank_again(pe, ph["xT_ready"], j, n)
                transpose_tile(nc, ph, pe, x1, j, 4 + j % 2, S.ident)
                after(pe, ph["xT_ready"], n)
                bank_again(pe, ph["hidden"], j, n)
                for m in range(2):
                    for c in range(2):
                        ins = nc.tensor.matmul(S.ps[:, j % 2, m * P:(m + 1) * P], W1[:, c, m * P:(m + 1) * P],
                                               xT[:, j, c, :], start=c == 0, stop=c == 1)
                ins.then_inc(ph["h_psum"], 1)
                after(pe, ph["hidden"], n)
                bank_again(pe, ph["y_done"], j, n)
                for c in range(2):
                    ins = nc.tensor.matmul(S.ps[:, 6 + j % 2, 0:D], hT[:, j, c, :], W2[:, c, :],
                                           start=c == 0, stop=c == 1)
                ins.then_inc(ph["y_psum"], 1)

            pe.sem_inc(ph["dst_psum"], lanes)
            pe.sem_inc(ph["qT_psum"], RING)
            pe.sem_inc(ph["num_psum"], RING)
            for i, h, k, n in paced(pe, attend, between, mlp):
                blocks = dst_blocks(pe, S, k)
                pe.wait_ge(ph["hot_ready"], n + lanes)
                pe.wait_ge(ph["rows_used"], n + lanes - (1 if h == 0 else 2))
                for j, b in enumerate(blocks):
                    last = nc.tensor.matmul(edge_k(h)[:, j:j + 1], hot[:, h, j * P:(j + 1) * P],
                                            S.qk[:, 1, bass.ds(b, 1)], start=True, stop=True)
                last.then_inc(ph["dst_psum"], 1)


def softmax_weights(nc, S, A, leaky):
    N = GROUP * P
    with Phase(nc, f"softmax_weights_{S.layer}") as ph:
        score = ph.sb("score_scan", [GROUPS, N])
        fwd = ph.sb("max_forward", [GROUPS, N])
        bwd = ph.sb("max_backward", [GROUPS, N])
        ends = ph.sb("row_ends", [GROUPS, 2])
        rows = ph.sb("row_ends_T", [1, 4, GROUPS])
        carry = ph.sb("carry_rows", [1, 2, GROUPS + 1])
        carryT = ph.sb("carry_cols", [GROUPS, 2])
        ps2 = S.ps[:, :, :].rearrange("p b n -> p (b n)")
        block = ph.block()

        @block.vector
        def _(dve):
            v, own = nc.vector, Own(dve, ph["dve_own"])
            if leaky:
                own(v.tensor_scalar(S.weightX[:, :], S.scoreX[:, :], 0.2, None, ALU.mult))
                own.wait()
                own(v.tensor_tensor(S.scoreX[:, :], S.scoreX[:, :], S.weightX[:, :], ALU.max))
                own.wait()
            own(v.tensor_tensor(S.scoreX[:, :], S.scoreX[:, :], S.validX[:, :], ALU.mult))
            own.wait()
            v.tensor_tensor(S.scoreX[:, :], S.scoreX[:, :], S.penX[:, :], ALU.add).then_inc(ph["score_ready"], 1)
            own(v.memset(carry[:, :, :], -BIG))
            dve.wait_ge(ph["score_psum"], 1)
            own(v.tensor_copy(score[:, :], ps2[0:GROUPS, 0:N]))
            own.wait()
            own(v.tensor_tensor_scan(fwd[:, :], S.cut[:, 0, :], score[:, :], -BIG, ALU.add, ALU.max))
            own(v.tensor_tensor_scan(bwd[:, ::-1], S.cut[:, 1, ::-1], score[:, ::-1], -BIG, ALU.add, ALU.max))
            own.wait()
            own(v.tensor_copy(ends[:, 0:1], fwd[:, N - 1:N]))
            v.tensor_copy(ends[:, 1:2], bwd[:, 0:1]).then_inc(ph["ends_ready"], 1)
            dve.wait_ge(ph["ends_psum"], 1)
            own(v.tensor_copy(rows[:, :, :], ps2[0:1, 1024:1024 + 4 * GROUPS].rearrange("p (a n) -> p a n", a=4)))
            own.wait()
            own(v.tensor_tensor_scan(carry[:, 0, 1:GROUPS + 1], rows[:, 2, :], rows[:, 0, :], -BIG, ALU.add, ALU.max))
            own(v.tensor_tensor_scan(carry[:, 1, 0:GROUPS][:, ::-1], rows[:, 3, ::-1], rows[:, 1, ::-1], -BIG, ALU.add,
                                     ALU.max))
            own.wait()
            S.carry_ready = own.total
            dve.wait_ge(ph["carry_psum"], 1)
            own(v.tensor_copy(carryT[:, :], ps2[0:GROUPS, 1536:1538]))
            own.wait()
            own(v.tensor_tensor_scan(fwd[:, :], S.cut[:, 0, :], score[:, :], carryT[:, 0:1], ALU.add, ALU.max))
            own(v.tensor_tensor_scan(bwd[:, ::-1], S.cut[:, 1, ::-1], score[:, ::-1], carryT[:, 1:2], ALU.add,
                                     ALU.max))
            own.wait()
            own(v.tensor_tensor(fwd[:, :], fwd[:, :], bwd[:, :], ALU.max))
            own.wait()
            v.tensor_tensor(score[:, :], score[:, :], fwd[:, :], ALU.subtract).then_inc(ph["shifted"], 1)
            dve.wait_ge(ph["weight_psum"], 1)
            own(v.tensor_tensor(S.weightX[:, :].rearrange("p (q g) -> p q g", g=GROUP),
                                ps2[:, 2048:2048 + STEPS].rearrange("p (g q) -> p q g", g=GROUP),
                                S.validX[:, :].rearrange("p (q g) -> p q g", g=GROUP), ALU.mult))
            own.wait()

        @block.scalar
        def _(act):
            act.wait_ge(ph["shifted"], 1)
            nc.scalar.activation(score[:, :], score[:, :], ACT.Exp).then_inc(ph["exps"], 1)

        @block.tensor
        def _(pe):
            t = nc.tensor
            pe.wait_ge(ph["score_ready"], 1)
            for g in range(GROUP):
                ins = t.transpose(ps2[0:GROUPS, g * P:(g + 1) * P], S.scoreX[:, g::GROUP], S.ident[:, :])
            ins.then_inc(ph["score_psum"], 1)
            pe.wait_ge(ph["ends_ready"], 1)
            idg = S.ident[0:GROUPS, 0:GROUPS]
            for m, col in enumerate((ends[:, 0:1], ends[:, 1:2], S.row_cut[:, 0:1], S.row_cut[:, 1:2])):
                ins = t.transpose(ps2[0:1, 1024 + m * GROUPS:1024 + (m + 1) * GROUPS], col, idg)
            ins.then_inc(ph["ends_psum"], 1)
            pe.wait_ge(ph["dve_own"], S.carry_ready)
            t.transpose(ps2[0:GROUPS, 1536:1537], carry[0:1, 0, 0:GROUPS], S.ident[0:1, 0:1])
            t.transpose(ps2[0:GROUPS, 1537:1538], carry[0:1, 1, 1:GROUPS + 1], S.ident[0:1, 0:1]
                        ).then_inc(ph["carry_psum"], 1)
            pe.wait_ge(ph["exps"], 1)
            for g in range(GROUP):
                ins = t.transpose(ps2[:, 2048 + g * GROUPS:2048 + (g + 1) * GROUPS], score[:, g * P:(g + 1) * P], idg)
            ins.then_inc(ph["weight_psum"], 1)


def aggregate(nc, S, A):
    with Phase(nc, f"aggregate_{S.layer}") as ph:
        rowsB = ph.sb("step_rows", [P, AGG_LANES, GROUP, D + 1])
        hotw = ph.sb("weighted_onehot", [P, AGG_LANES, GROUP, P])
        relw = ph.sb("rel_and_weight", [P, AGG_LANES, 3, GROUP])
        negw = ph.sb("minus_weight", [P, STEPS])
        far = ph.sb("distance", [P, AGG_LANES, ON_ACT, P])
        odd = ph.sb("odd_edge_sums", [P, NODE_TILES, D + 1])
        block = ph.block()

        @block.gpsimd
        def _(pool):
            g = nc.gpsimd

            def columns(i, h, k, n):
                pool.wait_ge(ph["sums_psum"], n * GROUP)
                g.tensor_copy(relw[:, h, 0, :], S.relX[:, bass.ds(k * GROUP, GROUP)])
                g.tensor_copy(relw[:, h, 1, :], S.weightX[:, bass.ds(k * GROUP, GROUP)])
                g.tensor_copy(relw[:, h, 2, :], negw[:, bass.ds(k * GROUP, GROUP)]).then_inc(ph["columns"], 1)

            g.memset(rowsB[:, :, :, D:D + 1], 1.0).then_inc(ph["ones_made"], 1)
            pool.wait_ge(ph["negated"], 1)
            columns(0, 0, 0, 1)
            for i, h, k, n, later in groups_ahead(pool, 1, AGG_LANES):
                if later:
                    columns(*later)
                pool.wait_ge(ph["columns"], n)
                pool.sem_inc(ph["weigh_gate"], 1)
                for j in range(ON_ACT, GROUP):
                    ins = g.tensor_scalar(hotw[:, h, j, :], S.iota_row[:, :], relw[:, h, 0, j:j + 1],
                                          relw[:, h, 1, j:j + 1], ALU.is_equal, ALU.mult)
                ins.then_inc(ph["hotw_ready"], 1)

        @block.scalar
        def _(act):
            a = nc.scalar
            for i, h, k, n in groups(act, AGG_LANES):
                act.wait_ge(ph["columns"], n)
                for j in range(ON_ACT):
                    ins = a.activation(far[:, h, j, :], S.iota_row[:, :], ACT.Abs, scale=-1.0,
                                       bias=relw[:, h, 0, j:j + 1])
                ins.then_inc(ph["distances"], 1)
                act.wait_ge(ph["distances"], n)
                for j in range(ON_ACT):
                    ins = a.activation(hotw[:, h, j, :], far[:, h, j, :], ACT.Relu, scale=relw[:, h, 2, j:j + 1],
                                       bias=relw[:, h, 1, j:j + 1])
                ins.then_inc(ph["hotw_by_act"], 1)

        @block.sync
        def _(sp):
            for i, h, k, n in groups(sp, AGG_LANES):
                sp.wait_ge(ph["sums_psum"], n * GROUP)
                sp.dma_start(rowsB[:, h, :, 0:D], S.step_dram[bass.ds(k, 1), :, :].rearrange(
                    "a p (g d) -> (a p) g d", d=D)).then_inc(ph[f"rows_in{h}"], 16)

        @block.vector
        def _(dve):
            v = nc.vector
            v.tensor_scalar(negw[:, :], S.weightX[:, :], -1.0, None, ALU.mult).then_inc(ph["negated"], 1)
            v.memset(S.acc[:, :, :], 0.0).then_inc(ph["cleared"], 1)
            v.memset(odd[:, :, :], 0.0).then_inc(ph["cleared"], 1)
            dve.wait_ge(ph["cleared"], 2)
            dve.sem_inc(ph["added"], GROUP)
            for i, h, k, n in groups(dve, AGG_LANES):
                for j, b in enumerate(dst_blocks(dve, S, k)):
                    m = n * GROUP + (j + 1 - GROUP)
                    sums = S.acc if j % 2 == 0 else odd
                    dve.wait_ge(ph["sums_psum"], m + AGG_LANES * GROUP)
                    dve.wait_ge(ph["added"], m + GROUP - (1 if j == 0 else 2))
                    v.tensor_tensor(sums[:, bass.ds(b, 1), :], S.ps[:, j:j + 1, 0:D + 1],
                                    sums[:, bass.ds(b, 1), :], ALU.add).then_inc(ph["added"], 1)
            dve.wait_ge(ph["added"], STEPS + GROUP)
            v.tensor_tensor(S.acc[:, :, :], S.acc[:, :, :], odd[:, :, :], ALU.add)

        @block.tensor
        def _(pe):
            pe.sem_inc(ph["sums_psum"], AGG_LANES * GROUP)
            pe.wait_ge(ph["ones_made"], 1)
            for i, h, k, n in groups(pe, AGG_LANES):
                pe.wait_ge(ph["hotw_ready"], n)
                pe.wait_ge(ph["hotw_by_act"], n)
                pe.wait_ge(ph[f"rows_in{h}"], i * 16 + 16)
                for j in range(GROUP):
                    pe.wait_ge(ph["added"], n * GROUP + (j + 1 - GROUP))
                    nc.tensor.matmul(S.ps[:, j, 0:D + 1], hotw[:, h, j, :], rowsB[:, h, j, :],
                                     start=True, stop=True).then_inc(ph["sums_psum"], 1)


def ln_scratch(ph):
    return (ph.sb("ln_stats", [P, NODE_TILES, 6]), ph.sb("ln_mean_var", [P, NODE_TILES, 2]),
            ph.sb("ln_rstd", [P, NODE_TILES]))


def ln_root(nc, ph, act, rstd):
    act.wait_ge(ph["eps_done"], 1)
    nc.scalar.activation(rstd[:, :], rstd[:, :], ACT.Sqrt).then_inc(ph["sqrt_done"], 1)


def add_edge_sums(nc, ph, S, dve):
    v, own = nc.vector, Own(dve, ph["dve_own_sums"])
    inv = S.inv_sum
    own(v.tensor_scalar_max(inv[:, :], S.acc[:, :, D], 1e-30))
    own.wait()
    own(v.reciprocal(inv[:, :], inv[:, :]))
    own.wait()
    for t in range(NODE_TILES):
        own(v.scalar_tensor_tensor(S.X[:, t, :], S.acc[:, t, 0:D], inv[:, t:t + 1], S.X[:, t, :],
                                   ALU.mult, ALU.add))
    own.wait()


def router(nc, S, A):
    with Phase(nc, "router") as ph:
        ph.ps = S.ps
        Wr = ph.sb("w_router", [P, 2, E0])
        br = ph.sb("b_router", [P, E0])
        rows = ph.sb("ln2_g_b", [P, 2, D])
        stats, mv, rstd = ln_scratch(ph)
        xt = ph.sb("xt_ring", [P, RING, D])
        xT = ph.sb("xt_T", [P, RING, 2, P])
        block = ph.block()

        @block.sync
        def _(sp):
            sp.dma_start(Wr[:, :, :], A["Wr"].rearrange("(c p) n -> p c n", p=P)).then_inc(ph["weights_in"], 16)
            sp.dma_start(br[:, :], bcast(A["br"])).then_inc(ph["weights_in"], 16)
            for m, src in enumerate(("ln2_g", "ln2_b")):
                sp.dma_start(rows[:, m, :], bcast(A[src])).then_inc(ph["weights_in"], 16)
            sp.wait_ge(ph["weights_in"], 64)

        @block.vector
        def _(dve):
            v, own = nc.vector, Own(dve, ph["dve_own"])
            dve.wait_ge(ph["weights_in"], 64)
            for t in range(NODE_TILES):
                own(v.scalar_tensor_tensor(S.QF[:, t, :], S.QF[:, t, :], S.ln2_mv[:, t, 0:1], rows[:, 0, :],
                                           ALU.subtract, ALU.mult))
            own.wait()
            dve.wait_ge(ph["bias_added"], 1)
            add_edge_sums(nc, ph, S, dve)
            for t in range(NODE_TILES):
                own(v.scalar_tensor_tensor(S.X[:, t, :], S.QF[:, t, :], S.ln2_rstd[:, t:t + 1], S.X[:, t, :],
                                           ALU.mult, ALU.add))
            own.wait()
            layernorm_stats(nc, dve, own, S.X, stats, mv, rstd, ph["eps_done"], ph["sqrt_done"])
            for name in ("xn_ready", "logits"):
                dve.sem_inc(ph[name], RING)

            def biased(i, t, j, n):
                after(dve, ph["l_psum"], n)
                v.tensor_tensor(S.logits[:, bass.ds(t, 1), :].squeeze(1), S.ps[:, j % 2, 0:E0], br[:, :], ALU.add
                                ).then_inc(ph["logits"], 1)

            skewed(dve, norm_tile(nc, ph, dve, S.X, mv, rstd, xt), nothing, nothing, biased)
            after(dve, ph["logits"], NODE_TILES)

        @block.gpsimd
        def _(pool):
            pool.wait_ge(ph["weights_in"], 64)
            nc.gpsimd.tensor_tensor(S.X[:, :, :], S.X[:, :, :], rows[:, 1, :].unsqueeze(1).broadcast_to(
                [P, NODE_TILES, D]), ALU.add).then_inc(ph["bias_added"], 1)
            pool.wait_ge(ph["qf_free"], 1)
            keep_tiles(nc, ph, pool, xt, S.QF)

        @block.scalar
        def _(act):
            act.wait_ge(ph["eps_done"], 1)
            act.sem_inc(ph["qf_free"], 1)
            nc.scalar.activation(rstd[:, :], rstd[:, :], ACT.Sqrt).then_inc(ph["sqrt_done"], 1)
            act.sem_inc(ph["xT_ready"], RING)
            for i, t, j, n in tiles(act):
                again(act, ph["l_psum"], n)
                copy_transposed(nc, ph, act, j, n, 4 + j % 2, xT)

        @block.tensor
        def _(pe):
            pe.wait_ge(ph["weights_in"], 64)
            for name in ("xT_psum", "l_psum"):
                pe.sem_inc(ph[name], RING)

            def transposes(i, t, j, n):
                after(pe, ph["xn_ready"], n)
                bank_again(pe, ph["xT_ready"], j, n)
                transpose_tile(nc, ph, pe, xt, j, 4 + j % 2, S.ident)

            def products(i, t, j, n):
                after(pe, ph["xT_ready"], n)
                bank_again(pe, ph["logits"], j, n)
                for c in range(2):
                    ins = nc.tensor.matmul(S.ps[:, j % 2, 0:E0], xT[:, j, c, :], Wr[:, c, :],
                                           start=c == 0, stop=c == 1)
                ins.then_inc(ph["l_psum"], 1)

            skewed(pe, transposes, products)


def top_two(nc, own, logits, top, idx, idxf, hot1, hot2, iota8, width):
    v = nc.vector
    for t in range(NODE_TILES):
        own(v.max(top[:, t, :], logits[:, t, :]))
    own.wait()
    for t in range(NODE_TILES):
        own(v.max_index(idx[:, t, :], top[:, t, :], logits[:, t, :]))
    own.wait()
    own(v.tensor_copy(idxf[:, :, :], idx[:, :, :]))
    own.wait()
    for m, hot in enumerate((hot1, hot2)):
        w = hot.shape[2]
        own(v.tensor_tensor(hot[:, :, :], iota8[:, 0:w].unsqueeze(1).broadcast_to([P, NODE_TILES, w]),
                            idxf[:, :, m:m + 1].broadcast_to([P, NODE_TILES, w]), ALU.is_equal))
    own.wait()


def dispatch_plan(nc, S, A):
    with Phase(nc, "dispatch_plan") as ph:
        top = ph.sb("top8", [P, NODE_TILES, 8])
        idx = ph.sb("top8_idx", [P, NODE_TILES, 8], U32)
        idxf = ph.sb("top8_idx_f", [P, NODE_TILES, 8])
        hot1 = ph.sb("hot1", [P, NODE_TILES, E0])
        hot2 = ph.sb("hot2", [P, NODE_TILES, E0])
        both = ph.sb("hot_both", [P, NODE_TILES, E0])
        tri = ph.sb("strictly_before", [P, P])
        tot = ph.sb("tile_totals", [P, NODE_TILES, E0])
        cum = ph.sb("totals_up_to", [P, NODE_TILES, E0])
        one = ph.sb("one_row", [P, NODE_TILES])
        tl = ph.sb("tiles_of_expert", [P, E0])
        tlI = ph.sb("tiles_of_expert_i", [P, E0], I32)
        end = ph.sb("end_tile", [P, E0])
        base = ph.sb("first_slot", [P, E0])
        posf = ph.sb("slot_f", [P, 2, NODE_TILES])
        trash = ph.sb("padding_slot", [P, 1])
        step = ph.sb("slot_tile_no", [P, SLOT_TILES])
        ex = ph.sb("expert_of_tile_f", [P, SLOT_TILES])
        partI = ph.sb("slot_parts_i", [P, 2, 2, NODE_TILES], I32)
        part = ph.sb("slot_parts", [P, 2, 2, NODE_TILES])
        node_no = ph.sb("node_no", [P, NODE_TILES])
        hot_row = ph.sb("slot_row_onehot", [P, RING, 2, P])
        hot_tile = ph.sb("slot_tile_onehot", [P, RING, 2, SLOT_TILES])
        block = ph.block()

        @block.sync
        def _(sp):
            for e in range(E0):
                sp.dma_start(S.W2[:, e, :, :], A["eW2"][e * HID:(e + 1) * HID, :].rearrange("(c p) n -> p c n", p=P)
                             ).then_inc(ph["w2_in"], 16)
            sp.wait_ge(ph["w2_in"], 16 * E0)

        @block.gpsimd
        def _(pool):
            g, made = nc.gpsimd, ph["pool_made"]
            g.memset(tri[:, :], 1.0).then_inc(made, 1)
            g.memset(one[:, :], 1.0).then_inc(made, 1)
            g.memset(S.node_mask[:, :], 1.0).then_inc(made, 1)
            g.iota(trash[:, :], [[0, 1]], base=SLOTS, channel_multiplier=1,
                   allow_small_or_imprecise_dtypes=True).then_inc(made, 1)
            g.iota(step[:, :], [[1, SLOT_TILES]], base=0, channel_multiplier=0,
                   allow_small_or_imprecise_dtypes=True).then_inc(made, 1)
            g.iota(node_no[:, :], [[P, NODE_TILES]], base=0, channel_multiplier=1,
                   allow_small_or_imprecise_dtypes=True).then_inc(made, 1)
            pool.wait_ge(made, 6)
            g.affine_select(out=tri[:, :], in_=tri[:, :], compare_op=ALU.is_gt, fill=0.0, base=0,
                            pattern=[[1, P]], channel_multiplier=-1).then_inc(made, 1)
            g.affine_select(out=S.node_mask[:, NODE_TILES - 1:], in_=S.node_mask[:, NODE_TILES - 1:],
                            compare_op=ALU.is_ge, fill=0.0, base=LAST_ROWS - 1, pattern=[[0, 1]],
                            channel_multiplier=-1).then_inc(made, 1)

        @block.vector
        def _(dve):
            v, own = nc.vector, Own(dve, ph["dve_own"])
            top_two(nc, own, S.logits, top, idx, idxf, hot1, hot2, S.iota_row, E0)
            v.tensor_tensor(S.w2[:, :], top[:, :, 1], top[:, :, 0], ALU.subtract).then_inc(ph["gap"], 1)
            own(v.tensor_tensor(both[:, :, :], hot1[:, :, :], hot2[:, :, :], ALU.add))
            dve.wait_ge(ph["pool_made"], 8)
            own.wait()
            own(v.tensor_tensor(both[:, :, :], both[:, :, :],
                                S.node_mask[:, :].unsqueeze(2).broadcast_to([P, NODE_TILES, E0]), ALU.mult))
            dve.wait_ge(ph["gap_exp"], 1)
            own(v.tensor_scalar_add(S.w1[:, :], S.w2[:, :], 1.0))
            own.wait()
            S.both_ready = own.total
            own(v.reciprocal(S.w1[:, :], S.w1[:, :]))
            own.wait()
            own(v.tensor_tensor(S.w2[:, :], S.w2[:, :], S.w1[:, :], ALU.mult))
            own.wait()
            for w, hot, dst in ((S.w1, hot1, S.wexp), (S.w2, hot2, tot)):
                own(v.tensor_tensor(dst[:, :, :], hot[:, :, :], w[:, :].unsqueeze(2).broadcast_to(
                    [P, NODE_TILES, E0]), ALU.mult))
            own.wait()
            own(v.tensor_tensor(S.wexp[:, :, :], S.wexp[:, :, :], tot[:, :, :], ALU.add))
            own.wait()
            dve.wait_ge(ph["counts"], 1)
            flat = NODE_TILES * E0
            own(v.tensor_copy(tot[:, :, :], S.ps[:, 1, 0:flat].rearrange("p (t e) -> p t e", e=E0)))
            own.wait()
            for e in range(E0):
                own(v.tensor_tensor_scan(cum[:, :, e], one[:, :], tot[:, :, e], 0.0, ALU.mult, ALU.add))
            own.wait()
            own(v.tensor_scalar_add(tlI[:, :], cum[:, NODE_TILES - 1, :], float(P - 1)))
            own.wait()
            own(v.tensor_scalar(tlI[:, :], tlI[:, :], 7, None, ALU.arith_shift_right))
            own.wait()
            own(v.tensor_copy(tl[:, :], tlI[:, :]))
            own.wait()
            own(v.tensor_tensor_scan(end[:, :], one[:, 0:E0], tl[:, :], 0.0, ALU.mult, ALU.add))
            own.wait()
            own(v.tensor_tensor(base[:, :], end[:, :], tl[:, :], ALU.subtract))
            own(v.memset(ex[:, :], 0.0))
            own(v.tensor_tensor(cum[:, :, :], cum[:, :, :], tot[:, :, :], ALU.subtract))
            own.wait()
            own(v.tensor_scalar(base[:, :], base[:, :], float(P), None, ALU.mult))
            own(v.tensor_tensor(cum[:, :, :], cum[:, :, :],
                                S.ps[:, 0, 0:flat].rearrange("p (t e) -> p t e", e=E0), ALU.add))
            for e in range(E0 - 1):
                own.wait()
                own(v.scalar_tensor_tensor(ex[:, :], step[:, :], end[:, e:e + 1], ex[:, :], ALU.is_ge, ALU.add))
            own.wait()
            own(v.tensor_copy(S.expertI[:, :], ex[0:1, :]))
            own(v.tensor_tensor(cum[:, :, :], cum[:, :, :],
                                base[:, :].unsqueeze(1).broadcast_to([P, NODE_TILES, E0]), ALU.add))
            own.wait()
            for m, hot in enumerate((hot1, hot2)):
                own(v.tensor_tensor(tot[:, :, :], cum[:, :, :], hot[:, :, :], ALU.mult))
                own.wait()
                own(v.tensor_reduce(posf[:, m, :], tot[:, :, :], AX.X, ALU.add))
                own.wait()
            own(v.tensor_scalar(posf[:, :, :], posf[:, :, :], trash[:, 0:1], None, ALU.subtract))
            own.wait()
            own(v.tensor_tensor(posf[:, :, :], posf[:, :, :],
                                S.node_mask[:, :].unsqueeze(1).broadcast_to([P, 2, NODE_TILES]), ALU.mult))
            own.wait()
            own(v.tensor_scalar(S.posI[:, :, :], posf[:, :, :], trash[:, 0:1], None, ALU.add))
            own.wait()
            own(v.tensor_scalar(partI[:, 0, :, :], S.posI[:, :, :], P - 1, None, ALU.bitwise_and))
            own(v.tensor_scalar(partI[:, 1, :, :], S.posI[:, :, :], 7, None, ALU.arith_shift_right))
            own.wait()
            own(v.tensor_copy(part[:, :, :, :], partI[:, :, :, :]))
            own.wait()
            dve.sem_inc(ph["places"], RING)
            for i, t, j, n in tiles(dve):
                again(dve, ph["listed"], n)
                for m in range(2):
                    v.tensor_scalar(hot_row[:, j, m, :], S.iota_row[:, :], part[:, 0, m, bass.ds(t, 1)], None,
                                    ALU.is_equal)
                    ins = v.tensor_scalar(hot_tile[:, j, m, :], step[:, :], part[:, 1, m, bass.ds(t, 1)],
                                          node_no[:, bass.ds(t, 1)], ALU.is_equal, ALU.mult)
                ins.then_inc(ph["places"], 1)
            after(dve, ph["listed"], NODE_TILES)
            own(v.tensor_copy(S.slot_node[:, :], S.ps[:, 2, 0:SLOT_TILES]))
            own.wait()

        @block.scalar
        def _(act):
            act.wait_ge(ph["gap"], 1)
            nc.scalar.activation(S.w2[:, :], S.w2[:, :], ACT.Exp).then_inc(ph["gap_exp"], 1)

        @block.tensor
        def _(pe):
            flat = NODE_TILES * E0
            rhs = both[:, :, :].rearrange("p t e -> p (t e)")
            pe.wait_ge(ph["dve_own"], S.both_ready)
            nc.tensor.matmul(S.ps[:, 0, 0:flat], tri[:, :], rhs, start=True, stop=True)
            nc.tensor.matmul(S.ps[:, 1, 0:flat], S.ones[:, :], rhs, start=True, stop=True).then_inc(ph["counts"], 1)
            pe.sem_inc(ph["listed"], RING)

            def five(i, first, last):
                for j in range(RING):
                    after(pe, ph["places"], i * RING + (j + 1))
                    for m in range(2):
                        ins = nc.tensor.matmul(S.ps[:, 2, 0:SLOT_TILES], hot_row[:, j, m, :], hot_tile[:, j, m, :],
                                               start=first and j + m == 0, stop=last and j == RING - 1 and m == 1)
                    ins.then_inc(ph["listed"], 1)
            five(0, True, False)
            with pe.Fori(1, T5 - 1) as i:
                five(i, False, False)
            five(T5 - 1, False, True)


def expert_inputs(nc, S, A):
    with Phase(nc, "expert_inputs") as ph:
        stats, mv, rstd = ln_scratch(ph)
        block = ph.block()

        @block.vector
        def _(dve):
            own = Own(dve, ph["dve_own"])
            layernorm_stats(nc, dve, own, S.QF, stats, mv, rstd, ph["eps_done"], ph["sqrt_done"])
            for t in range(NODE_TILES):
                nc.vector.tensor_scalar(S.QF[:, t, :], S.QF[:, t, :], mv[:, t, 0:1], rstd[:, t:t + 1],
                                        ALU.subtract, ALU.mult).then_inc(ph["xn_ready"], 1)

        @block.scalar
        def _(act):
            ln_root(nc, ph, act, rstd)

        @block.sync
        def _(sp):
            for k in range(T5):
                sp.wait_ge(ph["xn_ready"], RING * (k + 1))
                sp.dma_start(S.xn_dram[k * RING * P:(k + 1) * RING * P, :].rearrange("(t p) d -> p t d", p=P),
                             S.QF[:, k * RING:(k + 1) * RING, :]).then_inc(ph["table_out"], 16)
            sp.wait_ge(ph["table_out"], 16 * T5)


def experts(nc, S, A):
    HC = HID // P
    with Phase(nc, "experts") as ph:
        ph.for_gathers("x_in0", "x_in1")
        xs = ph.sb("slot_rows", [P, 2, D])
        idx = ph.sb("node_idx", [P, 2], I32)
        small = ph.sb("g_b_b1", [P, 2, 4 + HC])
        W1 = ph.sb("expert_w1", [P, 2, 2, HID])
        xT = ph.sb("xe_T", [P, 2, 2, P])
        hT = ph.sb("hidden_T", [P, 2, HC, P])
        ys = ph.sb("y_rows", [P, 2, D])
        block = ph.block()

        def pairs(eng, body):
            with eng.Fori(0, SLOT_TILES // 2) as i:
                for h in range(2):
                    body(i, h, i * 2 + h, i * 2 + (h + 1))

        @block.sync
        def _(sp):
            def load(i, h, t, n):
                e = sp.value_load(S.expertI[0:1, bass.ds(t, 1)], min_val=0, max_val=E0 - 1)
                sp.wait_ge(ph["h_half"], n * 2)
                sp.dma_start(W1[:, h, :, :], A["eW1"][bass.ds(e * D, D), :].rearrange("(c p) n -> p c n", p=P)
                             ).then_inc(ph[f"w1_in{h}"], 16)
                sp.wait_ge(ph["hidden"], n * 2)
                sp.dma_start(small[:, h, :], A["eSmall"][bass.ds(e, 1), :, :].squeeze(0)
                             ).then_inc(ph[f"small_in{h}"], 16)
            pairs(sp, load)

        @block.gpsimd
        def _(pool):
            def gather(i, h, t, n):
                pool.wait_ge(ph["xT_psum"], n)
                nc.gpsimd.tensor_copy(idx[:, h:h + 1], S.slot_node[:, bass.ds(t, 1)]).then_inc(ph["idx_ready"], 1)
                pool.wait_ge(ph["idx_ready"], n)
                pool.sem_inc(ph["gather_gate"], 1)
                nc.gpsimd.indirect_dma_start(xs[:, h, :], None, S.xn_dram,
                                             bass.IndirectOffsetOnAxis(ap=idx[:, h:h + 1], axis=0)
                                             ).then_inc(ph[f"x_in{h}"], 16)
            pairs(pool, gather)

        @block.vector
        def _(dve):
            dve.sem_inc(ph["xT_ready"], 2)
            dve.sem_inc(ph["y_ready"], 2)

            def xe(h, i, n):
                dve.wait_ge(ph["xT_psum"], n + 2)
                dve.wait_ge(ph[f"small_in{h}"], i * 16 + 16)
                dve.wait_ge(ph["h_half"], n * 2)
                for c in range(2):
                    ins = nc.vector.tensor_scalar(xT[:, h, c, :], S.ps[:, 0, c * P:(c + 1) * P], small[:, h, c:c + 1],
                                                  small[:, h, 2 + c:3 + c], ALU.mult, ALU.add)
                ins.then_inc(ph["xT_ready"], 1)

            def y(h, i, n):
                dve.wait_ge(ph["y_psum"], n + 2)
                dve.wait_ge(ph[f"y_out{h}"], i * 16 + 16)
                nc.vector.tensor_copy(ys[:, h, :], S.ps[:, 1, 0:D]).then_inc(ph["y_ready"], 1)

            xe(0, 0, 1)
            xe(1, 0, 2)
            with dve.Fori(0, SLOT_TILES // 2 - 1) as i:
                xe(0, i + 1, i * 2 + 3)
                y(0, i, i * 2 + 1)
                xe(1, i + 1, i * 2 + 4)
                y(1, i, i * 2 + 2)
            last = SLOT_TILES // 2 - 1
            y(0, last, last * 2 + 1)
            y(1, last, last * 2 + 2)

        @block.scalar
        def _(act):
            act.sem_inc(ph["hidden"], 2 * 2)
            for h in range(2):
                act.sem_inc(ph[f"y_out{h}"], 16)

            def gelu(i, h, t, n):
                act.wait_ge(ph["y_psum"], n)
                for m in range(HC):
                    if m % 4 == 0:
                        act.wait_ge(ph["h_half"], n * 2 + (m // 4 + 3))
                    ins = nc.scalar.activation(hT[:, h, m, :], S.ps[:, 2 + 2 * h + m // 4, (m % 4) * P:(m % 4 + 1) * P],
                                               ACT.Gelu, bias=small[:, h, 4 + m:5 + m])
                    if m % 4 == 3:
                        ins.then_inc(ph["hidden"], 1)

            def out(i, h, t, n):
                act.wait_ge(ph["y_ready"], n + 2)
                act.dma_start(S.y_dram[bass.ds(t * P, P), :], ys[:, h, :]).then_inc(ph[f"y_out{h}"], 16)


            gelu(0, 0, 0, 1)
            with act.Fori(0, SLOT_TILES // 2 - 1) as i:
                gelu(i, 1, None, i * 2 + 2)
                out(i, 0, i * 2, i * 2 + 1)
                gelu(i, 0, None, i * 2 + 3)
                out(i, 1, i * 2 + 1, i * 2 + 2)
            last = SLOT_TILES // 2 - 1
            gelu(last, 1, None, last * 2 + 2)
            out(last, 0, last * 2, last * 2 + 1)
            out(last, 1, last * 2 + 1, last * 2 + 2)
            for h in range(2):
                act.wait_ge(ph[f"y_out{h}"], 16 * (SLOT_TILES // 2) + 16)

        @block.tensor
        def _(pe):
            for name in ("xT_psum", "y_psum"):
                pe.sem_inc(ph[name], 2)
            pe.sem_inc(ph["h_half"], 4)

            def transposes(h, i, n):
                pe.wait_ge(ph[f"x_in{h}"], i * 16 + 16)
                pe.wait_ge(ph["xT_ready"], n + 1)
                for c in range(2):
                    ins = nc.tensor.transpose(S.ps[:, 0, c * P:(c + 1) * P], xs[:, h, c * P:(c + 1) * P], S.ident[:, :])
                ins.then_inc(ph["xT_psum"], 1)

            def up(h, i, n):
                pe.wait_ge(ph["xT_ready"], n + 2)
                pe.wait_ge(ph[f"w1_in{h}"], i * 16 + 16)
                pe.wait_ge(ph["hidden"], n * 2)
                for m in range(HC):
                    for c in range(2):
                        ins = nc.tensor.matmul(S.ps[:, 2 + 2 * h + m // 4, (m % 4) * P:(m % 4 + 1) * P],
                                               W1[:, h, c, m * P:(m + 1) * P], xT[:, h, c, :],
                                               start=c == 0, stop=c == 1)
                    if m % 4 == 3:
                        ins.then_inc(ph["h_half"], 1)

            def down(h, i, n):
                e = pe.value_load(S.expertI[0:1, bass.ds(i * 2 + h, 1)], min_val=0, max_val=E0 - 1)
                pe.wait_ge(ph["hidden"], n * 2 + 4)
                pe.wait_ge(ph["y_ready"], n + 1)
                for m in range(HC):
                    ins = nc.tensor.matmul(S.ps[:, 1, 0:D], hT[:, h, m, :], S.W2[:, bass.ds(e, 1), m, :].squeeze(1),
                                           start=m == 0, stop=m == HC - 1)
                ins.then_inc(ph["y_psum"], 1)

            transposes(0, 0, 1)
            up(0, 0, 1)
            transposes(1, 0, 2)
            with pe.Fori(0, SLOT_TILES // 2 - 1) as i:
                up(1, i, i * 2 + 2)
                transposes(0, i + 1, i * 2 + 3)
                down(0, i, i * 2 + 1)
                up(0, i + 1, i * 2 + 3)
                transposes(1, i + 1, i * 2 + 4)
                down(1, i, i * 2 + 2)
            last = SLOT_TILES // 2 - 1
            up(1, last, last * 2 + 2)
            down(0, last, last * 2 + 1)
            down(1, last, last * 2 + 2)


def combine(nc, S, A):
    with Phase(nc, "combine") as ph:
        ph.for_gathers(*[f"y_in{j}" for j in range(RING)])
        yr = ph.sb("y_of_slots", [P, RING, 2, D])
        idx = ph.sb("slot_ring", [P, RING, 2], I32)
        wr = ph.sb("weights_ring", [P, RING, E0])
        wT = ph.sb("weights_T", [E0, RING, P])
        b2 = ph.sb("expert_b2", [E0, D])
        block = ph.block()

        @block.sync
        def _(sp):
            sp.dma_start(b2[:, :], A["eb2"]).then_inc(ph["b2_in"], 16)

        @block.gpsimd
        def _(pool):
            def stage(i, t, j, n):
                again(pool, ph["x_done"], n)
                nc.gpsimd.tensor_copy(idx[:, j, :], S.posI[:, :, bass.ds(t, 1)].squeeze(2))
                nc.gpsimd.tensor_copy(wr[:, j, :], S.wexp[:, bass.ds(t, 1), :].squeeze(1)).then_inc(ph["w_staged"], 1)

            def gather(i, t, j, n):
                after(pool, ph["w_staged"], n)
                pool.sem_inc(ph["gather_gate"], 1)
                for m in range(2):
                    nc.gpsimd.indirect_dma_start(yr[:, j, m, :], None, S.y_dram,
                                                 bass.IndirectOffsetOnAxis(ap=idx[:, j, m:m + 1], axis=0)
                                                 ).then_inc(ph[f"y_in{j}"], 16)

            pool.sem_inc(ph["w_staged"], RING)
            skewed(pool, stage, gather)

        @block.scalar
        def _(act):
            act.sem_inc(ph["wT_ready"], RING)
            for i, t, j, n in tiles(act):
                after(act, ph["wT_psum"], n)
                again(act, ph["b_psum"], n)
                nc.scalar.activation(wT[:, j, :], S.ps[0:E0, 2 + j % 2, 0:P], ACT.Copy).then_inc(ph["wT_ready"], 1)

        @block.tensor
        def _(pe):
            pe.wait_ge(ph["b2_in"], 16)
            pe.sem_inc(ph["wT_psum"], RING)
            pe.sem_inc(ph["b_psum"], RING)
            for i, t, j, n in tiles(pe):
                after(pe, ph["w_staged"], n)
                bank_again(pe, ph["wT_ready"], j, n)
                nc.tensor.transpose(S.ps[0:E0, 2 + j % 2, 0:P], wr[:, j, :], S.ident[:, :]).then_inc(ph["wT_psum"], 1)
                after(pe, ph["wT_ready"], n)
                bank_again(pe, ph["b_added"], j, n)
                nc.tensor.matmul(S.ps[:, j % 2, 0:D], wT[:, j, :], b2[:, :], start=True, stop=True
                                 ).then_inc(ph["b_psum"], 1)

        @block.vector
        def _(dve):
            v = nc.vector
            for name in ("b_added", "y1_added", "x_done"):
                dve.sem_inc(ph[name], RING)
            for i, t, j, n in tiles(dve):
                x = S.X[:, bass.ds(t, 1), :].squeeze(1)
                after(dve, ph["b_psum"], n)
                v.tensor_tensor(x, S.ps[:, j % 2, 0:D], x, ALU.add).then_inc(ph["b_added"], 1)
                dve.wait_ge(ph[f"y_in{j}"], i * 32 + 32)
                after(dve, ph["b_added"], n)
                v.scalar_tensor_tensor(x, yr[:, j, 0, :], S.w1[:, bass.ds(t, 1)], x, ALU.mult, ALU.add
                                       ).then_inc(ph["y1_added"], 1)
                after(dve, ph["y1_added"], n)
                v.scalar_tensor_tensor(x, yr[:, j, 1, :], S.w2[:, bass.ds(t, 1)], x, ALU.mult, ALU.add
                                       ).then_inc(ph["x_done"], 1)


E1, EH1, EH2, SH2 = 4, 128, 64, 128


def project_layer1(nc, S, A):
    with Phase(nc, "project_layer1") as ph:
        ph.ps = S.ps
        W = ph.sb("w_src_dst", [P, 2, 2, D])
        rows = ph.sb("b_src_dst_kw_kb_vw_vb", [P, 6, D])
        stats, mv, rstd = ln_scratch(ph)
        xn = ph.sb("xn_ring", [P, RING, D])
        xT = ph.sb("xn_T", [P, RING, 2, P])
        el = ph.sb("el_rows", [P, RING, D + 1])
        er = ph.sb("er_rows", [P, 2, RING, D])
        prod = ph.sb("attn_times_row", [P, 2, RING, D])
        dots5 = ph.sb("attn_dots_of_five", [P, 2, RING])
        dn = ph.sb("head_centred", [P, RING * HEADS, HD])
        sq = ph.sb("head_squares", [P, RING * HEADS, HD])
        hm = ph.sb("head_mean", [P, RING * HEADS])
        hr = ph.sb("head_rstd", [P, RING * HEADS])
        kf = ph.sb("k_rows", [P, RING, D])
        vf = ph.sb("v_rows", [P, RING, D])
        block = ph.block()
        five_rows = lambda m: rows[:, m, :].unsqueeze(1).broadcast_to([P, RING, D])
        per_head = lambda x: x.unsqueeze(2).broadcast_to([P, RING * HEADS, HD])
        heads = lambda x: x.rearrange("p r (h m) -> p (r h) m", m=HD)

        def fives(eng, five):
            five(0, 0, True)
            with eng.Fori(0, T5 // 2 - 1) as i:
                five(i * 2 + 1, 1, True)
                five(i * 2 + 2, 0, True)
            five(T5 - 2, 1, True)
            five(T5 - 1, 0, False)

        @block.sync
        def _(sp):
            for m, src in enumerate(("Ws", "Wd")):
                sp.dma_start(W[:, :, m, :], A[src].rearrange("(c p) n -> p c n", p=P)).then_inc(ph["weights_in"], 16)
            for m, src in enumerate(("bs", "bd", "kw", "kb", "vw", "vb")):
                sp.dma_start(rows[:, m, :], bcast(A[src])).then_inc(ph["weights_in"], 16)
            sp.dma_start(S.attn[:, :], bcast(A["attn"])).then_inc(ph["weights_in"], 16)
            with sp.Fori(0, T5) as i:
                sp.wait_ge(ph["el_five"], i + 1)
                sp.dma_start(S.eltab_dram[bass.ds(i * (RING * P), RING * P), :].rearrange("(t p) d -> p t d", p=P),
                             el[:, :, :]).then_inc(ph["el_out"], 16)
            sp.wait_ge(ph["el_out"], 16 * T5 + 16)

        @block.gpsimd
        def _(pool):
            g = nc.gpsimd
            pool.sem_inc(ph["xn_kept"], RING)
            pool.sem_inc(ph["v_scaled"], 1)
            pool.wait_ge(ph["weights_in"], 144)

            def five(i, e, more):
                for j in range(RING):
                    after(pool, ph["xn_ready"], i * RING + (j + 1))
                    g.tensor_copy(S.XN[:, bass.ds(i * RING + j, 1), :], xn[:, j:j + 1, :]
                                  ).then_inc(ph["xn_kept"], 1)
                if not (isinstance(i, int) and i == 0):
                    left(i - 1, 1 - e)
                pool.wait_ge(ph["normed"], i + 1)
                pool.wait_ge(ph["kv_used"], i * RING + RING)
                g.tensor_tensor(vf[:, :, :], dn[:, :, :].rearrange("p (r h) m -> p r (h m)", r=RING), five_rows(4),
                                ALU.mult).then_inc(ph["v_scaled"], 1)
                pool.wait_ge(ph["v_scaled"], i + 2)
                g.tensor_tensor(vf[:, :, :], vf[:, :, :], five_rows(5), ALU.add).then_inc(ph["v_ready"], 1)

            def left(i, e):
                pool.wait_ge(ph["attn_dots"], i + 1)
                for m in range(2):
                    pool.wait_ge(ph["er_parts"], i * 3 + (m + 4))
                    g.tensor_tensor(er[:, e, :, :], er[:, e, :, :], S.er3[:, bass.ds(i * RING, RING), m, :],
                                    ALU.subtract).then_inc(ph["er_left"], 1)

            fives(pool, five)
            left(T5 - 1, 0)

        @block.vector
        def _(dve):
            v, own = nc.vector, Own(dve, ph["dve_own"])
            layernorm_stats(nc, dve, own, S.X, stats, mv, rstd, ph["eps_done"], ph["sqrt_done"])
            dve.wait_ge(ph["weights_in"], 144)
            own(v.tensor_scalar(S.attn[:, :], S.attn[:, :], 0.6, None, ALU.mult))
            own.wait()
            for name in ("xn_ready", "er_done"):
                dve.sem_inc(ph[name], RING)
            dve.sem_inc(ph["el_out"], 16)

            def five(i, e, more):
                v.tensor_reduce(hm[:, :], heads(xn[:, :, :]), AX.X, ALU.add).then_inc(ph["head_sums"], 1)
                dve.wait_ge(ph["head_sums"], i + 1)
                v.tensor_scalar(hm[:, :], hm[:, :], 1.0 / HD, None, ALU.mult).then_inc(ph["head_means"], 1)
                dve.wait_ge(ph["head_means"], i + 1)
                dve.wait_ge(ph["v_scaled"], i + 1)
                v.tensor_tensor(dn[:, :, :], heads(xn[:, :, :]), per_head(hm[:, :]), ALU.subtract
                                ).then_inc(ph["centred"], 1)
                dve.wait_ge(ph["el_out"], i * 16 + 16)
                dve.wait_ge(ph["er_parts"], i * 3)
                for j in range(RING):
                    after(dve, ph["p_psum"], i * RING + (j + 1))
                    v.tensor_tensor(el[:, j, 0:D], S.ps[:, j % 2, 0:D], rows[:, 0, :], ALU.add)
                    v.tensor_tensor(er[:, e, j, :], S.ps[:, j % 2, D:2 * D], rows[:, 1, :], ALU.add
                                    ).then_inc(ph["er_done"], 1)
                dve.wait_ge(ph["squared"], i + 1)
                v.tensor_reduce(hr[:, :], sq[:, :, :], AX.X, ALU.add).then_inc(ph["square_sums"], 1)
                if more:
                    dve.wait_ge(ph["centred"], i + 1)
                    norm_five(nc, ph, dve, S.X, mv, rstd, xn, i + 1)
                after(dve, ph["er_done"], i * RING + RING)
                for j in range(RING):
                    for m, row in enumerate((el[:, j, 0:D], er[:, e, j, :])):
                        ins = v.tensor_tensor_reduce(out=prod[:, m, j, :], in0=row, in1=S.attn[:, :], scale=1.0,
                                                     scalar=0.0, op0=ALU.mult, op1=ALU.add,
                                                     accum_out=dots5[:, m, j:j + 1])
                ins.then_inc(ph["attn_dots"], 1)
                dve.wait_ge(ph["stds"], i + 1)
                v.tensor_scalar_add(hr[:, :], hr[:, :], 1e-5).then_inc(ph["std_eps"], 1)
                dve.wait_ge(ph["attn_dots"], i + 1)
                v.tensor_copy(el[:, :, D], dots5[:, 0, :])
                v.tensor_copy(S.qk[:, 1, bass.ds(i * RING, RING)], dots5[:, 1, :]).then_inc(ph["el_five"], 1)
                dve.wait_ge(ph["std_eps"], i + 1)
                v.reciprocal(hr[:, :], hr[:, :]).then_inc(ph["std_inv"], 1)
                dve.wait_ge(ph["std_inv"], i + 1)
                v.tensor_tensor(dn[:, :, :], dn[:, :, :], per_head(hr[:, :]), ALU.mult).then_inc(ph["normed"], 1)
                dve.wait_ge(ph["normed"], i + 1)
                dve.wait_ge(ph["kv_used"], i * RING + RING)
                v.tensor_tensor(kf[:, :, :], dn[:, :, :].rearrange("p (r h) m -> p r (h m)", r=RING), five_rows(2),
                                ALU.mult).then_inc(ph["k_scaled"], 1)
                dve.wait_ge(ph["k_scaled"], i + 1)
                v.tensor_tensor(kf[:, :, :], kf[:, :, :], five_rows(3), ALU.add).then_inc(ph["k_ready"], 1)
                after(dve, ph["xn_ready"], (i + 1) * RING + (RING if more else 0))

            norm_five(nc, ph, dve, S.X, mv, rstd, xn, 0)
            after(dve, ph["xn_ready"], RING)
            fives(dve, five)
            for m in range(3):
                own(v.tensor_copy(S.er_dot3[:, :, m], S.qk[:, 1, :]))
                own.wait()
                own(v.tensor_tensor(S.qk[:, 1, :], S.qk[:, 1, :], S.er_dot3[:, :, m], ALU.subtract))
                own.wait()
            dve.wait_ge(ph["kv_used"], NODE_TILES + RING)
            for c in range(2):
                own(v.scalar_tensor_tensor(S.kvbd[:, c, 0:P], S.ps[:, 6 + c, 0:P], 1.0 / NODES, S.head_blocks[:, :],
                                           ALU.mult, ALU.mult))
            own.wait()

        @block.scalar
        def _(act):
            ln_root(nc, ph, act, rstd)
            act.sem_inc(ph["xT_ready"], RING)

            def copies(i):
                for j in range(RING):
                    n = i * RING + (j + 1)
                    again(act, ph["p_psum"], n)
                    copy_transposed(nc, ph, act, j, n, 4 + j % 2, xT)

            def five(i, e, more):
                act.wait_ge(ph["centred"], i + 1)
                nc.scalar.activation(sq[:, :, :], dn[:, :, :], ACT.Square).then_inc(ph["squared"], 1)
                act.wait_ge(ph["square_sums"], i + 1)
                nc.scalar.activation(hr[:, :], hr[:, :], ACT.Sqrt, scale=1.0 / (HD - 1)).then_inc(ph["stds"], 1)
                if not (isinstance(i, int) and i == 0):
                    parts(i - 1, 1 - e)
                if more:
                    copies(i + 1)

            def parts(i, e):
                for m in range(3):
                    if m == 0:
                        after(act, ph["er_done"], i * RING + RING)
                    else:
                        act.wait_ge(ph["er_left"], i * 2 + m)
                    nc.scalar.activation(S.er3[:, bass.ds(i * RING, RING), m, :], er[:, e, :, :], ACT.Copy
                                         ).then_inc(ph["er_parts"], 1)

            act.sem_inc(ph["er_parts"], 3)
            copies(0)
            fives(act, five)
            parts(T5 - 1, 0)

        @block.tensor
        def _(pe):
            pe.wait_ge(ph["weights_in"], 144)
            for name in ("xT_psum", "p_psum", "kv_used"):
                pe.sem_inc(ph[name], RING)

            def products(i):
                for j in range(RING):
                    n = i * RING + (j + 1)
                    after(pe, ph["xn_ready"], n)
                    bank_again(pe, ph["xT_ready"], j, n)
                    transpose_tile(nc, ph, pe, xn, j, 4 + j % 2, S.ident)
                    after(pe, ph["xT_ready"], n)
                    bank_again(pe, ph["er_done"], j, n)
                    for c in range(2):
                        ins = nc.tensor.matmul(S.ps[:, j % 2, :], xT[:, j, c, :],
                                               W[:, c, :, :].rearrange("p a n -> p (a n)"), start=c == 0, stop=c == 1)
                    ins.then_inc(ph["p_psum"], 1)

            def sums(i, first, last):
                pe.wait_ge(ph["k_ready"], i + 1)
                pe.wait_ge(ph["v_ready"], i + 1)
                for j in range(RING):
                    rows_ = LAST_ROWS if last and j == RING - 1 else P
                    for c in range(2):
                        ins = nc.tensor.matmul(S.ps[:, 6 + c, 0:P], kf[0:rows_, j, c * P:(c + 1) * P],
                                               vf[0:rows_, j, c * P:(c + 1) * P], start=first and j == 0,
                                               stop=last and j == RING - 1)
                    ins.then_inc(ph["kv_used"], 1)

            products(0)
            products(1)
            sums(0, True, False)
            with pe.Fori(1, T5 - 1) as i:
                products(i + 1)
                sums(i, False, False)
            sums(T5 - 1, False, True)


def score_and_mix_layer1(nc, S, A):
    N = GROUP * D
    lanes = MIX_LANES
    with Phase(nc, "score_mix_1") as ph:
        ph.ps = S.ps
        idx = ph.sb("gather_idx", [P, lanes, GROUP], I32)
        got = ph.sb("el_of_sources", [P, lanes, GROUP, D + 1])
        relB = ph.sb("rel_bcast", [P, lanes, GROUP * P])
        hot = ph.sb("dst_onehot_T", [P, lanes, GROUP * P], BF16)
        attn = ph.sb("attn_rows_04", [P, D])
        er_dot = ph.sb("er_dot", [P, lanes, GROUP])
        linear = ph.sb("linear_part", [P, lanes, GROUP])
        dots = ph.sb("dots", [P, GROUP])
        xr = ph.sb("xn_ring", [P, RING, D])
        xT = ph.sb("xn_T", [P, RING, 2, P])
        ps2 = S.ps[:, :, :].rearrange("p b n -> p (b n)")
        z = lambda half: ps2[:, half * 1536:half * 1536 + N]
        z3 = lambda half: z(half).rearrange("p (g d) -> p g d", d=D)
        lin = lambda half: ps2[:, half * 1536 + N:half * 1536 + N + 3 * GROUP]
        block = ph.block()

        def paced(eng, before, between, behind):
            with eng.Fori(0, T5) as i:
                for j in range(RING):
                    tile = (i * RING + j, j, i * RING + (j + 1))
                    before(*tile)
                    yield *group_at(i * 2, 2 * j, lanes), 0
                    between(*tile)
                    yield *group_at(i * 2, 2 * j + 1, lanes), 1
                    behind(*tile)
            loops = GROUPS // (2 * lanes)
            with eng.Fori(T5, loops) as i:
                for h in range(2 * lanes):
                    yield *group_at(i * 2, h, lanes), h % 2
            for h in range(GROUPS - 2 * lanes * loops):
                yield *group_at(2 * loops, h, lanes), h % 2

        def act_items(act):
            def stage(t, j, n):
                again(act, ph["xT_psum"], n)
                nc.scalar.activation(xr[:, j:j + 1, :], S.XN[:, bass.ds(t, 1), :], ACT.Copy
                                     ).then_inc(ph["x_staged"], 1)

            def copy(t, j, n):
                again(act, ph["m_psum"], n)
                copy_transposed(nc, ph, act, j, n, 6, xT)

            act.sem_inc(ph["xT_ready"], RING)
            act.sem_inc(ph["x_staged"], RING)
            for i, h, k, n, half in paced(act, stage, copy, nothing):
                yield i, h, k, n
                act.wait_ge(ph["z_ready"], n)
                nc.scalar.activation(z(half), z(half), ACT.Abs).then_inc(ph["abs_ready"], 1)

        gather_edges(nc, S, ph, block, S.eltab_dram, idx, got, relB, lanes, act_items)

        @block.vector
        def _(dve):
            v = nc.vector

            def mix(t, j, n):
                x = S.X[:, bass.ds(t, 1), :].squeeze(1)
                after(dve, ph["m_psum"], n)
                v.tensor_tensor(x, S.ps[:, 7, 0:D], x, ALU.add).then_inc(ph["added"], 1)
                after(dve, ph["added"], n)
                v.tensor_tensor(x, x, S.XN[:, bass.ds(t, 1), :].squeeze(1), ALU.add)

            for name in ("hot_ready", "rows_used", "dotted"):
                dve.sem_inc(ph[name], lanes)
            dve.sem_inc(ph["added"], RING)
            for h in range(AHEAD):
                onehot_T(nc, S, ph, dve, hot, relB, 0, h, h + 1)
            v.tensor_scalar(attn[:, :], S.attn[:, :], 0.4 / 0.6, None, ALU.mult).then_inc(ph["attn_scaled"], 1)
            dve.wait_ge(ph["attn_scaled"], 1)
            for i, h, k, n, half in paced(dve, nothing, nothing, mix):
                dve.wait_ge(ph[f"gathered{h}"], i * (16 * GROUP) + 16 * GROUP)
                dve.wait_ge(ph["dst_psum"], n + lanes)
                v.tensor_reduce(er_dot[:, h, :], lin(half).rearrange("p (g m) -> p g m", m=3), AX.X, ALU.add
                                ).then_inc(ph["er_dot"], 1)
                v.tensor_tensor(z3(half), z3(half), got[:, h, :, 0:D], ALU.add).then_inc(ph["z_ready"], 1)
                dve.wait_ge(ph["er_dot"], n)
                v.tensor_tensor(linear[:, h, :], er_dot[:, h, :], got[:, h, :, D], ALU.add
                                ).then_inc(ph["rows_used"], 1)
                if not (isinstance(k, int) and k + AHEAD >= GROUPS):
                    i2, h2, _, n2 = group_at(i, h + AHEAD, lanes)
                    onehot_T(nc, S, ph, dve, hot, relB, i2, h2, n2)
                dve.wait_ge(ph["abs_ready"], n)
                for j in range(GROUP):
                    ins = v.tensor_tensor_reduce(out=z(half)[:, j * D:(j + 1) * D], in0=z(half)[:, j * D:(j + 1) * D],
                                                 in1=attn[:, :], scale=1.0, scalar=0.0, op0=ALU.mult, op1=ALU.add,
                                                 accum_out=dots[:, j:j + 1])
                ins.then_inc(ph["dotted"], 1)
                dve.wait_ge(ph["dotted"], n + lanes)
                v.tensor_tensor(S.scoreX[:, bass.ds(k * GROUP, GROUP)], dots[:, :], linear[:, h, :], ALU.add)

        @block.tensor
        def _(pe):
            def transposes(t, j, n):
                after(pe, ph["x_staged"], n)
                pe.wait_ge(ph["xT_ready"], n + RING - 1)
                transpose_tile(nc, ph, pe, xr, j, 6, S.ident)

            def mix(t, j, n):
                after(pe, ph["xT_ready"], n)
                pe.wait_ge(ph["added"], n + RING - 1)
                for c in range(2):
                    ins = nc.tensor.matmul(S.ps[:, 7, c * P:(c + 1) * P], xT[:, j, c, :], S.kvbd[:, c, 0:P],
                                           start=True, stop=True)
                ins.then_inc(ph["m_psum"], 1)

            pe.sem_inc(ph["dst_psum"], lanes)
            for name in ("xT_psum", "m_psum"):
                pe.sem_inc(ph[name], RING)
            for i, h, k, n, half in paced(pe, nothing, transposes, mix):
                blocks = dst_blocks(pe, S, k)
                pe.wait_ge(ph["hot_ready"], n + lanes)
                pe.wait_ge(ph["dotted"], n + lanes - 2)
                for j, b in enumerate(blocks):
                    hot_j = hot[:, h, j * P:(j + 1) * P]
                    for m in range(3):
                        nc.tensor.matmul(z(half)[:, j * D:(j + 1) * D], hot_j, S.er3[:, bass.ds(b, 1), m, :].squeeze(1),
                                         start=m == 0, stop=m == 2)
                    last = nc.tensor.matmul(lin(half)[:, 3 * j:3 * j + 3], hot_j,
                                            S.er_dot3[:, bass.ds(b, 1), :].squeeze(1), start=True, stop=True)
                last.then_inc(ph["dst_psum"], 1)


def gates_layer1(nc, S, A):
    with Phase(nc, "gates_layer1") as ph:
        ph.ps = S.ps
        gW = ph.sb("w_gate", [P, 2, E1])
        gb = ph.sb("b_gate", [P, E1])
        stats, mv, rstd = ln_scratch(ph)
        xf = ph.sb("xf_ring", [P, RING, D])
        xT = ph.sb("xf_T", [P, RING, 2, P])
        lg = ph.sb("logits4", [P, NODE_TILES, E1])
        mx = ph.sb("logit_max", [P, NODE_TILES])
        top = ph.sb("top8", [P, NODE_TILES, 8])
        idx = ph.sb("top8_idx", [P, NODE_TILES, 8], U32)
        idxf = ph.sb("top8_idx_f", [P, NODE_TILES, 8])
        hot1 = ph.sb("hot1", [P, NODE_TILES, E1])
        hot2 = ph.sb("hot2", [P, NODE_TILES, E1])
        block = ph.block()
        wide = lambda x: x.unsqueeze(2).broadcast_to([P, NODE_TILES, E1])

        @block.sync
        def _(sp):
            sp.dma_start(gW[:, :, :], A["gW"].rearrange("(c p) n -> p c n", p=P)).then_inc(ph["weights_in"], 16)
            sp.dma_start(gb[:, :], bcast(A["gb"])).then_inc(ph["weights_in"], 16)
            sp.wait_ge(ph["weights_in"], 32)

        @block.gpsimd
        def _(pool):
            keep_tiles(nc, ph, pool, xf, S.QF)

        @block.vector
        def _(dve):
            v, own = nc.vector, Own(dve, ph["dve_own"])
            add_edge_sums(nc, ph, S, dve)
            layernorm_stats(nc, dve, own, S.X, stats, mv, rstd, ph["eps_done"], ph["sqrt_done"])
            dve.wait_ge(ph["weights_in"], 32)
            for name in ("xn_ready", "logits"):
                dve.sem_inc(ph[name], RING)

            def biased(i, t, j, n):
                after(dve, ph["l_psum"], n)
                v.tensor_tensor(lg[:, bass.ds(t, 1), :].squeeze(1), S.ps[:, j % 2, 0:E1], gb[:, :], ALU.add
                                ).then_inc(ph["logits"], 1)

            skewed(dve, norm_tile(nc, ph, dve, S.X, mv, rstd, xf), nothing, nothing, biased)
            after(dve, ph["logits"], NODE_TILES)
            own(v.memset(S.logits[:, :, :], -1.0))
            own(v.tensor_reduce(mx[:, :], lg[:, :, :], AX.X, ALU.max))
            own.wait()
            v.tensor_tensor(lg[:, :, :], lg[:, :, :], wide(mx[:, :]), ALU.subtract).then_inc(ph["shifted"], 1)
            dve.wait_ge(ph["exps"], 1)
            own(v.tensor_reduce(mx[:, :], lg[:, :, :], AX.X, ALU.add))
            own.wait()
            own(v.reciprocal(mx[:, :], mx[:, :]))
            own.wait()
            own(v.tensor_tensor(S.logits[:, :, 0:E1], lg[:, :, :], wide(mx[:, :]), ALU.mult))
            own.wait()
            top_two(nc, own, S.logits, top, idx, idxf, hot1, hot2, S.iota_row, 8)
            v.tensor_tensor(S.w2[:, :], top[:, :, 1], top[:, :, 0], ALU.subtract).then_inc(ph["gap"], 1)
            dve.wait_ge(ph["gap_exp"], 1)
            own(v.tensor_scalar_add(S.w1[:, :], S.w2[:, :], 1.0))
            own.wait()
            own(v.reciprocal(S.w1[:, :], S.w1[:, :]))
            own.wait()
            own(v.tensor_tensor(S.w2[:, :], S.w2[:, :], S.w1[:, :], ALU.mult))
            own.wait()
            own(v.tensor_tensor(hot1[:, :, :], hot1[:, :, :], wide(S.w1[:, :]), ALU.mult))
            own(v.tensor_tensor(hot2[:, :, :], hot2[:, :, :], wide(S.w2[:, :]), ALU.mult))
            own.wait()
            own(v.memset(S.wexp[:, :, :], 1.0))
            own.wait()
            own(v.tensor_tensor(S.wexp[:, :, 0:E1], hot1[:, :, :], hot2[:, :, :], ALU.add))
            own.wait()

        @block.scalar
        def _(act):
            ln_root(nc, ph, act, rstd)
            act.sem_inc(ph["xT_ready"], RING)
            for i, t, j, n in tiles(act):
                again(act, ph["l_psum"], n)
                copy_transposed(nc, ph, act, j, n, 4 + j % 2, xT)
            act.wait_ge(ph["shifted"], 1)
            nc.scalar.activation(lg[:, :, :], lg[:, :, :], ACT.Exp).then_inc(ph["exps"], 1)
            act.wait_ge(ph["gap"], 1)
            nc.scalar.activation(S.w2[:, :], S.w2[:, :], ACT.Exp).then_inc(ph["gap_exp"], 1)

        @block.tensor
        def _(pe):
            pe.wait_ge(ph["weights_in"], 32)
            for name in ("xT_psum", "l_psum"):
                pe.sem_inc(ph[name], RING)

            def transposes(i, t, j, n):
                after(pe, ph["xn_ready"], n)
                bank_again(pe, ph["xT_ready"], j, n)
                transpose_tile(nc, ph, pe, xf, j, 4 + j % 2, S.ident)

            def products(i, t, j, n):
                after(pe, ph["xT_ready"], n)
                bank_again(pe, ph["logits"], j, n)
                for c in range(2):
                    ins = nc.tensor.matmul(S.ps[:, j % 2, 0:E1], xT[:, j, c, :], gW[:, c, :],
                                           start=c == 0, stop=c == 1)
                ins.then_inc(ph["l_psum"], 1)

            skewed(pe, transposes, products)


def ffn_layer1(nc, S, A):
    with Phase(nc, "ffn_layer1") as ph:
        ph.ps = S.ps
        sW1 = ph.sb("shared_w1", [P, 2, D])
        sW2 = ph.sb("shared_w2", [P, 2, SH2])
        sW3 = ph.sb("shared_w3", [P, D])
        eW1 = ph.sb("expert_w1", [P, E1, 2, EH1])
        eW2 = ph.sb("expert_w2", [P, E1, EH2])
        eW3 = ph.sb("expert_w3", [EH2, E1, D])
        b3 = ph.sb("output_biases", [E1 + 1, D])
        bT = ph.sb("hidden_biases", [P, 3 + E1])
        bE2 = ph.sb("expert_b2", [EH2, E1])
        xr = ph.sb("xf_ring", [P, RING, D])
        wr = ph.sb("weights_ring", [P, RING, E1 + 1])
        xT = ph.sb("xf_T", [P, RING, 2, P])
        wT = ph.sb("weights_T", [E1 + 1, RING, P])
        s1 = ph.sb("shared_h1_T", [P, RING, 2, P])
        s2 = ph.sb("shared_h2_T", [P, RING, P])
        e1 = ph.sb("expert_h1_T", [P, RING, E1, P])
        e2 = ph.sb("expert_h2_T", [EH2, RING, E1, P])
        block = ph.block()
        ps = S.ps

        @block.sync
        def _(sp):
            for dst, src in ((sW1[:, :, :], A["sW1"].rearrange("(c p) n -> p c n", p=P)),
                             (sW2[:, :, :], A["sW2"].rearrange("(c p) n -> p c n", p=P)), (sW3[:, :], A["sW3"]),
                             (eW2[:, :, :], A["eW2b"].rearrange("e p n -> p e n")),
                             (eW3[:, :, :], A["eW3b"].rearrange("e p n -> p e n")), (b3[:, :], A["b3"]),
                             (bT[:, :], A["bT"]), (bE2[:, :], A["bE2"])):
                sp.dma_start(dst, src).then_inc(ph["weights_in"], 16)
            for e in range(E1):
                sp.dma_start(eW1[:, e, :, :], A["eW1b"][e, :, :].rearrange("(c p) n -> p c n", p=P)
                             ).then_inc(ph["weights_in"], 16)
            sp.wait_ge(ph["weights_in"], 16 * (8 + E1))

        @block.gpsimd
        def _(pool):
            pool.sem_inc(ph["staged"], RING)
            for i, t, j, n in tiles(pool):
                again(pool, ph["xT_psum"], n)
                nc.gpsimd.tensor_copy(wr[:, j, :], S.wexp[:, bass.ds(t, 1), 0:E1 + 1].squeeze(1))
                nc.gpsimd.tensor_copy(xr[:, j:j + 1, :], S.QF[:, bass.ds(t, 1), :]).then_inc(ph["staged"], 1)

        @block.tensor
        def _(pe):
            mm = nc.tensor.matmul

            def transposes(i, t, j, n):
                after(pe, ph["staged"], n)
                pe.wait_ge(ph["xT_ready"], n + RING - 1)
                nc.tensor.transpose(ps[0:E1 + 1, 0, D:D + P], wr[:, j, :], S.ident[:, :])
                transpose_tile(nc, ph, pe, xr, j, 0, S.ident)

            def hidden1(i, t, j, n):
                after(pe, ph["xT_ready"], n)
                pe.wait_ge(ph["h1_ready"], n + RING - 1)
                for m in range(2):
                    for c in range(2):
                        mm(ps[:, 1, m * P:(m + 1) * P], sW1[:, c, m * P:(m + 1) * P], xT[:, j, c, :],
                           start=c == 0, stop=c == 1)
                for e in range(E1):
                    for c in range(2):
                        ins = mm(ps[:, 2, e * P:(e + 1) * P], eW1[:, e, c, :], xT[:, j, c, :],
                                 start=c == 0, stop=c == 1)
                ins.then_inc(ph["h1_psum"], 1)

            def hidden2(i, t, j, n):
                after(pe, ph["h1_ready"], n)
                pe.wait_ge(ph["h2_ready"], n + RING - 1)
                for c in range(2):
                    mm(ps[:, 3, 0:P], sW2[:, c, :], s1[:, j, c, :], start=c == 0, stop=c == 1)
                for e in range(E1):
                    ins = mm(ps[0:EH2, 4, e * P:(e + 1) * P], eW2[:, e, :], e1[:, j, e, :], start=True, stop=True)
                ins.then_inc(ph["h2_psum"], 1)

            def outputs(i, t, j, n):
                after(pe, ph["h2_ready"], n)
                pe.wait_ge(ph["x_done"], n + RING - 1)
                mm(ps[:, 5, 0:D], s2[:, j, :], sW3[:, :], start=True, stop=False)
                mm(ps[:, 5, 0:D], wT[:, j, :], b3[:, :], start=False, stop=True)
                for e in range(E1):
                    ins = mm(ps[:, 6 + e // 2, (e % 2) * D:(e % 2 + 1) * D], e2[:, j, e, :], eW3[:, e, :],
                             start=True, stop=True)
                ins.then_inc(ph["o_psum"], 1)

            pe.wait_ge(ph["weights_in"], 16 * (8 + E1))
            for name in ("xT_psum", "h1_psum", "h2_psum", "o_psum"):
                pe.sem_inc(ph[name], RING)
            skewed(pe, transposes, hidden1, hidden2, outputs)

        @block.scalar
        def _(act):
            a = nc.scalar

            def copy(i, t, j, n):
                again(act, ph["o_psum"], n)
                after(act, ph["xT_psum"], n)
                a.activation(wT[:, j, :], ps[0:E1 + 1, 0, D:D + P], ACT.Copy)
                copy_transposed(nc, ph, act, j, n, 0, xT)

            def relu1(i, t, j, n):
                after(act, ph["h1_psum"], n)
                for m in range(2):
                    a.activation(s1[:, j, m, :], ps[:, 1, m * P:(m + 1) * P], ACT.Relu, bias=bT[:, m:m + 1])
                for e in range(E1):
                    ins = a.activation(e1[:, j, e, :], ps[:, 2, e * P:(e + 1) * P], ACT.Relu, bias=bT[:, 3 + e:4 + e])
                ins.then_inc(ph["h1_ready"], 1)

            def relu2(i, t, j, n):
                after(act, ph["h2_psum"], n)
                a.activation(s2[:, j, :], ps[:, 3, 0:P], ACT.Relu, bias=bT[:, 2:3])
                for e in range(E1):
                    ins = a.activation(e2[:, j, e, :], ps[0:EH2, 4, e * P:(e + 1) * P], ACT.Relu, bias=bE2[:, e:e + 1])
                ins.then_inc(ph["h2_ready"], 1)

            act.wait_ge(ph["weights_in"], 16 * (8 + E1))
            for name in ("xT_ready", "h1_ready", "h2_ready"):
                act.sem_inc(ph[name], RING)
            skewed(act, copy, relu1, relu2)

        @block.vector
        def _(dve):
            v = nc.vector
            dve.sem_inc(ph["x_done"], RING)
            dve.sem_inc(ph["x_step"], 1)
            for i, t, j, n in tiles(dve):
                x = S.X[:, bass.ds(t, 1), :].squeeze(1)
                after(dve, ph["o_psum"], n)
                v.tensor_tensor(x, ps[:, 5, 0:D], x, ALU.add).then_inc(ph["x_step"], 1)
                for e in range(E1):
                    dve.wait_ge(ph["x_step"], i * (RING * E1) + (j * E1 + e + 2))
                    ins = v.scalar_tensor_tensor(x, ps[:, 6 + e // 2, (e % 2) * D:(e % 2 + 1) * D],
                                                 S.wexp[:, bass.ds(t, 1), e], x, ALU.mult, ALU.add)
                    ins.then_inc(ph["x_step"] if e < E1 - 1 else ph["x_done"], 1)


def reset_semaphores(nc):
    with Phase(nc, "reset") as ph:
        numbers = sorted(Phase.numbers)
        block = ph.block()

        @block.gpsimd
        def _(pool):
            while numbers:
                first = last = numbers.pop(0)
                while numbers and numbers[0] == last + 1:
                    last = numbers.pop(0)
                pool.sem_clear(range(first, last + 1))
        Phase.numbers.clear()


def write_out(nc, S, out):
    with Phase(nc, "write_out") as ph:
        block = ph.block()

        @block.sync
        def _(sp):
            sp.dma_start(out[0:NODES_PAD - P, :].rearrange("(t p) d -> p t d", p=P),
                         S.X[:, 0:NODE_TILES - 1, :]).then_inc(ph["out"], 16)
            sp.dma_start(out[NODES_PAD - P:NODES, :], S.X[0:LAST_ROWS, NODE_TILES - 1, :]).then_inc(ph["out"], 16)
            sp.wait_ge(ph["out"], 32)


def build(nc, A, out):
    S = State()
    Phase.numbers.clear()
    with ExitStack() as ctx:
        Phase.lasting = ctx

        def sb(name, shape, dt=F32):
            return ctx.enter_context(nc.sbuf_tensor(name, shape, dt))

        def dram(name, shape, dt=F32):
            return nc.dram_tensor(name, shape, dt, kind="Internal").ap()
        S.ps = ctx.enter_context(nc.psum_tensor("ps", [P, 8, 512], F32))
        S.ident = sb("ident", [P, P])
        S.ones = sb("ones", [P, P])
        S.iota_row = sb("iota_row", [P, P])
        S.iota_col = sb("iota_col", [P, 1])
        S.srcX = sb("src_by_step", [P, STEPS], I32)
        S.relX = sb("rel_by_step", [P, STEPS])
        S.validX = sb("valid_by_step", [P, STEPS])
        S.penX = sb("penalty_by_step", [P, STEPS])
        S.scoreX = sb("score_by_step", [P, STEPS])
        S.weightX = sb("weight_by_step", [P, STEPS])
        S.blockI = sb("block_by_step", [1, GROUPS, 8], I32)
        S.cut = sb("segment_cuts", [GROUPS, 2, GROUP * P])
        S.row_cut = sb("row_has_cut", [GROUPS, 2])
        S.X = sb("x", [P, NODE_TILES, D])
        S.qk = sb("q_k_scalars", [P, 2, NODE_TILES])
        S.QF = sb("q_features", [P, NODE_TILES, D])
        S.attn = sb("attn_rows", [P, D])
        S.ln2_mv = sb("ln2_mean_var", [P, NODE_TILES, 2])
        S.ln2_rstd = sb("ln2_rstd", [P, NODE_TILES])
        S.kvbd = sb("kv_blocks", [P, 2, P + 4])
        S.inv_sum = sb("inv_softmax_sum", [P, NODE_TILES])
        S.node_mask = sb("node_mask", [P, NODE_TILES])
        S.logits = sb("logits", [P, NODE_TILES, E0])
        S.wexp = sb("expert_weights", [P, NODE_TILES, E0])
        S.w1 = sb("first_weight", [P, NODE_TILES])
        S.w2 = sb("second_weight", [P, NODE_TILES])
        S.posI = sb("slots_of_node", [P, 2, NODE_TILES], I32)
        S.slot_node = sb("node_of_slot", [P, SLOT_TILES], I32)
        S.expertI = sb("expert_of_tile", [1, SLOT_TILES], I32)
        S.head_blocks = sb("head_blocks", [P, P])
        S.rel_dram = dram("rel_by_step_rows", (STEPS, P))
        S.key_dram = dram("keys", (STEPS * P + 2,))
        S.htab_dram = dram("h_table", (NODES_PAD, D + 1))
        S.step_dram = dram("rows_by_step", (GROUPS, P, GROUP * D))
        S.xn_dram = dram("xn_table", (NODES_PAD, D))
        S.eltab_dram = dram("el_table", (NODES_PAD, D + 1))
        S.y_dram = dram("y_by_slot", (SLOT_ROWS, D))
        S.loads = 0
        S.layer = 0
        prepare_edges(nc, S, A)
        with nc.sbuf_tensor("xn_0", [P, NODE_TILES, D], F32) as S.XN:
            project_layer0(nc, S, A)
            score_and_mix_layer0(nc, S, A)
        softmax_weights(nc, S, A, True)
        with nc.sbuf_tensor("edge_sums_0", [P, NODE_TILES, D + 1], F32) as S.acc:
            aggregate(nc, S, A)
            router(nc, S, A)
        with nc.sbuf_tensor("expert_w2", [P, E0, HID // P, D], F32) as S.W2:
            dispatch_plan(nc, S, A)
            expert_inputs(nc, S, A)
            experts(nc, S, A)
        combine(nc, S, A)
        S.layer = 1
        reset_semaphores(nc)
        with nc.sbuf_tensor("xn_1", [P, NODE_TILES, D], F32) as S.XN:
            with (nc.sbuf_tensor("er_parts", [P, NODE_TILES, 3, D], BF16) as S.er3,
                  nc.sbuf_tensor("er_dot_parts", [P, NODE_TILES, 3], BF16) as S.er_dot3):
                project_layer1(nc, S, A)
                score_and_mix_layer1(nc, S, A)
        softmax_weights(nc, S, A, False)
        with nc.sbuf_tensor("edge_sums_1", [P, NODE_TILES, D + 1], F32) as S.acc:
            aggregate(nc, S, A)
            gates_layer1(nc, S, A)
        ffn_layer1(nc, S, A)
        write_out(nc, S, out)


def layout(inputs):
    import numpy as np
    c = np.ascontiguousarray
    a = {}
    x = np.zeros((NODES_PAD, D), np.float32)
    x[:NODES] = inputs["x"]
    src = np.zeros(EDGE_TILES * P, np.int32)
    src[:EDGES] = inputs["src"]
    dst = np.full(EDGE_TILES * P, PAD_NODE, np.int32)
    dst[:EDGES] = inputs["dst"]
    dst = dst.reshape(EDGE_TILES, P)
    before = np.zeros(EDGE_TILES, np.int32)
    before[1:] = dst[:-1, P - 1]
    a.update(x=x, src=src.reshape(EDGE_TILES, P), dst=dst, dst_before=c(before.reshape(EDGE_CHUNKS, EDGE_ROWS).T))
    a["Wv"] = c(inputs["L0_gnn_Wv"])
    a["bv"] = c(inputs["L0_gnn_bv"])
    a["wq"] = c(inputs["L0_gnn_wq"])
    a["wk"] = c(inputs["L0_gnn_wk"])
    a["bq"] = c(inputs["L0_gnn_bq"]).reshape(1)
    a["bk"] = c(inputs["L0_gnn_bk"]).reshape(1)
    a["WqkvT"] = c(np.asarray(inputs["L0_mix_Wqkv"]).T)
    for name in ("ln1_g", "ln1_b", "ln2_g", "ln2_b"):
        a[name] = c(inputs["L0_mix_" + name])
    a["mW1T"], a["mW2T"] = c(np.asarray(inputs["L0_mix_W1"]).T), c(np.asarray(inputs["L0_mix_W2"]).T)
    a["mb1"] = c(np.asarray(inputs["L0_mix_b1"]).reshape(2, P).T)
    a["mb2"] = c(inputs["L0_mix_b2"])
    a["Wr"], a["br"] = c(inputs["L0_ffn_Wr"]), c(inputs["L0_ffn_br"])
    a["eW1"] = c(inputs["L0_ffn_W1"]).reshape(E0 * D, HID)
    a["eW2"] = c(inputs["L0_ffn_W2"]).reshape(E0 * HID, D)
    a["eb2"] = c(inputs["L0_ffn_b2"])
    a["eSmall"] = c(np.concatenate([np.asarray(inputs["L0_ffn_" + n]).reshape(E0, -1, P).transpose(0, 2, 1)
                                    for n in ("ln_g", "ln_b", "b1")], axis=2))
    for name, key in (("Ws", "W_src"), ("bs", "b_src"), ("Wd", "W_dst"), ("bd", "b_dst"), ("attn", "attn")):
        a[name] = c(inputs["L1_gnn_" + key])
    for name, key in (("kw", "kln_weight"), ("kb", "kln_bias"), ("vw", "vln_weight"), ("vb", "vln_bias")):
        a[name] = c(inputs["L1_mix_" + key]).reshape(D)
    f = {k[7:]: np.asarray(v) for k, v in inputs.items() if k.startswith("L1_ffn_")}
    a.update(sW1=c(f["sW1"]), sW2=c(f["sW2"]), sW3=c(f["sW3"]), eW1b=c(f["eW1"]), eW2b=c(f["eW2"]), eW3b=c(f["eW3"]),
             gW=c(f["gW"]), gb=c(f["gb"]), b3=c(np.concatenate([f["eb3"], f["sb3"][None]], axis=0)),
             bT=c(np.concatenate([f["sb1"].reshape(2, P), f["sb2"].reshape(1, P), f["eb1"]], axis=0).T),
             bE2=c(f["eb2"].T))
    return a


def kernel(**inputs):
    import numpy as np
    import concourse.bacc as bacc
    from concourse.bass_utils import run_bass_kernel_spmd
    nc = bacc.Bacc("TRN2", target_bir_lowering=False, num_devices=1)
    arrays = {f"in_{k}": v for k, v in layout(inputs).items()}
    A = {k[3:]: nc.dram_tensor(k, v.shape, mybir.dt.from_np(v.dtype), kind="ExternalInput").ap()
         for k, v in arrays.items()}
    out = nc.dram_tensor("out", (NODES, D), F32, kind="ExternalOutput").ap()
    build(nc, A, out)
    return run_bass_kernel_spmd(nc, [arrays], core_ids=[0]).results[0]["out"]
```
